# Optimizing a Trainium2 kernel written in Bass

```python
import numpy as np
import jax
import jax.numpy as jnp

def _softmax(x, axis=-1):
    return jax.nn.softmax(x, axis=axis)

def _gelu(x):
    return jax.nn.gelu(x, approximate=True)

def _silu(x):
    return jax.nn.silu(x)

def _sigmoid(x):
    return jax.nn.sigmoid(x)

def _layernorm(x, axis=-1, eps=1e-05):
    m = jnp.mean(x, axis=axis, keepdims=True)
    v = jnp.var(x, axis=axis, keepdims=True)
    return (x - m) / jnp.sqrt(v + eps)

def _scatter_add(tgt, idx, src, axis=0):
    return tgt.at[idx].add(src)

def _segment_sum(src, seg, n):
    return jax.ops.segment_sum(src, seg, n)
kernel_name = 'mk_gps_d2_gnn_r16_e8e491'

def setup_inputs(seed: int=0):
    np.random.seed(seed)
    _w = jnp.asarray

    def _rec_inputs():
        import jax
        import jax.numpy as jnp
        _gk = jax.random.key(seed)
        x = -8.776e-05 + 1 * jax.random.normal(jax.random.fold_in(_gk, 1), (625, 512), jnp.float32)
        src = jax.random.randint(jax.random.fold_in(_gk, 2), (10000,), 0, 625, jnp.int32)
        dst = jnp.minimum((625 * jax.random.uniform(jax.random.fold_in(_gk, 3), (10000,)) ** 2.0).astype(jnp.int32), 9999)
        _o = jnp.argsort(dst, stable=True)
        src = src[_o]
        dst = dst[_o]
        edge_type_2 = jax.random.randint(jax.random.fold_in(_gk, 13), (10000,), 0, 2, jnp.int32)
        return (x, src, dst, edge_type_2)
    x, src, dst, edge_type_2 = _rec_inputs()

    def _L0_gnn_setup():
        import jax, jax.numpy as jnp
        import numpy as np
        NUM_RELATIONS = 2
        NUM_BASES = 30
        HIDDEN = 512
        N_NODES = 625
        N_EDGES = 10000

        def rgcn_gate_layer(x, row, col, edge_type, basis, att, gate_w, root, bias):
            H = x.shape[1]
            w = jnp.einsum('rb,bio->rio', att, basis)
            x_j = x[col]
            msgs = []
            for r in range(NUM_RELATIONS):
                gate = jax.nn.sigmoid(x_j @ gate_w[r, :, 0])
                msgs.append(gate[:, None] * x_j @ w[r])
            msg = jnp.where((edge_type == 0)[:, None], msgs[0], msgs[1])
            agg = jax.ops.segment_sum(msg, row, num_segments=x.shape[0])
            return agg + x @ root + bias
        key = jax.random.key(seed)
        ks = jax.random.split(key, 16)
        H, R, B = (HIDDEN, NUM_RELATIONS, NUM_BASES)
        bound = 1.0 / np.sqrt(B * H)
        u = lambda k, shape: jax.random.uniform(k, shape, jnp.float32, -bound, bound)
        inp = {'x': jax.random.normal(ks[0], (N_NODES, H), jnp.float32), 'edge_index': jax.random.randint(ks[1], (2, N_EDGES), 0, N_NODES, jnp.int32), 'edge_type': jax.random.randint(ks[2], (N_EDGES,), 0, R, jnp.int32), 'basis1': u(ks[3], (B, H, H)), 'att1': u(ks[4], (R, B)), 'gate_w1': u(ks[5], (R, H, 1)), 'root1': u(ks[6], (H, H)), 'bias1': u(ks[7], (H,)), 'basis2': u(ks[8], (B, H, H)), 'att2': u(ks[9], (R, B)), 'gate_w2': u(ks[10], (R, H, 1)), 'root2': u(ks[11], (H, H)), 'bias2': u(ks[12], (H,))}
        return inp
    _L0_gnn_all = _L0_gnn_setup()
    _L0_gnn_in = {k: v for k, v in _L0_gnn_all.items() if k in ('basis1', 'att1', 'gate_w1', 'root1', 'bias1', 'basis2', 'att2', 'gate_w2', 'root2', 'bias2')}
    del _L0_gnn_all

    def _L0_mix_setup():
        import jax, jax.numpy as jnp
        import numpy as np
        B, T, DIM = (32, 196, 512)
        EMB = 512
        M = 256
        EPS_ATTN = 1e-08
        EPS_LN = 0.001

        def layernorm(x, g, b):
            mu = jnp.mean(x, axis=-1, keepdims=True)
            var = jnp.var(x, axis=-1, keepdims=True)
            return (x - mu) / jnp.sqrt(var + EPS_LN) * g + b

        def prm_exp(x, w):
            xd = jnp.sum(x * x, axis=-1, keepdims=True) / 2.0
            wtx = jnp.einsum('bti,mi->btm', x, w)
            return jnp.exp(wtx - xd) / jnp.sqrt(jnp.float32(M))
        key = jax.random.key(seed)
        ks = jax.random.split(key, 16)
        s_in = 1.0 / np.sqrt(DIM)
        s_emb = 1.0 / np.sqrt(EMB)
        x = jax.random.normal(ks[0], (B, T, DIM), dtype=jnp.float32)
        kqv_w = jax.random.normal(ks[1], (DIM, 3 * EMB), dtype=jnp.float32) * s_in
        kqv_b = jnp.zeros((3 * EMB,), dtype=jnp.float32)
        proj_w = jax.random.normal(ks[2], (EMB, EMB), dtype=jnp.float32) * s_emb
        proj_b = jnp.zeros((EMB,), dtype=jnp.float32)
        n1_g = jnp.ones((DIM,), dtype=jnp.float32)
        n1_b = jnp.zeros((DIM,), dtype=jnp.float32)
        n2_g = jnp.ones((EMB,), dtype=jnp.float32)
        n2_b = jnp.zeros((EMB,), dtype=jnp.float32)
        mlp_w1 = jax.random.normal(ks[3], (EMB, EMB), dtype=jnp.float32) * s_emb
        mlp_b1 = jnp.zeros((EMB,), dtype=jnp.float32)
        mlp_w2 = jax.random.normal(ks[4], (EMB, EMB), dtype=jnp.float32) * s_emb
        mlp_b2 = jnp.zeros((EMB,), dtype=jnp.float32)
        a = jax.random.normal(ks[5], (EMB, M), dtype=jnp.float32)
        q, _ = jnp.linalg.qr(a)
        w = q.T * jnp.sqrt(jnp.float32(M))
        return {'x': x, 'kqv_w': kqv_w, 'kqv_b': kqv_b, 'proj_w': proj_w, 'proj_b': proj_b, 'n1_g': n1_g, 'n1_b': n1_b, 'n2_g': n2_g, 'n2_b': n2_b, 'mlp_w1': mlp_w1, 'mlp_b1': mlp_b1, 'mlp_w2': mlp_w2, 'mlp_b2': mlp_b2, 'w': w}
    _L0_mix_all = _L0_mix_setup()
    _L0_mix_in = {k: v for k, v in _L0_mix_all.items() if k in ('kqv_w', 'kqv_b', 'proj_w', 'proj_b', 'n1_g', 'n1_b', 'n2_g', 'n2_b', 'mlp_w1', 'mlp_b1', 'mlp_w2', 'mlp_b2', 'w')}
    del _L0_mix_all

    def _L0_ffn_setup():
        import jax, jax.numpy as jnp
        import numpy as np
        E = 64
        K = 2
        CAP = 512
        H = 512
        FFN = 128
        B, S = (8, 256)
        key = jax.random.key(seed)
        ks = jax.random.split(key, 6)
        hidden_states = jax.random.normal(ks[0], (B, S, H), dtype=jnp.float32)
        router_w = jax.random.normal(ks[1], (E, H), dtype=jnp.float32) * (0.01 / np.sqrt(H))
        w1 = jax.random.normal(ks[2], (FFN, H), dtype=jnp.float32) * (1.0 / np.sqrt(H))
        b1 = jnp.zeros((FFN,), dtype=jnp.float32)
        w2 = jax.random.normal(ks[3], (H, FFN), dtype=jnp.float32) * (1.0 / np.sqrt(FFN))
        b2 = jnp.zeros((H,), dtype=jnp.float32)
        return {'hidden_states': hidden_states, 'router_w': router_w, 'w1': w1, 'b1': b1, 'w2': w2, 'b2': b2}
    _L0_ffn_all = _L0_ffn_setup()
    _L0_ffn_in = {k: v for k, v in _L0_ffn_all.items() if k in ('router_w', 'w1', 'b1', 'w2', 'b2')}
    del _L0_ffn_all

    def _L1_gnn_setup():
        import jax, jax.numpy as jnp
        import numpy as np
        B = 32
        MAXN = 128
        HEADS = 8
        DH = 64
        M = 256
        D = 512
        EPS = 1e-05
        KEPS = 1e-06

        def _batchnorm(x, g, b):
            mu = jnp.mean(x, axis=0)
            var = jnp.mean((x - mu) ** 2, axis=0)
            return (x - mu) * jax.lax.rsqrt(var + EPS) * g + b

        def _forward(x, batch, edge_index, norm1_g, norm1_b, norm2_g, norm2_b, W_conv, b_conv, Wq, Wk, Wv, Wo, proj):
            N = x.shape[0]
            E = edge_index.shape[1]
            h = x
            xn = _batchnorm(x, norm1_g, norm1_b)
            msg = xn[edge_index[0]]
            agg = jax.ops.segment_sum(msg, edge_index[1], num_segments=N)
            deg = jax.ops.segment_sum(jnp.ones((E,), x.dtype), edge_index[1], num_segments=N)
            agg = agg / jnp.maximum(deg, 1.0)[:, None]
            conv_out = jax.nn.relu(agg @ W_conv + b_conv)
            counts = jax.ops.segment_sum(jnp.ones((N,), jnp.int32), batch, num_segments=B)
            offsets = jnp.concatenate([jnp.zeros((1,), jnp.int32), jnp.cumsum(counts)[:-1]])
            pos = jnp.arange(N, dtype=jnp.int32) - offsets[batch]
            h_dense = jnp.zeros((B, MAXN, D), x.dtype).at[batch, pos].set(h)
            mask = jnp.zeros((B, MAXN), bool).at[batch, pos].set(True)

            def heads(t, W):
                return (t @ W).reshape(B, MAXN, HEADS, DH).transpose(0, 2, 1, 3)
            q, k, v = (heads(h_dense, Wq), heads(h_dense, Wk), heads(h_dense, Wv))
            scale = DH ** (-0.25)

            def phi(t, is_query):
                t = t * scale
                u = jnp.einsum('bhnd,md->bhnm', t, proj)
                diag = 0.5 * jnp.sum(t * t, axis=-1, keepdims=True)
                if is_query:
                    m_ = jnp.max(u, axis=-1, keepdims=True)
                else:
                    m_ = jnp.max(u, axis=(-2, -1), keepdims=True)
                return jnp.exp(u - diag - jax.lax.stop_gradient(m_)) / np.sqrt(M) + KEPS
            qf = phi(q, True)
            kf = phi(k, False) * mask[:, None, :, None]
            vm = v * mask[:, None, :, None]
            kv = jnp.einsum('bhnm,bhnd->bhmd', kf, vm)
            z = 1.0 / (jnp.einsum('bhnm,bhm->bhn', qf, kf.sum(axis=2)) + KEPS)
            attn = jnp.einsum('bhnm,bhmd->bhnd', qf, kv) * z[..., None]
            attn = attn.transpose(0, 2, 1, 3).reshape(B, MAXN, D) @ Wo
            h_attn = attn[batch, pos]
            return _batchnorm(conv_out + h_attn + h, norm2_g, norm2_b)
        key = jax.random.key(seed)
        ks = jax.random.split(key, 10)
        sizes = 1024 + np.arange(B) * 131 % 1025
        N = int(sizes.sum())
        E = N * 8
        batch = jnp.asarray(np.repeat(np.arange(B), sizes), dtype=jnp.int32)
        edge_index = jax.random.randint(ks[0], (2, E), 0, N, dtype=jnp.int32)
        s = 1.0 / np.sqrt(D)
        return {'x': jax.random.normal(ks[1], (N, D), jnp.float32), 'batch': batch, 'edge_index': edge_index, 'norm1_g': jnp.ones((D,), jnp.float32), 'norm1_b': jnp.zeros((D,), jnp.float32), 'norm2_g': jnp.ones((D,), jnp.float32), 'norm2_b': jnp.zeros((D,), jnp.float32), 'W_conv': jax.random.normal(ks[2], (D, D), jnp.float32) * s, 'b_conv': jnp.zeros((D,), jnp.float32), 'Wq': jax.random.normal(ks[3], (D, D), jnp.float32) * s, 'Wk': jax.random.normal(ks[4], (D, D), jnp.float32) * s, 'Wv': jax.random.normal(ks[5], (D, D), jnp.float32) * s, 'Wo': jax.random.normal(ks[6], (D, D), jnp.float32) * s, 'proj': jax.random.normal(ks[7], (M, DH), jnp.float32)}
    _L1_gnn_all = _L1_gnn_setup()
    _L1_gnn_in = {k: v for k, v in _L1_gnn_all.items() if k in ('norm1_g', 'norm1_b', 'norm2_g', 'norm2_b', 'W_conv', 'b_conv', 'Wq', 'Wk', 'Wv', 'Wo', 'proj')}
    del _L1_gnn_all

    def _L1_mix_setup():
        import jax, jax.numpy as jnp
        import numpy as np
        DIM = 512
        HEADS = 8
        HEAD_DIM = DIM // HEADS
        SCALE = HEAD_DIM ** (-0.5)

        def phi(t):
            return jax.nn.elu(t) + 1.0
        key = jax.random.key(seed)
        k1, k2, k3, k4 = jax.random.split(key, 4)
        B, N, C = (4, 512, DIM)
        x = jax.random.normal(k1, (B, N, C), dtype=jnp.float32)
        w_qkv = jax.random.normal(k2, (3 * C, C), dtype=jnp.float32) * (1.0 / np.sqrt(C))
        w_proj = jax.random.normal(k3, (C, C), dtype=jnp.float32) * (1.0 / np.sqrt(C))
        b_proj = jax.random.normal(k4, (C,), dtype=jnp.float32) * 0.01
        return {'x': x, 'w_qkv': w_qkv, 'w_proj': w_proj, 'b_proj': b_proj}
    _L1_mix_all = _L1_mix_setup()
    _L1_mix_in = {k: v for k, v in _L1_mix_all.items() if k in ('w_qkv', 'w_proj', 'b_proj')}
    del _L1_mix_all

    def _L1_ffn_setup():
        import jax, jax.numpy as jnp
        import numpy as np
        H = 512
        FF = 4 * H
        E = 8
        K = 2
        B, S = (4, 256)
        key = jax.random.key(seed)
        ks = jax.random.split(key, 4)
        s = 0.02
        return {'x': jax.random.normal(ks[0], (B, S, H), dtype=jnp.float32), 'Wg': jax.random.normal(ks[1], (H, E), dtype=jnp.float32) * s, 'bg': jnp.zeros((E,), dtype=jnp.float32), 'W1': jax.random.normal(ks[2], (E, H, FF), dtype=jnp.float32) * s, 'b1': jnp.zeros((E, FF), dtype=jnp.float32), 'W2': jax.random.normal(ks[3], (E, FF, H), dtype=jnp.float32) * s, 'b2': jnp.zeros((E, H), dtype=jnp.float32)}
    _L1_ffn_all = _L1_ffn_setup()
    _L1_ffn_in = {k: v for k, v in _L1_ffn_all.items() if k in ('Wg', 'bg', 'W1', 'b1', 'W2', 'b2')}
    del _L1_ffn_all
    return {'x': x, 'src': src, 'dst': dst, 'edge_type_2': edge_type_2, 'L0_gnn_basis1': _L0_gnn_in['basis1'], 'L0_gnn_att1': _L0_gnn_in['att1'], 'L0_gnn_gate_w1': _L0_gnn_in['gate_w1'], 'L0_gnn_root1': _L0_gnn_in['root1'], 'L0_gnn_bias1': _L0_gnn_in['bias1'], 'L0_gnn_basis2': _L0_gnn_in['basis2'], 'L0_gnn_att2': _L0_gnn_in['att2'], 'L0_gnn_gate_w2': _L0_gnn_in['gate_w2'], 'L0_gnn_root2': _L0_gnn_in['root2'], 'L0_gnn_bias2': _L0_gnn_in['bias2'], 'L0_mix_kqv_w': _L0_mix_in['kqv_w'], 'L0_mix_kqv_b': _L0_mix_in['kqv_b'], 'L0_mix_proj_w': _L0_mix_in['proj_w'], 'L0_mix_proj_b': _L0_mix_in['proj_b'], 'L0_mix_n1_g': _L0_mix_in['n1_g'], 'L0_mix_n1_b': _L0_mix_in['n1_b'], 'L0_mix_n2_g': _L0_mix_in['n2_g'], 'L0_mix_n2_b': _L0_mix_in['n2_b'], 'L0_mix_mlp_w1': _L0_mix_in['mlp_w1'], 'L0_mix_mlp_b1': _L0_mix_in['mlp_b1'], 'L0_mix_mlp_w2': _L0_mix_in['mlp_w2'], 'L0_mix_mlp_b2': _L0_mix_in['mlp_b2'], 'L0_mix_w': _L0_mix_in['w'], 'L0_ffn_router_w': _L0_ffn_in['router_w'], 'L0_ffn_w1': _L0_ffn_in['w1'], 'L0_ffn_b1': _L0_ffn_in['b1'], 'L0_ffn_w2': _L0_ffn_in['w2'], 'L0_ffn_b2': _L0_ffn_in['b2'], 'L1_gnn_norm1_g': _L1_gnn_in['norm1_g'], 'L1_gnn_norm1_b': _L1_gnn_in['norm1_b'], 'L1_gnn_norm2_g': _L1_gnn_in['norm2_g'], 'L1_gnn_norm2_b': _L1_gnn_in['norm2_b'], 'L1_gnn_W_conv': _L1_gnn_in['W_conv'], 'L1_gnn_b_conv': _L1_gnn_in['b_conv'], 'L1_gnn_Wq': _L1_gnn_in['Wq'], 'L1_gnn_Wk': _L1_gnn_in['Wk'], 'L1_gnn_Wv': _L1_gnn_in['Wv'], 'L1_gnn_Wo': _L1_gnn_in['Wo'], 'L1_gnn_proj': _L1_gnn_in['proj'], 'L1_mix_w_qkv': _L1_mix_in['w_qkv'], 'L1_mix_w_proj': _L1_mix_in['w_proj'], 'L1_mix_b_proj': _L1_mix_in['b_proj'], 'L1_ffn_Wg': _L1_ffn_in['Wg'], 'L1_ffn_bg': _L1_ffn_in['bg'], 'L1_ffn_W1': _L1_ffn_in['W1'], 'L1_ffn_b1': _L1_ffn_in['b1'], 'L1_ffn_W2': _L1_ffn_in['W2'], 'L1_ffn_b2': _L1_ffn_in['b2']}

def reference(x, src, dst, edge_type_2, L0_gnn_basis1, L0_gnn_att1, L0_gnn_gate_w1, L0_gnn_root1, L0_gnn_bias1, L0_gnn_basis2, L0_gnn_att2, L0_gnn_gate_w2, L0_gnn_root2, L0_gnn_bias2, L0_mix_kqv_w, L0_mix_kqv_b, L0_mix_proj_w, L0_mix_proj_b, L0_mix_n1_g, L0_mix_n1_b, L0_mix_n2_g, L0_mix_n2_b, L0_mix_mlp_w1, L0_mix_mlp_b1, L0_mix_mlp_w2, L0_mix_mlp_b2, L0_mix_w, L0_ffn_router_w, L0_ffn_w1, L0_ffn_b1, L0_ffn_w2, L0_ffn_b2, L1_gnn_norm1_g, L1_gnn_norm1_b, L1_gnn_norm2_g, L1_gnn_norm2_b, L1_gnn_W_conv, L1_gnn_b_conv, L1_gnn_Wq, L1_gnn_Wk, L1_gnn_Wv, L1_gnn_Wo, L1_gnn_proj, L1_mix_w_qkv, L1_mix_w_proj, L1_mix_b_proj, L1_ffn_Wg, L1_ffn_bg, L1_ffn_W1, L1_ffn_b1, L1_ffn_W2, L1_ffn_b2):
    import jax
    import jax.numpy as jnp

    def _L0_gnn_ref(x, edge_index, edge_type, basis1, att1, gate_w1, root1, bias1, basis2, att2, gate_w2, root2, bias2):
        import jax, jax.numpy as jnp
        import numpy as np
        NUM_RELATIONS = 2
        NUM_BASES = 30
        HIDDEN = 512
        N_NODES = 625
        N_EDGES = 10000

        def rgcn_gate_layer(x, row, col, edge_type, basis, att, gate_w, root, bias):
            H = x.shape[1]
            w = jnp.einsum('rb,bio->rio', att, basis)
            x_j = x[col]
            msgs = []
            for r in range(NUM_RELATIONS):
                gate = jax.nn.sigmoid(x_j @ gate_w[r, :, 0])
                msgs.append(gate[:, None] * x_j @ w[r])
            msg = jnp.where((edge_type == 0)[:, None], msgs[0], msgs[1])
            agg = jax.ops.segment_sum(msg, row, num_segments=x.shape[0])
            return agg + x @ root + bias
        row, col = (edge_index[0], edge_index[1])
        h = jax.nn.relu(rgcn_gate_layer(x, row, col, edge_type, basis1, att1, gate_w1, root1, bias1))
        out = rgcn_gate_layer(h, row, col, edge_type, basis2, att2, gate_w2, root2, bias2)
        return out

    def _L0_mix_ref(x, kqv_w, kqv_b, proj_w, proj_b, n1_g, n1_b, n2_g, n2_b, mlp_w1, mlp_b1, mlp_w2, mlp_b2, w):
        import jax, jax.numpy as jnp
        import numpy as np
        B, T, DIM = (32, 196, 512)
        EMB = 512
        M = 256
        EPS_ATTN = 1e-08
        EPS_LN = 0.001

        def layernorm(x, g, b):
            mu = jnp.mean(x, axis=-1, keepdims=True)
            var = jnp.var(x, axis=-1, keepdims=True)
            return (x - mu) / jnp.sqrt(var + EPS_LN) * g + b

        def prm_exp(x, w):
            xd = jnp.sum(x * x, axis=-1, keepdims=True) / 2.0
            wtx = jnp.einsum('bti,mi->btm', x, w)
            return jnp.exp(wtx - xd) / jnp.sqrt(jnp.float32(M))
        h = layernorm(x, n1_g, n1_b)
        kqv = h @ kqv_w + kqv_b
        k, q, v = jnp.split(kqv, 3, axis=-1)
        kp = prm_exp(k, w)
        qp = prm_exp(q, w)
        D = jnp.einsum('btm,bm->bt', qp, jnp.sum(kp, axis=1))[..., None]
        kptv = jnp.einsum('btn,btm->bnm', v, kp)
        y = jnp.einsum('btm,bnm->btn', qp, kptv) / (D + EPS_ATTN)
        y = v + (y @ proj_w + proj_b)
        h2 = layernorm(y, n2_g, n2_b)
        h2 = jax.nn.gelu(h2 @ mlp_w1 + mlp_b1, approximate=False)
        h2 = h2 @ mlp_w2 + mlp_b2
        return y + h2

    def _L0_ffn_ref(hidden_states, router_w, w1, b1, w2, b2):
        import jax, jax.numpy as jnp
        import numpy as np
        E = 64
        K = 2
        CAP = 512
        H = 512
        FFN = 128
        B, S = (8, 256)
        orig_shape = hidden_states.shape
        x = hidden_states.reshape(-1, orig_shape[-1])
        T = x.shape[0]
        N = T * K
        logits = jnp.einsum('th,eh->te', x, router_w)
        probs_full = jax.nn.softmax(logits, axis=-1)
        probs, idx = jax.lax.top_k(probs_full, K)
        flat_e = idx.reshape(-1)
        flat_p = probs.reshape(-1)
        order = jnp.argsort(flat_e, stable=True)
        sorted_e = flat_e[order]
        counts = jnp.zeros((E,), jnp.int32).at[flat_e].add(1)
        offsets = jnp.concatenate([jnp.zeros((1,), jnp.int32), jnp.cumsum(counts)[:-1]])
        pos = jnp.arange(N, dtype=jnp.int32) - offsets[sorted_e]
        keep = pos < CAP
        slot = sorted_e * CAP + jnp.minimum(pos, CAP - 1)
        dest = jnp.where(keep, slot, E * CAP)
        tok = order // K
        buf = jnp.zeros((E * CAP + 1, x.shape[-1]), x.dtype).at[dest].set(x[tok])
        buf = buf[:-1]
        h = jax.nn.gelu(jnp.einsum('nh,fh->nf', buf, w1) + b1, approximate=False)
        y = jnp.einsum('nf,hf->nh', h, w2) + b2
        gate = jnp.where(keep, flat_p[order], 0.0)
        contrib = y[jnp.minimum(slot, E * CAP - 1)] * gate[:, None]
        out = jnp.zeros_like(x).at[tok].add(contrib)
        return out.reshape(orig_shape)

    def _L1_gnn_ref(x, batch, edge_index, norm1_g, norm1_b, norm2_g, norm2_b, W_conv, b_conv, Wq, Wk, Wv, Wo, proj):
        import jax, jax.numpy as jnp
        import numpy as np
        B = 32
        MAXN = 128
        HEADS = 8
        DH = 64
        M = 256
        D = 512
        EPS = 1e-05
        KEPS = 1e-06

        def _batchnorm(x, g, b):
            mu = jnp.mean(x, axis=0)
            var = jnp.mean((x - mu) ** 2, axis=0)
            return (x - mu) * jax.lax.rsqrt(var + EPS) * g + b

        def _forward(x, batch, edge_index, norm1_g, norm1_b, norm2_g, norm2_b, W_conv, b_conv, Wq, Wk, Wv, Wo, proj):
            N = x.shape[0]
            E = edge_index.shape[1]
            h = x
            xn = _batchnorm(x, norm1_g, norm1_b)
            msg = xn[edge_index[0]]
            agg = jax.ops.segment_sum(msg, edge_index[1], num_segments=N)
            deg = jax.ops.segment_sum(jnp.ones((E,), x.dtype), edge_index[1], num_segments=N)
            agg = agg / jnp.maximum(deg, 1.0)[:, None]
            conv_out = jax.nn.relu(agg @ W_conv + b_conv)
            counts = jax.ops.segment_sum(jnp.ones((N,), jnp.int32), batch, num_segments=B)
            offsets = jnp.concatenate([jnp.zeros((1,), jnp.int32), jnp.cumsum(counts)[:-1]])
            pos = jnp.arange(N, dtype=jnp.int32) - offsets[batch]
            h_dense = jnp.zeros((B, MAXN, D), x.dtype).at[batch, pos].set(h)
            mask = jnp.zeros((B, MAXN), bool).at[batch, pos].set(True)

            def heads(t, W):
                return (t @ W).reshape(B, MAXN, HEADS, DH).transpose(0, 2, 1, 3)
            q, k, v = (heads(h_dense, Wq), heads(h_dense, Wk), heads(h_dense, Wv))
            scale = DH ** (-0.25)

            def phi(t, is_query):
                t = t * scale
                u = jnp.einsum('bhnd,md->bhnm', t, proj)
                diag = 0.5 * jnp.sum(t * t, axis=-1, keepdims=True)
                if is_query:
                    m_ = jnp.max(u, axis=-1, keepdims=True)
                else:
                    m_ = jnp.max(u, axis=(-2, -1), keepdims=True)
                return jnp.exp(u - diag - jax.lax.stop_gradient(m_)) / np.sqrt(M) + KEPS
            qf = phi(q, True)
            kf = phi(k, False) * mask[:, None, :, None]
            vm = v * mask[:, None, :, None]
            kv = jnp.einsum('bhnm,bhnd->bhmd', kf, vm)
            z = 1.0 / (jnp.einsum('bhnm,bhm->bhn', qf, kf.sum(axis=2)) + KEPS)
            attn = jnp.einsum('bhnm,bhmd->bhnd', qf, kv) * z[..., None]
            attn = attn.transpose(0, 2, 1, 3).reshape(B, MAXN, D) @ Wo
            h_attn = attn[batch, pos]
            return _batchnorm(conv_out + h_attn + h, norm2_g, norm2_b)
        return _forward(x, batch, edge_index, norm1_g, norm1_b, norm2_g, norm2_b, W_conv, b_conv, Wq, Wk, Wv, Wo, proj)

    def _L1_mix_ref(x, w_qkv, w_proj, b_proj):
        import jax, jax.numpy as jnp
        import numpy as np
        DIM = 512
        HEADS = 8
        HEAD_DIM = DIM // HEADS
        SCALE = HEAD_DIM ** (-0.5)

        def phi(t):
            return jax.nn.elu(t) + 1.0
        B, N, C = x.shape
        H, D = (HEADS, C // HEADS)
        qkv = x @ w_qkv.T
        qkv = qkv.reshape(B, N, 3, H, D).transpose(2, 0, 3, 1, 4)
        q, k, v = (qkv[0], qkv[1], qkv[2])
        kv = jnp.einsum('bhnd,bhne->bhde', phi(k), v) * SCALE
        out = jnp.einsum('bhnd,bhde->bhne', phi(q), kv)
        out = out.transpose(0, 2, 1, 3).reshape(B, N, C)
        return out @ w_proj.T + b_proj

    def _L1_ffn_ref(x, Wg, bg, W1, b1, W2, b2):
        import jax, jax.numpy as jnp
        import numpy as np
        H = 512
        FF = 4 * H
        E = 8
        K = 2
        B, S = (4, 256)
        logits = x @ Wg + bg
        w, idx = jax.lax.top_k(logits, K)
        w = jax.nn.softmax(w, axis=-1)
        h = jax.nn.silu(jnp.einsum('bsh,ehf->ebsf', x, W1) + b1[:, None, None, :])
        y = jnp.einsum('ebsf,efh->ebsh', h, W2) + b2[:, None, None, :]
        comb = jnp.einsum('bske,bsk->ebs', jax.nn.one_hot(idx, E, dtype=x.dtype), w)
        return jnp.einsum('ebsh,ebs->bsh', y, comb)
    edge_index = jnp.stack([src, dst])
    batch0 = jnp.zeros((625,), jnp.int32)
    xn = _layernorm(x, axis=-1)
    x = x + _L0_gnn_ref(xn, edge_index, edge_type_2, L0_gnn_basis1, L0_gnn_att1, L0_gnn_gate_w1, L0_gnn_root1, L0_gnn_bias1, L0_gnn_basis2, L0_gnn_att2, L0_gnn_gate_w2, L0_gnn_root2, L0_gnn_bias2) + _L0_mix_ref(xn[None], L0_mix_kqv_w, L0_mix_kqv_b, L0_mix_proj_w, L0_mix_proj_b, L0_mix_n1_g, L0_mix_n1_b, L0_mix_n2_g, L0_mix_n2_b, L0_mix_mlp_w1, L0_mix_mlp_b1, L0_mix_mlp_w2, L0_mix_mlp_b2, L0_mix_w)[0]
    x = x + _L0_ffn_ref(_layernorm(x, axis=-1)[None], L0_ffn_router_w, L0_ffn_w1, L0_ffn_b1, L0_ffn_w2, L0_ffn_b2)[0]
    xn = _layernorm(x, axis=-1)
    x = x + _L1_gnn_ref(xn, batch0, edge_index, L1_gnn_norm1_g, L1_gnn_norm1_b, L1_gnn_norm2_g, L1_gnn_norm2_b, L1_gnn_W_conv, L1_gnn_b_conv, L1_gnn_Wq, L1_gnn_Wk, L1_gnn_Wv, L1_gnn_Wo, L1_gnn_proj) + _L1_mix_ref(xn[None], L1_mix_w_qkv, L1_mix_w_proj, L1_mix_b_proj)[0]
    x = x + _L1_ffn_ref(_layernorm(x, axis=-1)[None], L1_ffn_Wg, L1_ffn_bg, L1_ffn_W1, L1_ffn_b1, L1_ffn_W2, L1_ffn_b2)[0]
    return x

_drawn_inputs = setup_inputs


def setup_inputs(seed=0):
    import zlib

    import numpy as np

    out = dict(_drawn_inputs(seed))
    spreads = {'L0_mix_kqv_b': (0.0, 0.1),
     'L0_mix_proj_b': (0.0, 0.1),
     'L0_mix_n1_g': (1.0, 0.6),
     'L0_mix_n1_b': (0.0, 0.1),
     'L0_mix_n2_g': (1.0, 0.2),
     'L0_mix_n2_b': (0.0, 0.1),
     'L0_mix_mlp_b1': (0.0, 0.1),
     'L0_mix_mlp_b2': (0.0, 0.1),
     'L0_ffn_b1': (0.0, 2.0),
     'L0_ffn_b2': (0.0, 0.8),
     'L1_gnn_norm1_g': (1.0, 0.6),
     'L1_gnn_norm1_b': (0.0, 2.0),
     'L1_gnn_norm2_g': (1.0, 0.6),
     'L1_gnn_norm2_b': (0.0, 2.0),
     'L1_gnn_b_conv': (0.0, 2.0),
     'L1_ffn_bg': (0.0, 2.0),
     'L1_ffn_b1': (0.0, 2.0),
     'L1_ffn_b2': (0.0, 2.0)}
    factors = {'L0_gnn_basis1': 8.0,
     'L0_gnn_att1': 8.0,
     'L0_gnn_gate_w1': 8.0,
     'L0_gnn_root1': 8.0,
     'L0_gnn_bias1': 8.0,
     'L0_gnn_basis2': 8.0,
     'L0_gnn_att2': 8.0,
     'L0_gnn_gate_w2': 8.0,
     'L0_gnn_root2': 4.848,
     'L0_gnn_bias2': 4.484,
     'L0_ffn_router_w': 44.801,
     'L0_ffn_w1': 5.923,
     'L1_gnn_W_conv': 64.0,
     'L1_gnn_Wq': 8.0,
     'L1_gnn_Wk': 8.0,
     'L1_gnn_Wv': 64.0,
     'L1_gnn_Wo': 64.0,
     'L1_gnn_proj': 8.0,
     'L1_mix_b_proj': 64.0,
     'L1_ffn_Wg': 64.0,
     'L1_ffn_W1': 64.0,
     'L1_ffn_W2': 64.0}
    for name, (base, spread) in spreads.items():
        noise = np.random.default_rng([zlib.crc32(name.encode()), seed]).standard_normal(out[name].shape)
        drawn = base * np.exp(spread * noise) if base else spread * noise
        out[name] = jnp.asarray(drawn.astype(out[name].dtype))
    for name, factor in factors.items():
        out[name] = (out[name] * factor).astype(out[name].dtype)
    return out
```

```python
import concourse.bass as bass
from concourse import mybir
from contextlib import ExitStack

N = 625
H = 512
NE = 10000
P = 125
TT = N // P
KT = H // 128
ET = NE // P
EP = ET // 2
NB = 30
M = 256
E0 = 64
CAP = 512
F0 = 128
E1, F1 = 8, 2048
HEADS, DH = 8, 64
NA = 128
HALF = ((0, 312), (312, 313))
ROW = TT * H
COLW = 626
SLOT = 2624

COLS = [("n1_g", 4), ("n1_b", 4), ("kq_b", 8), ("n2_g", 4), ("n2_b", 4), ("mlp_b1", 4), ("bias1", 4),
        ("ffn_b1", 1), ("b_conv", 4), ("g1", 4), ("b1n", 4), ("g2", 4), ("b2n", 4), ("b_proj", 4)]
COL_AT, _at = {}, 0
for _n, _c in COLS:
    COL_AT[_n] = _at
    _at += _c
NCOLS = _at
ROWS = {"v_b": 0, "proj_b": 1, "mlp_b2": 2, "bias2": 3, "ffn_b2": 4}

PSUM_ORDER = [("xnT", 5), ("hT", 5), ("rng", 1), ("A", 20),
              ("kq", 16), ("v", 5), ("wk", 3), ("xdk", 1), ("wq", 3), ("xdq", 1),
              ("qpT", 5), ("kptv", 2), ("ks", 1), ("D", 1), ("yT", 8), ("proj", 5), ("h2T", 5), ("m1", 8), ("m2", 5),
              ("gate1", 1), ("Z1", 16), ("h1T", 8), ("gate2", 1), ("h1r", 5), ("Z2", 16), ("o2", 5),
              ("xfT", 5), ("rt", 1), ("hf", 2), ("pos", 1), ("fy", 5),
              ("AnT", 7), ("xn2T", 5), ("xbr", 5), ("agg", 8), ("conv", 8),
              ("aq", 1), ("ak", 1), ("av", 1), ("ad", 1), ("uk", 4), ("uq", 4), ("kv", 3), ("qfT", 4),
              ("at", 2), ("atT", 1), ("ha", 1),
              ("xq", 8), ("xk", 5), ("xv", 5), ("xkv", 1), ("xo", 8), ("xp", 8), ("x3r", 5),
              ("xeT", 5), ("el", 1), ("en", 1), ("combT", 2), ("eb2", 5)]
TILE0, _at = {}, 0
for _n, _c in PSUM_ORDER:
    TILE0[_n] = _at
    _at += _c
ACT_READS = [("xnT", 5), ("hT", 5), ("A", 20), ("kq", 16), ("v", 5), ("xdk", 1), ("wk", 5), ("xdq", 1), ("wq", 5),
             ("qpT", 5), ("kptv", 2), ("ks", 1), ("yT", 8), ("proj", 5), ("h2T", 5), ("m1", 8), ("m2", 5),
             ("gate1", 1), ("Z1", 16), ("h1T", 8), ("gate2", 1), ("h1r", 5), ("Z2", 16), ("xfT", 5), ("hf", 2),
             ("AnT", 7), ("xn2T", 5), ("xbr", 5), ("agg", 8), ("conv", 8), ("aq", 1), ("ak", 1), ("av", 1), ("ad", 1),
             ("uk", 8), ("uq", 8), ("kv", 3), ("qfT", 4), ("atT", 1), ("ha", 1), ("xv", 5), ("xo", 8), ("xeT", 5),
             ("combT", 2)]
READ0, _at = {}, 0
for _n, _c in ACT_READS:
    READ0[_n] = _at
    _at += _c


def gps_two_layers(nc, I, out):
    f32, f16, i32, f32r = mybir.dt.float32, mybir.dt.float16, mybir.dt.int32, mybir.dt.float32r
    ALU, ACT, AX = mybir.AluOpType, mybir.ActivationFunctionType, mybir.AxisListType
    ctx = ExitStack()
    with ctx:
        def sb(name, shape, dt=f32):
            return ctx.enter_context(nc.sbuf_tensor(name, shape, dt))

        sems = {}

        def S(name):
            if name not in sems:
                sems[name] = ctx.enter_context(nc.semaphore(name))
            return sems[name]

        slot = [None] * 8
        slot[0], slot[7] = sb("slot0", [128, SLOT]), sb("slot7", [128, SLOT])
        bank = [ctx.enter_context(nc.psum_tensor(f"bank{i}", [128, 512], f32)) for i in range(8)]
        ident = sb("ident", [128, 128])
        ones = sb("ones", [128, 128])
        tri = sb("tri", [P, P])
        tmp = sb("tmp", [128, 2, 512])
        zero = sb("zero", [1, 320], f16)
        cols = sb("cols", [128, NCOLS])
        att = sb("att", [128, 2, 2, NB])
        gate_w = sb("gate_w", [128, 2, KT, 2])
        eps = sb("eps", [128, 3])
        st = sb("st", [128, TT, 6])
        mv = sb("mv", [128, TT, 2])
        sd = sb("sd", [128, TT])
        rs = sb("rs", [128, TT])
        gates = sb("gates", [P, 2, TT, 2])
        edges = sb("edges", [P, 3, ET], i32)
        small = sb("small", [128, 1024])
        rng_i = sb("rng_i", [1, 16], i32)
        el_i = sb("el_i", [1, 16], i32)

        with ExitStack() as before:
            def sb_before(name, shape, dt=f32):
                return before.enter_context(nc.sbuf_tensor(name, shape, dt))

            for i in range(1, 7):
                slot[i] = sb_before(f"slot{i}", [128, SLOT])
            AT = sb_before("AT", [P, 2, TT, N])
            weights = sb_before("weights", [128, 20736])
        sb("_slots12", [128, 2 * SLOT])
        xe_hi, xe_lo = (sb(name, [128, KT, COLW], f32r) for name in ("xe_hi", "xe_lo"))
        sb("_slots56", [128, 4 * SLOT - 2 * KT * COLW])
        hid_hi, hid_lo = (sb(name, [128, 4, COLW], f32r) for name in ("hid_hi", "hid_lo"))
        sb("_rest_of_AT", [128, 2 * TT * N - 8 * COLW])
        sb("_raw_chunks", [128, 8192])
        ew_hi, ew_lo = (sb(name, [128, 2, 2048], f32r) for name in ("ew_hi", "ew_lo"))
        sb("_rest_of_weights", [128, 20736 - 16384])

        def row(s):
            return slot[s][0:P, 0:ROW].rearrange("p (j n) -> p j n", j=TT)

        def col(s):
            return slot[s][:, 0:KT * COLW].rearrange("p (k t) -> p k t", k=KT)

        def wmat(at, k=KT, n=H):
            return weights[:, at:at + k * n].rearrange("p (k n) -> p k n", k=k)

        def rowvec(name):
            return slot[7][0:P, ROWS[name] * H:(ROWS[name] + 1) * H]

        def colvec(name, k):
            return cols[:, COL_AT[name] + k:COL_AT[name] + k + 1]

        x, xn, xnT = row(0), row(1), col(2)
        basis = [wmat(2048 * u) for u in range(2)]
        wrel = [[wmat(4096 + 2048 * (2 * l + r)) for r in range(2)] for l in range(2)]
        kqv_w = wmat(12288, KT, 3 * H)
        proj_w, mlp_w1, mlp_w2 = wmat(12288), wmat(14336), wmat(16384)
        root = [wmat(12288), wmat(14336)]
        prm_w = wmat(18432, KT, M)
        ffn_rt, ffn_w1, ffn_w2 = wmat(19456, KT, E0), wmat(19712, KT, F0), weights[:, 20224:20736]
        Wq, Wk, Wv, Wo = wmat(0), wmat(2048), wmat(4096), wmat(6144)
        W_conv, w_proj2, w_qkv = wmat(8192), wmat(10240), wmat(12288, KT, 3 * H)
        projT = weights[:, 18432:18432 + M]
        Wg = wmat(18688, KT, E1)
        oh = weights[0:P, 8192:8192 + 1600].bitcast(f16)
        oh_src = [oh[:, 626 * u:626 * u + N] for u in range(2)]
        oh_dst = [oh[:, 1252 + 250 * u:1252 + 250 * u + 250] for u in range(2)]
        iota_src = oh[:, 1752:1752 + N]
        iota_dst = oh[:, 2378:2378 + 250]
        srcf = small[0:P, 0:ET]
        keyf = small[0:P, ET:ET * (1 + TT)].rearrange("p (j t) -> p j t", j=TT)
        dstf, relf = small[0:P, 480:560], small[0:P, 560:640]
        pres = tmp[0:P, 0, 0:TT * ET].rearrange("p (j t) -> p j t", j=TT)
        gez = tmp[0:P, 1, 0:TT * ET].rearrange("p (j t) -> p j t", j=TT)
        rg = small[0:1, 640:960]
        AT0 = AT[:, 0, :, :].rearrange("p j s -> p (j s)")
        AT1 = AT[:, 1, :, :].rearrange("p j s -> p (j s)")
        An = AT[:, 1, :, :]

        def raw1(c):
            return wmat(2048 * (c % 4), KT, 256)

        def raw2(c):
            return wmat(2048 * (c % 4) + 1024, 2, H)

        def w1_half(t, f):
            return t[:, f // 2 % 2, 0:1024].rearrange("p (k f) -> p k f", k=KT)[:, :, 128 * (f % 2):128 * (f % 2) + 128]

        def w2_half(t, f):
            return t[:, f // 2 % 2, 1024 + H * (f % 2):1024 + H * (f % 2) + H]

        eb1 = sb("eb1", [128, E1 * F1 // 128])
        eb1_now = sb("eb1_now", [128, F1 // 128])
        eb2 = slot[7][0:E1, 512:1024]
        combT = slot[7][0:E1, 1024:1024 + N]

        aqT = slot[1][:, 0:512].rearrange("p (k t) -> p k t", k=KT)
        akT = slot[1][:, 512:1024].rearrange("p (k t) -> p k t", k=KT)
        sq_aq = slot[1][:, 1024:1536].rearrange("p (k t) -> p k t", k=KT)
        sq_ak = slot[1][:, 1536:2048].rearrange("p (k t) -> p k t", k=KT)
        haT = slot[1][:, 2048:2560].rearrange("p (k t) -> p k t", k=KT)
        qe = slot[3][:, 0:HEADS * M].rearrange("p (h m) -> p h m", h=HEADS)
        ke = slot[4][:, 0:HEADS * M].rearrange("p (h m) -> p h m", h=HEADS)
        qfT = slot[5][:, 0:HEADS * M].rearrange("p (h c t) -> p h c t", h=HEADS, c=2)
        v_aug = slot[7][:, 0:HEADS * (DH + 1)].rearrange("p (h d) -> p h d", h=HEADS)
        attn = slot[7][:, 520:1032]
        attnT = slot[7][:, 1032:1544].rearrange("p (k t) -> p k t", k=KT)
        kv_sb = slot[7][:, 1544:1544 + 1040].rearrange("p (g d) -> p g d", g=16)
        halfsum = sb("halfsum", [128, 2])
        kvb = slot[7][:, 0:512].rearrange("p (k e) -> p k e", k=KT)
        adiag = small[:, 16:32]
        amax_k, amax_kr, amax_q, abias_k, abias_q = (small[:, 32 + 8 * i:40 + 8 * i] for i in range(5))
        aden = small[:, 72:80]
        hid = col(5)
        comb = small[0:P, 128:128 + TT * E1].rearrange("p (j e) -> p j e", j=TT)

        kp = slot[4][0:P, 0:TT * M].rearrange("p (j m) -> p j m", j=TT)
        qp = slot[4][0:P, TT * M:2 * TT * M].rearrange("p (j m) -> p j m", j=TT)
        qpT = slot[6][:, 0:2 * COLW].rearrange("p (c t) -> p c t", c=2)
        kptvT = slot[6][:, 1252:1252 + 1024].rearrange("p (c n) -> p c n", c=2)
        xdk, xdq, ksum, rD = small[0:P, 960:965], small[0:P, 965:970], small[:, 970:972], small[0:P, 972:977]
        hfT = slot[3][:, 0:N]
        HEAD_ORDER = [0, 2, 1, 3, 4, 6, 5, 7]

        def ub(stage, h):
            at = HEAD_ORDER.index(h)
            return B(stage, at // 2)[:, M * (at % 2):M * (at % 2) + M]

        def table(s, i, e):
            return slot[s][0:P, TT * e * i:TT * e * (i + 1)].rearrange("p (j e) -> p j e", j=TT)

        rtp, eexp = table(6, 1, E0), small[0:P, 40:45]
        iota_e = sb("iota_e", [128, E0])

        def B(stage, n=0):
            return bank[(TILE0[stage] + n) % 8]

        freed = {}
        for name, count in PSUM_ORDER:
            for n in range(count):
                freed[TILE0[name] + n] = (name, n + 1)
        for n in range(4):
            freed[TILE0["uk"] + n] = ("uk", 2 * n + 2)
            freed[TILE0["uq"] + n] = ("uq", 2 * n + 2)
        for n in range(3):
            freed[TILE0["wk"] + n] = ("wk", min(2 * n + 2, TT))
            freed[TILE0["wq"] + n] = ("wq", min(2 * n + 2, TT))

        def filled(stage, count):
            return TILE0[stage] + count

        def claim(pe, stage, n=0):
            g = TILE0[stage] + n
            if g >= 8:
                name, value = freed[g - 8]
                if name in READ0:
                    pe.wait_ge(S("act_read"), READ0[name] + value)
                else:
                    pe.wait_ge(S(name + "_out"), value)
            return B(stage, n)

        block = ctx.enter_context(nc.Block())

        @block.sync
        def _(sp):
            def load(dst, src, name):
                sp.dma_start(dst, src).then_inc(S(name), 16)

            load(x, I["x"].rearrange("(j p) n -> p j n", p=P), "x_in")
            load(edges[:, :, :], I["edges"], "edges_in")
            load(att[:, :, :, :], I["att"].partition_broadcast(128), "att_in")
            for l in range(2):
                b = I[f"L0_gnn_basis{l + 1}"].rearrange("b (k p) n -> b p k n", p=128)
                done = S(f"w{l}_sum")
                for u in range(2):
                    if l == 1:
                        sp.wait_ge(S("w0_sum"), 4 * 14 + 2 * u + 2)
                    load(basis[u], b[u], f"basis_in{u}")
                with sp.Fori(1, NB // 2) as p:
                    for u in range(2):
                        sp.wait_ge(done, 4 * p + (2 * u - 2))
                        sp.dma_start(basis[u], b[bass.ds(2 * p + u, 1)].rearrange("o p k n -> (o p) k n")).then_inc(S(f"basis_in{u}"), 16)
            sp.wait_ge(S("w1_sum"), 4 * 15)
            load(Wq, I["L1_gnn_Wq"].rearrange("(k p) n -> p k n", p=128), "Wqkvo_in")
            load(Wk, I["L1_gnn_Wk"].rearrange("(k p) n -> p k n", p=128), "Wqkvo_in")
            sp.wait_ge(S("psum_full"), filled("h1T", 8))
            load(Wv, I["L1_gnn_Wv"].rearrange("(k p) n -> p k n", p=128), "Wqkvo_in")
            load(Wo, I["L1_gnn_Wo"].rearrange("(k p) n -> p k n", p=128), "Wqkvo_in")
            sp.wait_ge(S("psum_full"), filled("o2", 5))
            load(W_conv, I["L1_gnn_W_conv"].rearrange("(k p) n -> p k n", p=128), "Wconv_in")
            load(projT[0:64, :], I["projT"], "projT_in")
            load(projT[64:128, :], I["projT"], "projT_in")
            load(w_qkv, I["w_qkvT"].rearrange("(k p) n -> p k n", p=128), "wqkv_in")
            load(w_proj2, I["w_projT"].rearrange("(k p) n -> p k n", p=128), "wproj_in")
            load(Wg, I["L1_ffn_Wg"].rearrange("(k p) n -> p k n", p=128), "Wg_in")
            load(small[0:P, 0:E1], I["L1_ffn_bg"].partition_broadcast(P), "Wg_in")
            load(eb1[:, :], I["eb1"], "eb_in")
            sp.wait_ge(S("psum_full"), filled("ha", 1))
            load(eb2, I["L1_ffn_b2"], "eb_in")
            sp.wait_ge(S("elist"), 1)
            sp.wait_ge(S("psum_full"), filled("xp", 8))
            n_act = sp.value_load(el_i[0:1, 8:9], min_val=2, max_val=E1)
            w1v = I["L1_ffn_W1"].rearrange("e (k p) f -> e p k f", p=128)
            w2v = I["L1_ffn_W2"].rearrange("e (f p) n -> e p f n", p=128)

            def load_chunk(e, c):
                w1c, w2c = raw1(c), raw2(c)
                sp.dma_start(w1c, w1v[bass.ds(e, 1), :, :, 256 * c:256 * c + 256].rearrange("o p k f -> (o p) k f")).then_inc(S(f"ew_in{c % 4}"), 16)
                sp.dma_start(w2c, w2v[bass.ds(e, 1), :, 2 * c:2 * c + 2, :].rearrange("o p f n -> (o p) f n")).then_inc(S(f"ew_in{c % 4}"), 16)

            e = sp.value_load(el_i[0:1, 0:1], min_val=0, max_val=E1 - 1)
            for c in range(8):
                if c >= 4:
                    sp.wait_ge(S("ew_split"), c - 3)
                load_chunk(e, c)
            with sp.Fori(0, n_act - 1) as it:
                e = sp.value_load(el_i[0:1, bass.ds(it + 1, 1)], min_val=0, max_val=E1 - 1)
                for c in range(8):
                    sp.wait_ge(S("ew_split"), 8 * it + c + 5)
                    load_chunk(e, c)
            sp.wait_ge(S("result"), 1)
            sp.dma_start(out.rearrange("(j p) n -> p j n", p=P), x).then_inc(S("stored"), 16)
            sp.wait_ge(S("stored"), 16)

        @block.gpsimd
        def _(pool):
            step = [0]

            def link(ins):
                step[0] += 1
                ins.then_inc(S("pool_step"), 1)
                pool.wait_ge(S("pool_step"), step[0])

            link(pool.memset(ident[:, :], 0.0))
            link(pool.memset(ones[:, :], 1.0))
            link(pool.memset(zero[:, :], 0.0))
            link(pool.memset(halfsum[:, :], 0.5))
            link(pool.memset(eps[:, 0:1], 1e-5))
            link(pool.memset(eps[:, 1:2], 1e-3))
            link(pool.memset(eps[:, 2:3], -0.5))
            link(pool.affine_select(out=ident[:, :], in_=ident[:, :], compare_op=ALU.not_equal, fill=1.0,
                                    base=0, pattern=[[-1, 128]], channel_multiplier=1))
            link(pool.affine_select(out=tri[:, :], in_=ones[0:P, 0:P], compare_op=ALU.is_gt, fill=0.0,
                                    base=0, pattern=[[1, P]], channel_multiplier=-1))
            link(pool.affine_select(out=halfsum[:, 0:1], in_=halfsum[:, 0:1], compare_op=ALU.is_ge, fill=0.0,
                                    base=63, pattern=[[0, 1]], channel_multiplier=-1))
            link(pool.affine_select(out=halfsum[:, 1:2], in_=halfsum[:, 1:2], compare_op=ALU.is_ge, fill=0.0,
                                    base=-64, pattern=[[0, 1]], channel_multiplier=1))
            link(pool.iota(iota_src, pattern=[[1, N]], base=0, channel_multiplier=0, allow_small_or_imprecise_dtypes=True))
            link(pool.iota(iota_e[:, :], pattern=[[1, E0]], base=0, channel_multiplier=0, allow_small_or_imprecise_dtypes=True))
            pool.iota(iota_dst, pattern=[[1024, 2], [1, P]], base=0, channel_multiplier=0,
                      allow_small_or_imprecise_dtypes=True).then_inc(S("consts"), 1)

            pool.wait_ge(S("rows_in"), 16 * len(ROWS))
            for j in range(TT):
                pool.wait_ge(S("act_read"), READ0["v"] + j + 1)
                pool.tensor_tensor(row(3)[:, j, :], row(3)[:, j, :], rowvec("v_b"), ALU.add).then_inc(S("vrow"), 1)
            pool.wait_ge(S("vrow"), 5)
            pool.wait_ge(S("psum_full"), filled("kptv", 2))
            for j in range(TT):
                pool.tensor_tensor(row(3)[:, j, :], row(3)[:, j, :], rowvec("proj_b"), ALU.add).then_inc(S("vb"), 1)
            for j in range(TT):
                pool.wait_ge(S("act_read"), READ0["proj"] + j + 1)
                pool.wait_ge(S("vb"), j + 1)
                pool.tensor_tensor(row(4)[:, j, :], row(4)[:, j, :], row(3)[:, j, :], ALU.add).then_inc(S("y_row"), 1)
            link(pool.tensor_tensor(rowvec("mlp_b2"), rowvec("mlp_b2"), rowvec("bias2"), ALU.add))
            pool.wait_ge(S("xn_row"), 5)
            for j in range(TT):
                link(pool.tensor_tensor(x[:, j, :], x[:, j, :], rowvec("mlp_b2"), ALU.add))
            pool.wait_ge(S("y_row"), 5)
            for j in range(TT):
                pool.tensor_tensor(x[:, j, :], x[:, j, :], row(4)[:, j, :], ALU.add).then_inc(S("x_y"), 1)
            for j in range(TT):
                pool.wait_ge(S("act_read"), READ0["m2"] + j + 1)
                pool.wait_ge(S("x_y"), j + 1)
                pool.tensor_tensor(x[:, j, :], x[:, j, :], row(5)[:, j, :], ALU.add).then_inc(S("x_mix"), 1)

            pool.wait_ge(S("psum_full"), filled("Z2", 16))
            pool.tensor_tensor(AT0, AT0, AT1, ALU.add).then_inc(S("A_sum"), 1)
            pool.wait_ge(S("act_read"), READ0["ak"] + 1)
            pool.tensor_tensor(sq_ak, akT, akT, ALU.mult).then_inc(S("a_sq"), 1)
            pool.wait_ge(S("act_read"), READ0["aq"] + 1)
            pool.tensor_tensor(sq_aq, aqT, aqT, ALU.mult).then_inc(S("a_sq"), 1)
            pool.wait_ge(S("kmax"), 1)
            pool.partition_all_reduce(amax_kr, amax_k, 128, bass.bass_isa.ReduceOp.max).then_inc(S("kmax_all"), 1)
            pool.wait_ge(S("psum_full"), filled("xo", 8))
            link(pool.memset(xe_hi[:, :, N:COLW].bitcast(f32), 0.0))
            pool.memset(xe_lo[:, :, N:COLW].bitcast(f32), 0.0).then_inc(S("x_pad"), 1)

        @block.scalar
        def _(act):
            def load(dst, src, name):
                act.dma_start(dst, src).then_inc(S(name), 16)

            step = [0]

            def link(ins):
                step[0] += 1
                ins.then_inc(S("act_step"), 1)
                act.wait_ge(S("act_step"), step[0])

            def sqrt_for(n, e):
                act.wait_ge(S("ln_var"), n + 1)
                act.activation(sd[:, :] if e == 2 else sd[0:P, :], mv[0:P, :, 1:2].rearrange("p j o -> p (j o)"), ACT.Sqrt,
                               bias=eps[0:P, e:e + 1]).then_inc(S("ln_std"), 1)

            def copy_out(stage, n, dst, src, func=ACT.Copy, **kw):
                act.wait_ge(S("psum_full"), filled(stage, n + 1))
                act.activation(dst, src, func, **kw).then_inc(S("act_read"), 1)

            def transposed(stage, dst):
                for j in range(TT):
                    copy_out(stage, j, dst[:, :, P * j:P * j + P], B(stage, j)[:, 0:KT * P].rearrange("p (k t) -> p k t", k=KT))

            load(cols[:, :], I["cols"], "cols_in")
            load(kqv_w, I["L0_mix_kqv_w"].rearrange("(k p) n -> p k n", p=128), "kqv_in")
            load(prm_w, I["prm_wT"].rearrange("(k p) n -> p k n", p=128), "prm_in")
            load(gate_w[:, :, :, :], I["gate_w"], "gate_in")
            for name in ROWS:
                load(rowvec(name), I["row_" + name].partition_broadcast(P), "rows_in")
            load(ffn_rt, I["router_wT"].rearrange("(k p) n -> p k n", p=128), "ffn_in")
            load(ffn_w1, I["ffn_w1T"].rearrange("(k p) n -> p k n", p=128), "ffn_in")
            load(ffn_w2, I["ffn_w2T"], "ffn_in")

            act.wait_ge(S("consts"), 1)
            sqrt_for(0, 0)
            sqrt_for(1, 1)
            transposed("xnT", xnT)
            act.wait_ge(S("cols_in"), 16)
            for j in range(TT):
                act.wait_ge(S("psum_full"), filled("hT", j + 1))
                for k in range(KT):
                    ins = act.activation(col(4)[:, k, P * j:P * j + P], B("hT", j)[:, P * k:P * k + P], ACT.Identity,
                                         scale=colvec("n1_g", k), bias=colvec("n1_b", k))
                ins.then_inc(S("act_read"), 1)
            for j in range(TT):
                for q in range(4):
                    r, (a, w) = q // 2, HALF[q % 2]
                    copy_out("A", 4 * j + q, AT[:, r, j, a:a + w], B("A", 4 * j + q)[0:P, 0:w])
            for n in range(16):
                m, (a, w) = n // 2, HALF[n % 2]
                copy_out("kq", n, col(5 if m < 4 else 6)[:, m % 4, a:a + w], B("kq", n)[:, 0:w], ACT.Identity, bias=colvec("kq_b", m))
            for j in range(TT):
                copy_out("v", j, row(3)[:, j, :], B("v", j)[0:P, :])
            act.wait_ge(S("act_read"), READ0["kq"] + 8)
            act.activation(col(4)[:, :, 0:N], col(5)[:, :, 0:N], ACT.Square).then_inc(S("sqk"), 1)
            load(proj_w, I["L0_mix_proj_w"].rearrange("(k p) n -> p k n", p=128), "projw_in")
            load(mlp_w1, I["L0_mix_mlp_w1"].rearrange("(k p) n -> p k n", p=128), "mlp1_in")
            load(mlp_w2, I["L0_mix_mlp_w2"].rearrange("(k p) n -> p k n", p=128), "mlp2_in")

            def exps(w, xd, dst, xdv):
                copy_out(xd, 0, xdv, B(xd)[0:P, 0:TT])
                act.wait_ge(S("act_read"), READ0[xd] + 1)
                for j in range(TT):
                    act.wait_ge(S("psum_full"), filled(w, j // 2 + 1))
                    act.activation(dst[:, j, :], B(w, j // 2)[0:P, M * (j % 2):M * (j % 2) + M], ACT.Exp,
                                   bias=xdv[:, j:j + 1]).then_inc(S("act_read"), 1)

            exps("wk", "xdk", kp, xdk)
            act.wait_ge(S("sqk"), 1)
            act.wait_ge(S("act_read"), READ0["kq"] + 16)
            act.activation(col(5)[:, :, 0:N], col(6)[:, :, 0:N], ACT.Square).then_inc(S("sqq"), 1)
            exps("wq", "xdq", qp, xdq)
            for j in range(TT):
                copy_out("qpT", j, qpT[:, :, P * j:P * j + P], B("qpT", j)[:, 0:2 * P].rearrange("p (c t) -> p c t", c=2))
            for n in range(2):
                copy_out("kptv", n, kptvT[:, n, :], B("kptv", n)[:, :])
            copy_out("ks", 0, ksum, B("ks")[:, 0:2])
            for n in range(8):
                m, (a, w) = n // 2, HALF[n % 2]
                copy_out("yT", n, col(5)[:, m, a:a + w], B("yT", n)[:, 0:w])
            act.wait_ge(S("rD"), 1)
            for j in range(TT):
                copy_out("proj", j, row(4)[:, j, :], B("proj", j)[0:P, :], ACT.Copy, scale=rD[:, j:j + 1])
            load(root[0], I["L0_gnn_root1"].rearrange("(k p) n -> p k n", p=128), "root1_in")
            sqrt_for(2, 1)
            for j in range(TT):
                act.wait_ge(S("psum_full"), filled("h2T", j + 1))
                for k in range(KT):
                    ins = act.activation(col(5)[:, k, P * j:P * j + P], B("h2T", j)[:, P * k:P * k + P], ACT.Identity,
                                         scale=colvec("n2_g", k), bias=colvec("n2_b", k))
                ins.then_inc(S("act_read"), 1)
            for n in range(8):
                m, (a, w) = n // 2, HALF[n % 2]
                copy_out("m1", n, col(6)[:, m, a:a + w], B("m1", n)[:, 0:w], ACT.Gelu, bias=colvec("mlp_b1", m))
            load(root[1], I["L0_gnn_root2"].rearrange("(k p) n -> p k n", p=128), "root2_in")
            for j in range(TT):
                copy_out("m2", j, row(5)[:, j, :], B("m2", j)[0:P, :])

            copy_out("gate1", 0, gates[:, 0, :, :], B("gate1")[0:P, 0:2 * TT].rearrange("p (j r) -> p j r", r=2), ACT.Sigmoid)
            act.wait_ge(S("act_read"), READ0["gate1"] + 1)
            act.wait_ge(S("y_row"), 5)
            act.wait_ge(S("psum_full"), filled("h2T", 5))
            act.wait_ge(S("x_y"), 5)
            for j in range(TT):
                for r in range(2):
                    act.activation(row(3 + r)[:, j, :], xn[:, j, :], ACT.Copy, scale=gates[:, 0, j, r:r + 1]).then_inc(S("xg1"), 1)
            act.wait_ge(S("x_mix"), 5)
            for l, (Z, last) in enumerate((("Z1", "h1T"), ("Z2", "o2"))):
                if l == 1:
                    for n in range(8):
                        m, (a, w) = n // 2, HALF[n % 2]
                        copy_out("h1T", n, col(1)[:, m, a:a + w], B("h1T", n)[:, 0:w], ACT.Relu, bias=colvec("bias1", m))
                    copy_out("gate2", 0, gates[:, 1, :, :], B("gate2")[0:P, 0:2 * TT].rearrange("p (j r) -> p j r", r=2), ACT.Sigmoid)
                    act.wait_ge(S("act_read"), READ0["gate2"] + 1)
                    for j in range(TT):
                        act.wait_ge(S("psum_full"), filled("h1r", j + 1))
                        for r in range(2):
                            ins = act.activation(row(3 + r)[:, j, :], B("h1r", j)[0:P, :], ACT.Copy, scale=gates[:, 1, j, r:r + 1])
                        ins.then_inc(S("act_read"), 1)
                for n in range(16):
                    r, m, (a, w) = n // 8, n // 2 % 4, HALF[n % 2]
                    copy_out(Z, n, col(5 + r)[:, m, a:a + w], B(Z, n)[:, 0:w])

            sqrt_for(3, 0)
            transposed("xfT", col(2))
            act.wait_ge(S("rt_sub"), 1)
            act.activation(rtp, rtp, ACT.Exp).then_inc(S("rt_exp"), 1)
            for n in range(2):
                a, w = HALF[n]
                copy_out("hf", n, hfT[:, a:a + w], B("hf", n)[:, 0:w], ACT.Gelu, bias=colvec("ffn_b1", 0))
            for n in range(7):
                w = min(4, 25 - 4 * n) * P
                copy_out("AnT", n, AT1[:, 500 * n:500 * n + w], B("AnT", n)[0:P, 0:w])
            sqrt_for(4, 0)
            transposed("xn2T", col(2))
            act.wait_ge(S("bn_var"), 1)
            act.activation(sd[:, 0:KT], mv[:, 0:KT, 1:2].rearrange("p j o -> p (j o)"), ACT.Sqrt, bias=eps[:, 0:1]).then_inc(S("bn_std"), 1)
            for k in range(KT):
                act.wait_ge(S("bn1"), k + 1)
                act.activation(col(3)[:, k, 0:N], col(3)[:, k, 0:N], ACT.Identity, bias=colvec("b1n", k)).then_inc(S("xbT"), 1)
            for j in range(TT):
                copy_out("xbr", j, row(4)[:, j, :], B("xbr", j)[0:P, :])
            for n in range(8):
                m, (a, w) = n // 2, HALF[n % 2]
                copy_out("agg", n, col(5)[:, m, a:a + w], B("agg", n)[:, 0:w])
            for n in range(8):
                m, (a, w) = n // 2, HALF[n % 2]
                copy_out("conv", n, col(6)[:, m, a:a + w], B("conv", n)[:, 0:w], ACT.Relu, bias=colvec("b_conv", m))
            SC = float(DH) ** -0.25
            copy_out("aq", 0, aqT, B("aq")[:, :].rearrange("p (k t) -> p k t", k=KT), ACT.Copy, scale=SC)
            copy_out("ak", 0, akT, B("ak")[:, :].rearrange("p (k t) -> p k t", k=KT), ACT.Copy, scale=SC)
            copy_out("av", 0, v_aug[:, :, 0:DH], B("av")[:, :].rearrange("p (h d) -> p h d", h=HEADS))
            copy_out("ad", 0, adiag, B("ad")[:, 0:16])
            act.wait_ge(S("kbias"), 1)
            for h in HEAD_ORDER:
                act.activation(ke[:, h, :], ub("uk", h), ACT.Exp, bias=abias_k[:, h:h + 1]).then_inc(S("act_read"), 1)
            act.wait_ge(S("qbias"), 1)
            for h in HEAD_ORDER:
                act.activation(qe[:, h, :], ub("uq", h), ACT.Exp, bias=abias_q[:, h:h + 1]).then_inc(S("act_read"), 1)
            for n in range(3):
                w = min(6, 16 - 6 * n)
                copy_out("kv", n, kv_sb[:, 6 * n:6 * n + w, :], B("kv", n)[:, 0:65 * w].rearrange("p (g d) -> p g d", g=w))
            for n in range(4):
                copy_out("qfT", n, qfT[:, 2 * n:2 * n + 2, :, :], B("qfT", n)[:, :].rearrange("p (h c t) -> p h c t", h=2, c=2))
            copy_out("atT", 0, attnT, B("atT")[:, :].rearrange("p (k t) -> p k t", k=KT))
            copy_out("ha", 0, haT, B("ha")[:, :].rearrange("p (k t) -> p k t", k=KT))
            for n in range(8 + TT):
                act.wait_ge(S("xmin"), n + 1)
                w = HALF[n % 2][1] if n < 8 else H
                t = tmp[:, n % 2, 0:w] if n < 8 else tmp[0:P, n % 2, 0:w]
                act.activation(t, t, ACT.Exp).then_inc(S("xexp"), 1)
            for j in range(TT):
                copy_out("xv", j, row(5)[:, j, :], B("xv", j)[0:P, :])
            for n in range(8):
                m, (a, w) = n // 2, HALF[n % 2]
                copy_out("xo", n, col(1)[:, m, a:a + w], B("xo", n)[:, 0:w])
            act.wait_ge(S("bn_var"), 2)
            act.activation(sd[:, 0:KT], mv[:, 0:KT, 1:2].rearrange("p j o -> p (j o)"), ACT.Sqrt, bias=eps[:, 0:1]).then_inc(S("bn_std"), 1)
            sqrt_for(5, 0)
            transposed("xeT", col(2))
            act.wait_ge(S("el_sub"), 1)
            act.activation(eexp, eexp, ACT.Exp).then_inc(S("el_exp"), 1)
            act.wait_ge(S("elist"), 1)
            act.wait_ge(S("x_pad"), 1)
            act.wait_ge(S("act_read"), READ0["xeT"] + 5)
            act.activation(xe_hi[:, :, 0:N], col(2)[:, :, 0:N], ACT.Copy).then_inc(S("xe_high"), 1)
            for n in range(2):
                w = (500, 125)[n]
                copy_out("combT", n, combT[:, 500 * n:500 * n + w], B("combT", n)[0:E1, 0:w])
            n_act = act.value_load(el_i[0:1, 8:9], min_val=2, max_val=E1)
            with act.Fori(0, n_act) as it:
                e = act.value_load(el_i[0:1, bass.ds(it, 1)], min_val=0, max_val=E1 - 1)
                act.wait_ge(S("eh_out"), 32 * it + 1)
                act.wait_ge(S("eb_in"), 32)
                act.activation(eb1_now[:, :], eb1[:, bass.ds(16 * e, 16)], ACT.Copy).then_inc(S("eb1_now"), 1)
                act.wait_ge(S("eb1_now"), it + 1)
                def split_chunk(c):
                    act.wait_ge(S(f"ew_in{c % 4}"), 64 * it + 32 * (c // 4) + 32)
                    act.wait_ge(S("y_mm"), 16 * it + max(2 * c - 2, 0) + 1 if c else 16 * it + 1)
                    act.activation(ew_hi[:, c % 2, :], weights[:, 2048 * (c % 4):2048 * (c % 4) + 2048], ACT.Copy).then_inc(S("ew_high"), 1)

                for f in range(16):
                    if f % 2 == 0:
                        split_chunk(f // 2)
                    for hf in range(2):
                        a, w = ((0, 312), (312, 314))[hf]
                        n = 2 * f + hf
                        act.wait_ge(S("hid_split"), 16 * it + max(f - 3, 0) + 1)
                        act.wait_ge(S("eh_mm"), 32 * it + n + 1)
                        act.activation(hid[:, f % 4, a:a + w], bank[5 + n % 3][:, 0:w], ACT.Silu,
                                       bias=eb1_now[:, f:f + 1]).then_inc(S("eh_out"), 1)

        @block.vector
        def _(dve):
            step = [0]

            def link(ins):
                step[0] += 1
                ins.then_inc(S("dve_step"), 1)
                dve.wait_ge(S("dve_step"), step[0])

            norms = [0]

            def layernorm(src, dst, name, wait=None):
                for j in range(TT):
                    if wait:
                        dve.wait_ge(S(wait), j + 1)
                    ins = dve.bn_stats(st[0:P, j, :], src[:, j, :])
                link(ins)
                for j in range(TT):
                    ins = dve.bn_aggr(mv[0:P, j, :], st[0:P, j, :])
                ins.then_inc(S("ln_var"), 1)
                norms[0] += 1
                dve.wait_ge(S("ln_std"), norms[0])
                link(dve.reciprocal(rs[0:P, :], sd[0:P, :]))
                for j in range(TT):
                    dve.tensor_scalar(dst[:, j, :], src[:, j, :], mv[0:P, j, 0:1], rs[0:P, j:j + 1],
                                      ALU.subtract, ALU.mult).then_inc(S(name), 1)

            bns = [0]

            def batchnorm(src, dst, gain, name):
                for k in range(KT):
                    for hf, (a, w) in enumerate(HALF):
                        ins = dve.bn_stats(tmp[:, 0, 12 * k + 6 * hf:12 * k + 6 * hf + 6], src[:, k, a:a + w])
                link(ins)
                for k in range(KT):
                    ins = dve.bn_aggr(mv[:, k, :], tmp[:, 0, 12 * k:12 * k + 12])
                ins.then_inc(S("bn_var"), 1)
                bns[0] += 1
                dve.wait_ge(S("bn_std"), bns[0])
                link(dve.reciprocal(rs[:, 0:KT], sd[:, 0:KT]))
                link(dve.tensor_tensor(rs[:, 0:KT], rs[:, 0:KT], cols[:, COL_AT[gain]:COL_AT[gain] + KT], ALU.mult))
                for k in range(KT):
                    dve.tensor_scalar(dst[:, k, 0:N], src[:, k, 0:N], mv[:, k, 0:1], rs[:, k:k + 1],
                                      ALU.subtract, ALU.mult).then_inc(S(name), 1)

            def bc(v, e):
                return v.unsqueeze(2).to_broadcast([P, TT, e])

            def iota_bc(e):
                return iota_e[0:P, 0:e].unsqueeze(1).to_broadcast([P, TT, e])

            def top_two(val, e, tables, best, low):
                eq, hot = tables[0], tables[1:3]
                idx = small[0:P, 20:25]
                for i in range(2):
                    link(dve.tensor_reduce(best[i], val, AX.X, ALU.max))
                    link(dve.tensor_tensor(eq, val, bc(best[i], e), ALU.is_equal))
                    link(dve.scalar_tensor_tensor(eq, eq, -float(e), iota_bc(e), ALU.mult, ALU.add))
                    link(dve.tensor_reduce(idx, eq, AX.X, ALU.min))
                    link(dve.tensor_tensor(hot[i], eq, bc(idx, e), ALU.is_equal))
                    if i == 0:
                        link(dve.scalar_tensor_tensor(tables[3], hot[0], -low, val, ALU.mult, ALU.add))
                        val = tables[3]

            dve.wait_ge(S("x_in"), 16)
            dve.wait_ge(S("consts"), 1)
            layernorm(x, xn, "xn_row")
            layernorm(xn, row(3), "h_row", wait="xn_row")

            dve.wait_ge(S("edges_in"), 16)
            link(dve.tensor_copy(srcf, edges[:, 0, :]))
            link(dve.tensor_copy(dstf, edges[:, 1, :]))
            link(dve.tensor_copy(relf, edges[:, 2, :]))
            link(dve.tensor_scalar(relf, relf, 0.0, 1024.0, ALU.not_equal, ALU.mult))
            link(dve.tensor_tensor(relf, relf, dstf, ALU.add))
            for j in range(TT):
                dve.tensor_scalar(keyf[:, j, :], relf, -float(P * j), None, ALU.add)
                link(dve.tensor_scalar(gez[:, j, :], dstf, float(P * j), None, ALU.is_ge))
            for j in range(TT - 1):
                dve.tensor_tensor(pres[:, j, :], gez[:, j, :], gez[:, j + 1, :], ALU.subtract)
            dve.tensor_copy(pres[:, TT - 1, :], gez[:, TT - 1, :]).then_inc(S("presence"), 1)
            rr = rg[:, 0:200].rearrange("p (j q) -> p j q", j=TT)
            rt2 = rg[:, 200:210]
            iq = iota_e[0:1, 0:EP].unsqueeze(1).to_broadcast([1, TT, EP])
            dve.wait_ge(S("psum_full"), filled("rng", 1))
            cnt = B("rng")[0:1, 0:TT * ET].rearrange("p (j q u) -> p j q u", j=TT, u=2)
            dve.tensor_reduce(rr, cnt, AX.X, ALU.add).then_inc(S("rng_out"), 1)
            dve.wait_ge(S("rng_out"), 1)
            link(dve.tensor_scalar(rr, rr, 0.5, None, ALU.is_ge))
            hit = small[0:1, 850:850 + 100]
            last, first = rt2[:, 0:5], rt2[:, 5:10]
            t5 = rg[:, 210:310].rearrange("p (j q) -> p j q", j=TT)
            t40 = tmp[0:1, 1, 0:TT * EP].rearrange("p (j q) -> p j q", j=TT)
            link(dve.scalar_tensor_tensor(t40, iq, 1.0, rr, ALU.add, ALU.mult))
            link(dve.tensor_reduce(last, t40, AX.X, ALU.max))
            link(dve.scalar_tensor_tensor(t40, iq, -float(EP), rr, ALU.add, ALU.mult))
            link(dve.tensor_reduce(first, t40, AX.X, ALU.min))
            link(dve.tensor_scalar(first, first, float(EP), float(EP - 1), ALU.add, ALU.min))
            link(dve.tensor_tensor(last, last, first, ALU.subtract))
            link(dve.tensor_scalar(last, last, 1.0, None, ALU.max))
            dve.tensor_copy(rng_i[0:1, 0:10], rt2).then_inc(S("ranges"), 1)
            dve.wait_ge(S("ranges"), 1)
            for j in range(TT):
                pairs = dve.value_load(rng_i[0:1, j:j + 1], min_val=1, max_val=EP)
                q0 = dve.value_load(rng_i[0:1, 5 + j:6 + j], min_val=0, max_val=EP - 1)
                if j:
                    dve.wait_ge(S("psum_full"), filled("A", 4 * j))
                with dve.Fori(0, pairs) as i:
                    for u in range(2):
                        dve.wait_ge(S(f"oh_used{j}"), 2 * i + u + 1)
                        dve.tensor_scalar(oh_src[u], iota_src, small[0:P, bass.ds(2 * q0 + 2 * i + u, 1)], None, ALU.is_equal)
                        dve.tensor_scalar(oh_dst[u], iota_dst, small[0:P, bass.ds(2 * q0 + 2 * i + (ET * (j + 1) + u), 1)], None,
                                          ALU.is_equal).then_inc(S(f"oh_ready{j}"), 1)

            def sum_bases(l, p0, p1):
                done = S(f"w{l}_sum")
                if p0 == 0:
                    if l == 0:
                        dve.wait_ge(S("att_in"), 16)
                    for u in range(2):
                        dve.wait_ge(S(f"basis_in{u}"), 16 * (15 * l + 1))
                        for r in range(2):
                            if u == 0:
                                dve.tensor_scalar(wrel[l][r], basis[u], att[:, l, r, 0:1], None, ALU.mult).then_inc(done, 1)
                            else:
                                dve.wait_ge(done, r + 1)
                                dve.scalar_tensor_tensor(wrel[l][r], basis[u], att[:, l, r, 1:2], wrel[l][r],
                                                         ALU.mult, ALU.add).then_inc(done, 1)
                    p0 = 1
                with dve.Fori(p0, p1) as p:
                    for u in range(2):
                        dve.wait_ge(S(f"basis_in{u}"), 16 * p + 16 * (15 * l + 1))
                        for r in range(2):
                            dve.wait_ge(done, 4 * p + (2 * u + r - 1))
                            dve.scalar_tensor_tensor(wrel[l][r], basis[u], att[:, l, r, bass.ds(2 * p + u, 1)], wrel[l][r],
                                                     ALU.mult, ALU.add).then_inc(done, 1)

            dve.wait_ge(S("psum_full"), filled("A", 20))
            sum_bases(0, 0, 10)
            dve.wait_ge(S("psum_full"), filled("D", 1))
            dve.tensor_scalar(rD, B("D")[0:P, 0:TT], 256e-8, None, ALU.add).then_inc(S("D_out"), 1)
            dve.wait_ge(S("D_out"), 1)
            dve.reciprocal(rD, rD).then_inc(S("rD"), 1)
            sum_bases(0, 10, 13)
            layernorm(row(4), row(3), "yn_row", wait="y_row")
            sum_bases(0, 13, 15)
            sum_bases(1, 0, 15)

            for j in range(TT):
                dve.wait_ge(S("psum_full"), filled("o2", j + 1))
                dve.wait_ge(S("x_mix"), j + 1)
                dve.tensor_tensor(x[:, j, :], B("o2", j)[0:P, :], x[:, j, :], ALU.add).then_inc(S("o2_out"), 1)
            layernorm(x, row(1), "xf_row", wait="o2_out")

            dve.wait_ge(S("psum_full"), filled("rt", 1))
            T = [table(6, i, E0) for i in range(8)]
            b1, b2, s1 = small[0:P, 25:30], small[0:P, 30:35], small[0:P, 35:40]
            logit = B("rt")[0:P, 0:TT * E0].rearrange("p (j e) -> p j e", j=TT)
            dve.tensor_copy(T[0], logit).then_inc(S("rt_out"), 1)
            dve.wait_ge(S("rt_out"), 1)
            link(dve.tensor_reduce(b1, T[0], AX.X, ALU.max))
            dve.tensor_tensor(T[1], T[0], bc(b1, E0), ALU.subtract).then_inc(S("rt_sub"), 1)
            dve.wait_ge(S("rt_exp"), 1)
            link(dve.tensor_reduce(s1, T[1], AX.X, ALU.add))
            link(dve.reciprocal(s1, s1))
            link(dve.tensor_tensor(T[1], T[1], bc(s1, E0), ALU.mult))
            top_two(T[1], E0, [T[2], T[3], T[4], T[5]], [b1, b2], 4.0)
            dve.tensor_tensor(T[6], T[3], T[4], ALU.add).then_inc(S("chosen"), 1)
            dve.wait_ge(S("chosen"), 1)
            link(dve.tensor_tensor(T[1], T[1], T[6], ALU.mult))
            dve.wait_ge(S("psum_full"), filled("pos", 1))
            pos = B("pos")[0:P, 0:TT * E0].rearrange("p (j e) -> p j e", j=TT)
            dve.tensor_scalar(T[2], pos, float(CAP) - 0.5, None, ALU.is_lt).then_inc(S("pos_out"), 1)
            dve.wait_ge(S("pos_out"), 1)
            link(dve.tensor_tensor(T[2], T[2], T[1], ALU.mult))
            gate = small[0:P, 977:982]
            link(dve.tensor_reduce(gate, T[2], AX.X, ALU.add))
            for j in range(TT):
                dve.wait_ge(S("psum_full"), filled("fy", j + 1))
                dve.tensor_tensor(row(4)[:, j, :], B("fy", j)[0:P, :], rowvec("ffn_b2"), ALU.add).then_inc(S("fy_out"), 1)
                dve.wait_ge(S("fy_out"), j + 1)
                dve.scalar_tensor_tensor(x[:, j, :], row(4)[:, j, :], gate[:, j:j + 1], x[:, j, :],
                                         ALU.mult, ALU.add).then_inc(S("x2"), 1)
            dve.wait_ge(S("A_sum"), 1)
            deg = small[0:P, 982:987]
            link(dve.tensor_reduce(deg, AT[:, 0, :, :], AX.X, ALU.add))
            link(dve.tensor_scalar(deg, deg, 1.0, None, ALU.max))
            link(dve.reciprocal(deg, deg))
            for j in range(TT):
                dve.tensor_scalar(AT[:, 0, j, :], AT[:, 0, j, :], deg[:, j:j + 1], None, ALU.mult).then_inc(S("A_mean"), 1)
            layernorm(x, row(1), "xn2_row", wait="x2")
            dve.memset(v_aug[:, :, DH:DH + 1], 1.0).then_inc(S("v_ones"), 1)
            dve.wait_ge(S("act_read"), READ0["xn2T"] + 5)
            batchnorm(col(2), col(3), "g1", "bn1")

            for n in range(4):
                dve.wait_ge(S("psum_full"), filled("uk", n + 1))
                h = HEAD_ORDER[2 * n]
                ins = dve.tensor_reduce(amax_k[:, h:h + 3:2], B("uk", n)[:, :].rearrange("p (h m) -> p h m", h=2), AX.X, ALU.max)
            ins.then_inc(S("kmax"), 1)
            dve.wait_ge(S("kmax_all"), 1)
            dve.wait_ge(S("act_read"), READ0["ad"] + 1)
            dve.scalar_tensor_tensor(abias_k, adiag[:, 8:16], -1.0, amax_kr, ALU.mult, ALU.subtract).then_inc(S("kbias"), 1)
            for n in range(4):
                dve.wait_ge(S("psum_full"), filled("uq", n + 1))
                h = HEAD_ORDER[2 * n]
                ins = dve.tensor_reduce(amax_q[:, h:h + 3:2], B("uq", n)[:, :].rearrange("p (h m) -> p h m", h=2), AX.X, ALU.max)
            link(ins)
            dve.scalar_tensor_tensor(abias_q, adiag[:, 0:8], -1.0, amax_q, ALU.mult, ALU.subtract).then_inc(S("qbias"), 1)
            dve.wait_ge(S("act_read"), READ0["uk"] + 8)
            dve.tensor_scalar(ke, ke, 1.0 / 16, 1e-6, ALU.mult, ALU.add).then_inc(S("kf"), 1)
            dve.wait_ge(S("act_read"), READ0["uq"] + 8)
            dve.tensor_scalar(qe, qe, 1.0 / 16, 1e-6, ALU.mult, ALU.add).then_inc(S("qf"), 1)
            for n in range(2):
                dve.wait_ge(S("psum_full"), filled("at", n + 1))
                heads = B("at", n)[:, 0:4 * 65].rearrange("p (h d) -> p h d", h=4)
                den = aden[:, 4 * n:4 * n + 4]
                link(dve.tensor_scalar(den, heads[:, :, DH:DH + 1].rearrange("p h o -> p (h o)"), 1e-6, None, ALU.add))
                link(dve.reciprocal(den, den))
                dve.tensor_tensor(attn[:, 256 * n:256 * n + 256].rearrange("p (h d) -> p h d", h=4), heads[:, :, 0:DH],
                                  den.unsqueeze(2).to_broadcast([128, 4, DH]), ALU.mult).then_inc(S("at_out"), 1)
            dve.wait_ge(S("act_read"), READ0["conv"] + 8)
            link(dve.tensor_tensor(col(6)[:, :, 0:N], col(6)[:, :, 0:N], col(2)[:, :, 0:N], ALU.add))
            dve.wait_ge(S("act_read"), READ0["ha"] + 1)
            dve.tensor_tensor(col(6)[:, :, 0:NA], col(6)[:, :, 0:NA], haT, ALU.add)
            for k in range(KT):
                ins = dve.tensor_scalar(col(6)[:, k, NA:N], col(6)[:, k, NA:N], haT[:, k, NA - 1:NA], None, ALU.add)
            link(ins)
            dve.memset(kvb, 0.0).then_inc(S("kvb_zero"), 1)

            def phi_tile(n):
                if n < 8:
                    a, w = HALF[n % 2]
                    return B("xq", n)[:, 0:w], tmp[:, n % 2, 0:w], col(3)[:, n // 2, a:a + w]
                return B("xk", n - 8)[0:P, :], tmp[0:P, n % 2, :], row(4)[:, n - 8, :]

            def phi_min(n):
                name, at = ("xq", n) if n < 8 else ("xk", n - 8)
                dve.wait_ge(S("psum_full"), filled(name, at + 1))
                if n >= 2:
                    dve.wait_ge(S("xq_out" if n - 2 < 8 else "xk_out"), n - 1 if n - 2 < 8 else n - 9)
                src, t, _ = phi_tile(n)
                dve.tensor_scalar(t, src, 0.0, None, ALU.min).then_inc(S("xmin"), 1)

            phi_min(0)
            for n in range(8 + TT):
                if n + 1 < 8 + TT:
                    phi_min(n + 1)
                dve.wait_ge(S("xexp"), n + 1)
                src, t, dst = phi_tile(n)
                dve.scalar_tensor_tensor(dst, src, 0.0, t, ALU.max, ALU.add).then_inc(S("xq_out" if n < 8 else "xk_out"), 1)
            dve.wait_ge(S("psum_full"), filled("xkv", 1))
            dve.wait_ge(S("kvb_zero"), 1)
            kvp = B("xkv")[:, :].rearrange("p (k e) -> p k e", k=KT)
            SCALE = float(DH) ** -0.5
            dve.tensor_scalar(kvb[0:64, :, 0:64], kvp[0:64, :, 0:64], SCALE, None, ALU.mult)
            dve.tensor_scalar(kvb[64:128, :, 64:128], kvp[64:128, :, 64:128], SCALE, None, ALU.mult).then_inc(S("xkv_out"), 1)
            bsum = small[:, 990:994]
            link(dve.tensor_tensor(bsum, cols[:, COL_AT["b_proj"]:COL_AT["b_proj"] + KT], cols[:, COL_AT["b2n"]:COL_AT["b2n"] + KT], ALU.add))
            batchnorm(col(6), col(6), "g2", "bn2")
            dve.wait_ge(S("bn2"), 4)
            for n in range(8):
                m, (a, w) = n // 2, HALF[n % 2]
                dve.wait_ge(S("psum_full"), filled("xp", n + 1))
                dve.scalar_tensor_tensor(col(6)[:, m, a:a + w], B("xp", n)[:, 0:w], bsum[:, m:m + 1], col(6)[:, m, a:a + w],
                                         ALU.add, ALU.add).then_inc(S("xp_out"), 1)
            for j in range(TT):
                dve.wait_ge(S("psum_full"), filled("x3r", j + 1))
                dve.tensor_tensor(x[:, j, :], B("x3r", j)[0:P, :], x[:, j, :], ALU.add).then_inc(S("x3r_out"), 1)
            layernorm(x, row(1), "xe_row", wait="x3r_out")

            U = [table(6, i, E1) for i in range(6)]
            dve.wait_ge(S("psum_full"), filled("el", 1))
            dve.wait_ge(S("Wg_in"), 32)
            dve.tensor_tensor(U[0], B("el")[0:P, 0:TT * E1].rearrange("p (j e) -> p j e", j=TT),
                              small[0:P, 0:E1].unsqueeze(1).to_broadcast([P, TT, E1]), ALU.add).then_inc(S("el_out"), 1)
            dve.wait_ge(S("el_out"), 1)
            top_two(U[0], E1, [U[1], U[2], U[3], U[4]], [b1, b2], 1e30)
            link(dve.tensor_tensor(U[4], U[2], U[3], ALU.add))
            sel = U[5].rearrange("p j e -> p (j e)")[:, 0:E1]
            dve.tensor_reduce(sel, U[4].rearrange("p j e -> p e j"), AX.X, ALU.add).then_inc(S("selected"), 1)
            dve.tensor_tensor(eexp, b2, b1, ALU.subtract).then_inc(S("el_sub"), 1)
            dve.wait_ge(S("el_exp"), 1)
            link(dve.tensor_scalar(s1, eexp, 1.0, None, ALU.add))
            link(dve.reciprocal(s1, s1))
            link(dve.tensor_tensor(b2, s1, eexp, ALU.mult))
            link(dve.tensor_tensor(U[2], U[2], bc(s1, E1), ALU.mult))
            link(dve.tensor_tensor(U[3], U[3], bc(b2, E1), ALU.mult))
            dve.tensor_tensor(comb, U[2], U[3], ALU.add).then_inc(S("comb"), 1)
            for i, name in enumerate(("y_mm", "eh_out", "x4", "hid_split")):
                dve.memset(small[0:1, 1015 + i:1016 + i], 0.0).then_inc(S(name), 1)
            dve.wait_ge(S("psum_full"), filled("en", 1))
            act1, key1, srt = small[0:1, 800:808], small[0:1, 808:816], small[0:1, 816:824]
            dve.tensor_scalar(act1, B("en")[0:1, 0:E1], 0.5, None, ALU.is_ge).then_inc(S("en_out"), 1)
            dve.wait_ge(S("en_out"), 1)
            link(dve.scalar_tensor_tensor(key1, iota_e[0:1, 0:E1], -float(E1), act1, ALU.add, ALU.mult))
            link(dve.tensor_scalar(key1, key1, -1.0, None, ALU.mult))
            link(dve.max(srt, key1))
            link(dve.tensor_scalar(srt, srt, -1.0, float(E1), ALU.mult, ALU.add))
            link(dve.tensor_scalar(srt, srt, float(E1 - 1), None, ALU.min))
            link(dve.tensor_copy(el_i[0:1, 0:8], srt))
            link(dve.tensor_reduce(key1[:, 0:1], act1, AX.X, ALU.add))
            dve.tensor_copy(el_i[0:1, 8:9], key1[:, 0:1]).then_inc(S("elist"), 1)
            dve.wait_ge(S("elist"), 1)
            for j in range(TT):
                dve.wait_ge(S("psum_full"), filled("eb2", j + 1))
                dve.tensor_tensor(x[:, j, :], B("eb2", j)[0:P, :], x[:, j, :], ALU.add).then_inc(S("eb2_out"), 1)
            dve.wait_ge(S("eb2_out"), 5)
            dve.wait_ge(S("xe_high"), 1)
            dve.tensor_tensor(xe_lo[:, :, 0:N], col(2)[:, :, 0:N], xe_hi[:, :, 0:N].bitcast(f32), ALU.subtract).then_inc(S("xe_low"), 1)
            n_act = dve.value_load(el_i[0:1, 8:9], min_val=2, max_val=E1)
            with dve.Fori(0, n_act) as it:
                e = dve.value_load(el_i[0:1, bass.ds(it, 1)], min_val=0, max_val=E1 - 1)
                for f in range(16):
                    if f % 2 == 0:
                        c = f // 2
                        dve.wait_ge(S("ew_high"), 8 * it + c + 1)
                        dve.tensor_tensor(ew_lo[:, c % 2, :], weights[:, 2048 * (c % 4):2048 * (c % 4) + 2048],
                                          ew_hi[:, c % 2, :].bitcast(f32), ALU.subtract).then_inc(S("ew_split"), 1)
                    dve.wait_ge(S("y_mm"), 16 * it + max(f - 3, 0) + 1)
                    dve.wait_ge(S("eh_out"), 32 * it + 2 * f + 3)
                    dve.tensor_copy(hid_hi[:, f % 4, :], hid[:, f % 4, :]).then_inc(S("hid_high"), 1)
                    dve.wait_ge(S("hid_high"), 16 * it + f + 1)
                    dve.tensor_tensor(hid_lo[:, f % 4, :], hid[:, f % 4, :], hid_hi[:, f % 4, :].bitcast(f32),
                                      ALU.subtract).then_inc(S("hid_split"), 1)
                dve.wait_ge(S("y_mm"), 16 * it + 17)
                dve.wait_ge(S("x4"), TT * it + 1)
                for j in range(TT):
                    dve.scalar_tensor_tensor(x[:, j, :], bank[j][0:P, :], comb[:, j, bass.ds(e, 1)], x[:, j, :],
                                             ALU.mult, ALU.add).then_inc(S("x4"), 1)
            dve.wait_ge(S("x4"), TT * n_act + 1)
            dve.memset(small[0:1, 1019:1020], 0.0).then_inc(S("result"), 1)

        @block.tensor
        def _(pe):
            def group(out, pairs):
                for i, (a, b) in enumerate(pairs):
                    ins = pe.matmul(out, a, b, start=i == 0, stop=i == len(pairs) - 1)
                return ins

            def to_cols(stage, src, ready, n=TT, free=P):
                for j in range(n):
                    bk = claim(pe, stage, j)
                    pe.wait_ge(S(ready), j + 1)
                    for k in range(KT):
                        ins = pe.transpose(bk[:, P * k:P * k + P], src[:, j, 128 * k:128 * k + 128], ident[0:P, 0:P])
                    ins.then_inc(S("psum_full"), 1)

            def to_rows(stage, src):
                for j in range(TT):
                    bk = claim(pe, stage, j)
                    for k in range(KT):
                        ins = pe.transpose(bk[0:P, 128 * k:128 * k + 128], src[:, k, P * j:P * j + P], ident[:, :])
                    ins.then_inc(S("psum_full"), 1)

            def cols_out(stage, w, at, act_in, tiles=KT, n0=0, k_in=KT):
                for m in range(tiles):
                    for hf, (a, wd) in enumerate(HALF):
                        n = n0 + 2 * m + hf
                        bk = claim(pe, stage, n)
                        group(bk[:, 0:wd], [(w[:, k, at + 128 * m:at + 128 * m + 128], act_in[:, k, a:a + wd])
                                            for k in range(k_in)]).then_inc(S("psum_full"), 1)

            def rows_out(stage, act_in, w, at=0, k_in=KT, width=H):
                for j in range(TT):
                    bk = claim(pe, stage, j)
                    group(bk[0:P, 0:width], [(act_in[:, k, P * j:P * j + P], w[:, k, at:at + width])
                                             for k in range(k_in)]).then_inc(S("psum_full"), 1)

            def small_rows(stage, act_in, w, width):
                bk = claim(pe, stage)
                for j in range(TT):
                    ins = group(bk[0:P, width * j:width * j + width], [(act_in[:, k, P * j:P * j + P], w[:, k, :]) for k in range(KT)])
                ins.then_inc(S("psum_full"), 1)

            pe.wait_ge(S("consts"), 1)
            to_cols("xnT", xn, "xn_row")
            to_cols("hT", row(3), "h_row")
            bk = claim(pe, "rng")
            pe.wait_ge(S("presence"), 1)
            group(bk[0:1, 0:TT * ET], [(ones[0:P, 0:1], pres.rearrange("p j t -> p (j t)"))]).then_inc(S("psum_full"), 1)
            pe.wait_ge(S("ranges"), 1)
            for j in range(TT):
                pairs = pe.value_load(rng_i[0:1, j:j + 1], min_val=1, max_val=EP)
                parts = [(B("A", 4 * j + q), q // 2, HALF[q % 2]) for q in range(4)]
                for q, (bkq, r, (a, w)) in enumerate(parts):
                    claim(pe, "A", 4 * j + q)
                    pe.matmul(bkq[0:P, 0:w], zero[:, 0:P], zero[:, 0:w], start=True, stop=False)
                    if q % 2:
                        pe.matmul(bkq[0:P, 0:1], zero[:, 0:P], zero[:, 0:1], start=False, stop=False).then_inc(S(f"oh_used{j}"), 1)
                with pe.Fori(0, pairs) as i:
                    for u in range(2):
                        pe.wait_ge(S(f"oh_ready{j}"), 2 * i + u + 1)
                        for bkq, r, (a, w) in parts:
                            ins = pe.matmul(bkq[0:P, 0:w], oh_dst[u][:, P * r:P * r + P], oh_src[u][:, a:a + w], start=False, stop=False)
                        ins.then_inc(S(f"oh_used{j}"), 1)
                for bkq, r, (a, w) in parts:
                    pe.matmul(bkq[0:P, 0:w], zero[:, 0:P], zero[:, 0:w], start=False, stop=True).then_inc(S("psum_full"), 1)

            pe.wait_ge(S("act_read"), READ0["hT"] + 5)
            pe.wait_ge(S("kqv_in"), 16)
            cols_out("kq", kqv_w, 0, col(4), tiles=8)
            rows_out("v", col(4), kqv_w, at=2 * H)
            pe.wait_ge(S("prm_in"), 16)

            def features(w, xd, srcT, squares, ready):
                for j in range(TT):
                    if j % 2 == 0:
                        bk = claim(pe, w, j // 2)
                    ins = group(bk[0:P, M * (j % 2):M * (j % 2) + M], [(srcT[:, k, P * j:P * j + P], prm_w[:, k, :]) for k in range(KT)])
                    if j % 2 == 1 or j == TT - 1:
                        ins.then_inc(S("psum_full"), 1)
                bk = claim(pe, xd)
                pe.wait_ge(S(ready), 1)
                for j in range(TT):
                    ins = group(bk[0:P, j:j + 1], [(squares[:, k, P * j:P * j + P], eps[:, 2:3]) for k in range(KT)])
                ins.then_inc(S("psum_full"), 1)

            pe.wait_ge(S("act_read"), READ0["kq"] + 8)
            features("wk", "xdk", col(5), col(4), "sqk")
            pe.wait_ge(S("act_read"), READ0["kq"] + 16)
            features("wq", "xdq", col(6), col(5), "sqq")
            for j in range(TT):
                bk = claim(pe, "qpT", j)
                pe.wait_ge(S("act_read"), READ0["wq"] + j + 1)
                for c in range(2):
                    ins = pe.transpose(bk[:, P * c:P * c + P], qp[:, j, 128 * c:128 * c + 128], ident[0:P, 0:P])
                ins.then_inc(S("psum_full"), 1)
            pe.wait_ge(S("act_read"), READ0["wk"] + 5)
            pe.wait_ge(S("vrow"), 5)
            for c in range(2):
                bk = claim(pe, "kptv", c)
                group(bk[:, :], [(kp[:, j, 128 * c:128 * c + 128], row(3)[:, j, :]) for j in range(TT)]).then_inc(S("psum_full"), 1)
            bk = claim(pe, "ks")
            for c in range(2):
                ins = group(bk[:, c:c + 1], [(kp[:, j, 128 * c:128 * c + 128], ones[0:P, 0:1]) for j in range(TT)])
            ins.then_inc(S("psum_full"), 1)
            bk = claim(pe, "D")
            pe.wait_ge(S("act_read"), READ0["ks"] + 1)
            pe.wait_ge(S("act_read"), READ0["qpT"] + 5)
            for j in range(TT):
                ins = group(bk[0:P, j:j + 1], [(qpT[:, c, P * j:P * j + P], ksum[:, c:c + 1]) for c in range(2)])
            ins.then_inc(S("psum_full"), 1)
            pe.wait_ge(S("act_read"), READ0["kptv"] + 2)
            cols_out("yT", kptvT, 0, qpT, k_in=2)
            pe.wait_ge(S("act_read"), READ0["yT"] + 8)
            pe.wait_ge(S("projw_in"), 16)
            rows_out("proj", col(5), proj_w)
            to_cols("h2T", row(3), "yn_row")
            pe.wait_ge(S("act_read"), READ0["h2T"] + 5)
            pe.wait_ge(S("mlp1_in"), 16)
            cols_out("m1", mlp_w1, 0, col(5))
            pe.wait_ge(S("act_read"), READ0["m1"] + 8)
            pe.wait_ge(S("mlp2_in"), 16)
            rows_out("m2", col(6), mlp_w2)

            def neighbours(stage):
                for n in range(16):
                    r, m, (a, w) = n // 8, n // 2 % 4, HALF[n % 2]
                    bk = claim(pe, stage, n)
                    group(bk[:, 0:w], [(row(3 + r)[:, j, 128 * m:128 * m + 128], AT[:, r, j, a:a + w]) for j in range(TT)])\
                        .then_inc(S("psum_full"), 1)

            pe.wait_ge(S("gate_in"), 16)
            small_rows("gate1", xnT, gate_w[:, 0, :, :], 2)
            pe.wait_ge(S("act_read"), READ0["A"] + 20)
            pe.wait_ge(S("xg1"), 10)
            neighbours("Z1")
            pe.wait_ge(S("act_read"), READ0["Z1"] + 16)
            pe.wait_ge(S("root1_in"), 16)
            pe.wait_ge(S("w0_sum"), 60)
            for m in range(KT):
                for hf, (a, w) in enumerate(HALF):
                    bk = claim(pe, "h1T", 2 * m + hf)
                    group(bk[:, 0:w], [(wt[:, k, 128 * m:128 * m + 128], act_in[:, k, a:a + w])
                                       for wt, act_in in ((root[0], xnT), (wrel[0][0], col(5)), (wrel[0][1], col(6)))
                                       for k in range(KT)]).then_inc(S("psum_full"), 1)
            pe.wait_ge(S("act_read"), READ0["h1T"] + 8)
            small_rows("gate2", col(1), gate_w[:, 1, :, :], 2)
            to_rows("h1r", col(1))
            pe.wait_ge(S("act_read"), READ0["h1r"] + 5)
            neighbours("Z2")
            pe.wait_ge(S("act_read"), READ0["Z2"] + 16)
            pe.wait_ge(S("root2_in"), 16)
            pe.wait_ge(S("w1_sum"), 60)
            for j in range(TT):
                bk = claim(pe, "o2", j)
                group(bk[0:P, :], [(act_in[:, k, P * j:P * j + P], wt[:, k, :])
                                   for wt, act_in in ((root[1], col(1)), (wrel[1][0], col(5)), (wrel[1][1], col(6)))
                                   for k in range(KT)]).then_inc(S("psum_full"), 1)

            to_cols("xfT", row(1), "xf_row")
            pe.wait_ge(S("act_read"), READ0["xfT"] + 5)
            pe.wait_ge(S("ffn_in"), 48)
            small_rows("rt", col(2), ffn_rt, E0)
            cols_out("hf", ffn_w1, 0, col(2), tiles=1)
            bk = claim(pe, "pos")
            pe.wait_ge(S("chosen"), 1)
            chosen = table(6, 6, E0)
            for j in range(TT):
                ins = group(bk[0:P, E0 * j:E0 * j + E0], [(ones[0:P, 0:P], chosen[:, i, :]) for i in range(j)] + [(tri[:, :], chosen[:, j, :])])
            ins.then_inc(S("psum_full"), 1)
            pe.wait_ge(S("act_read"), READ0["hf"] + 2)
            for j in range(TT):
                bk = claim(pe, "fy", j)
                group(bk[0:P, :], [(hfT[:, P * j:P * j + P], ffn_w2)]).then_inc(S("psum_full"), 1)

            pe.wait_ge(S("A_mean"), 5)
            for n in range(7):
                bk = claim(pe, "AnT", n)
                for b in range(4 * n, min(4 * n + 4, 25)):
                    i, j = b // TT, b % TT
                    ins = pe.transpose(bk[0:P, P * (b % 4):P * (b % 4) + P], AT[:, 0, j, P * i:P * i + P], ident[0:P, 0:P])
                ins.then_inc(S("psum_full"), 1)
            to_cols("xn2T", row(1), "xn2_row")
            pe.wait_ge(S("xbT"), 4)
            to_rows("xbr", col(3))
            pe.wait_ge(S("act_read"), READ0["xbr"] + 5)
            pe.wait_ge(S("act_read"), READ0["AnT"] + 7)
            for n in range(8):
                m, (a, w) = n // 2, HALF[n % 2]
                bk = claim(pe, "agg", n)
                group(bk[:, 0:w], [(row(4)[:, i, 128 * m:128 * m + 128], An[:, i, a:a + w]) for i in range(TT)]).then_inc(S("psum_full"), 1)
            pe.wait_ge(S("act_read"), READ0["agg"] + 8)
            pe.wait_ge(S("Wconv_in"), 16)
            cols_out("conv", W_conv, 0, col(5))
            pe.wait_ge(S("Wqkvo_in"), 64)
            for stage, w in (("aq", Wq), ("ak", Wk)):
                bk = claim(pe, stage)
                for m in range(KT):
                    ins = group(bk[:, NA * m:NA * m + NA], [(w[:, k, 128 * m:128 * m + 128], col(2)[:, k, 0:NA]) for k in range(KT)])
                ins.then_inc(S("psum_full"), 1)
            bk = claim(pe, "av")
            group(bk[:, :], [(col(2)[:, k, 0:NA], Wv[:, k, :]) for k in range(KT)]).then_inc(S("psum_full"), 1)
            bk = claim(pe, "ad")
            pe.wait_ge(S("a_sq"), 2)
            for i, sq in enumerate((sq_aq, sq_ak)):
                for k in range(KT):
                    ins = group(bk[:, 8 * i + 2 * k:8 * i + 2 * k + 2], [(sq[:, k, :], halfsum[:, :])])
            ins.then_inc(S("psum_full"), 1)
            pe.wait_ge(S("projT_in"), 32)
            for stage, t in (("uk", akT), ("uq", aqT)):
                for n in range(4):
                    claim(pe, stage, n)
                    for h in HEAD_ORDER[2 * n:2 * n + 2]:
                        o = 64 * (h % 2)
                        ins = group(ub(stage, h), [(t[o:o + 64, h // 2, :], projT[o:o + 64, :])])
                    ins.then_inc(S("psum_full"), 1)
            pe.wait_ge(S("kf"), 1)
            pe.wait_ge(S("act_read"), READ0["av"] + 1)
            pe.wait_ge(S("v_ones"), 1)
            for g in range(16):
                if g % 6 == 0:
                    bk = claim(pe, "kv", g // 6)
                h, c = g // 2, g % 2
                ins = group(bk[:, 65 * (g % 6):65 * (g % 6) + 65], [(ke[:, h, 128 * c:128 * c + 128], v_aug[:, h, :])])
                if g % 6 == 5 or g == 15:
                    ins.then_inc(S("psum_full"), 1)
            pe.wait_ge(S("qf"), 1)
            for n in range(4):
                bk = claim(pe, "qfT", n)
                for i in range(4):
                    h, c = 2 * n + i // 2, i % 2
                    ins = pe.transpose(bk[:, 128 * i:128 * i + 128], qe[:, h, 128 * c:128 * c + 128], ident[:, :])
                ins.then_inc(S("psum_full"), 1)
            pe.wait_ge(S("act_read"), READ0["kv"] + 3)
            pe.wait_ge(S("act_read"), READ0["qfT"] + 4)
            for n in range(2):
                bk = claim(pe, "at", n)
                for i in range(4):
                    h = 4 * n + i
                    ins = group(bk[:, 65 * i:65 * i + 65], [(qfT[:, h, c, :], kv_sb[:, 2 * h + c, :]) for c in range(2)])
                ins.then_inc(S("psum_full"), 1)
            bk = claim(pe, "atT")
            pe.wait_ge(S("at_out"), 2)
            for k in range(KT):
                ins = pe.transpose(bk[:, 128 * k:128 * k + 128], attn[:, 128 * k:128 * k + 128], ident[:, :])
            ins.then_inc(S("psum_full"), 1)
            bk = claim(pe, "ha")
            pe.wait_ge(S("act_read"), READ0["atT"] + 1)
            for m in range(KT):
                ins = group(bk[:, 128 * m:128 * m + 128], [(Wo[:, k, 128 * m:128 * m + 128], attnT[:, k, :]) for k in range(KT)])
            ins.then_inc(S("psum_full"), 1)
            pe.wait_ge(S("wqkv_in"), 16)
            cols_out("xq", w_qkv, 0, col(2))
            rows_out("xk", col(2), w_qkv, at=H)
            rows_out("xv", col(2), w_qkv, at=2 * H)
            bk = claim(pe, "xkv")
            pe.wait_ge(S("xk_out"), 5)
            pe.wait_ge(S("act_read"), READ0["xv"] + 5)
            for p in range(KT):
                ins = group(bk[:, 128 * p:128 * p + 128], [(row(4)[:, j, 128 * p:128 * p + 128], row(5)[:, j, 128 * p:128 * p + 128]) for j in range(TT)])
            ins.then_inc(S("psum_full"), 1)
            pe.wait_ge(S("xkv_out"), 1)
            pe.wait_ge(S("xq_out"), 8)
            for n in range(8):
                m, (a, w) = n // 2, HALF[n % 2]
                bk = claim(pe, "xo", n)
                group(bk[:, 0:w], [(kvb[:, m, :], col(3)[:, m, a:a + w])]).then_inc(S("psum_full"), 1)
            pe.wait_ge(S("act_read"), READ0["xo"] + 8)
            pe.wait_ge(S("wproj_in"), 16)
            cols_out("xp", w_proj2, 0, col(1))
            pe.wait_ge(S("xp_out"), 8)
            to_rows("x3r", col(6))
            to_cols("xeT", row(1), "xe_row")
            pe.wait_ge(S("act_read"), READ0["xeT"] + 5)
            pe.wait_ge(S("Wg_in"), 32)
            small_rows("el", col(2), Wg, E1)
            bk = claim(pe, "en")
            pe.wait_ge(S("selected"), 1)
            group(bk[0:1, 0:E1], [(ones[0:P, 0:1], table(6, 5, E1).rearrange("p j e -> p (j e)")[:, 0:E1])]).then_inc(S("psum_full"), 1)
            pe.wait_ge(S("comb"), 1)
            for n in range(2):
                bk = claim(pe, "combT", n)
                for j in ((0, 1, 2, 3), (4,))[n]:
                    ins = pe.transpose(bk[0:E1, P * (j % 4):P * (j % 4) + P], comb[:, j, :], ident[0:P, 0:P])
                ins.then_inc(S("psum_full"), 1)
            pe.wait_ge(S("act_read"), READ0["combT"] + 2)
            pe.wait_ge(S("eb_in"), 32)
            for j in range(TT):
                bk = claim(pe, "eb2", j)
                group(bk[0:P, :], [(combT[:, P * j:P * j + P], eb2)]).then_inc(S("psum_full"), 1)
            pe.wait_ge(S("eb2_out"), 5)
            pe.wait_ge(S("elist"), 1)
            pe.wait_ge(S("xe_low"), 1)
            n_act = pe.value_load(el_i[0:1, 8:9], min_val=2, max_val=E1)
            with pe.Fori(0, n_act) as it:
                def output(f):
                    pe.wait_ge(S("hid_split"), 16 * it + f + 2)
                    for j in range(TT):
                        hh, hl = (t[:, f % 4, P * j:P * j + P] for t in (hid_hi, hid_lo))
                        products = ((hh, w2_half(ew_hi, f)), (hh, w2_half(ew_lo, f)), (hl, w2_half(ew_hi, f)))
                        for i, (a, b) in enumerate(products):
                            ins = pe.matmul(bank[j][0:P, :], a, b, start=f == 0 and i == 0, stop=f == 15 and i == 2)
                    ins.then_inc(S("y_mm"), 1)

                for f in range(16):
                    if f % 2 == 0:
                        pe.wait_ge(S("ew_split"), 8 * it + f // 2 + 1)
                    for hf, (a, w) in enumerate(((0, 312), (312, 314))):
                        n = 2 * f + hf
                        pe.wait_ge(S("eh_out"), 32 * it + max(n - 2, 0) + 1)
                        wh, wl = w1_half(ew_hi, f), w1_half(ew_lo, f)
                        group(bank[5 + n % 3][:, 0:w], [(wt[:, k, :], xt[:, k, a:a + w]) for k in range(KT)
                                                        for wt, xt in ((wh, xe_hi), (wh, xe_lo), (wl, xe_hi))]).then_inc(S("eh_mm"), 1)
                    if f == 1:
                        pe.wait_ge(S("x4"), TT * it + 1)
                    if f:
                        output(f - 1)
                output(15)


_COLS = {"n1_g": "L0_mix_n1_g", "n1_b": "L0_mix_n1_b", "n2_g": "L0_mix_n2_g", "n2_b": "L0_mix_n2_b", "mlp_b1": "L0_mix_mlp_b1",
         "bias1": "L0_gnn_bias1", "ffn_b1": "L0_ffn_b1", "b_conv": "L1_gnn_b_conv", "g1": "L1_gnn_norm1_g", "b1n": "L1_gnn_norm1_b",
         "g2": "L1_gnn_norm2_g", "b2n": "L1_gnn_norm2_b", "b_proj": "L1_mix_b_proj"}
_PLAIN = ["x", "L0_gnn_basis1", "L0_gnn_basis2", "L0_gnn_root1", "L0_gnn_root2", "L0_mix_kqv_w",
          "L0_mix_proj_w", "L0_mix_mlp_w1", "L0_mix_mlp_w2", "L1_gnn_Wq", "L1_gnn_Wk", "L1_gnn_Wv", "L1_gnn_Wo", "L1_gnn_W_conv",
          "L1_ffn_Wg", "L1_ffn_bg", "L1_ffn_W1", "L1_ffn_W2", "L1_ffn_b2"]


def kernel(**inputs):
    import numpy as _np
    import concourse.bacc as _bacc
    from concourse import mybir as _mybir
    from concourse.bass_utils import run_bass_kernel_spmd as _run

    g = {k: _np.asarray(v) for k, v in inputs.items()}
    laid = {name: g[name] for name in _PLAIN}
    by_feature = dict({n: g[src] for n, src in _COLS.items()}, kq_b=g["L0_mix_kqv_b"][:2 * H])
    laid["cols"] = _np.concatenate([by_feature[n].reshape(-1, 128).T for n, _ in COLS], axis=1)
    laid["edges"] = _np.stack([g["src"], g["dst"], g["edge_type_2"]]).reshape(3, ET, P).transpose(2, 0, 1)
    laid["att"] = _np.stack([g["L0_gnn_att1"], g["L0_gnn_att2"]])
    laid["gate_w"] = _np.stack([g[f"L0_gnn_gate_w{l}"][:, :, 0].reshape(2, KT, 128).transpose(2, 1, 0) for l in (1, 2)], axis=1)
    laid["prm_wT"] = g["L0_mix_w"].T
    laid["router_wT"] = g["L0_ffn_router_w"].T
    laid["ffn_w1T"] = g["L0_ffn_w1"].T
    laid["ffn_w2T"] = g["L0_ffn_w2"].T
    laid["projT"] = g["L1_gnn_proj"].T
    laid["w_qkvT"] = g["L1_mix_w_qkv"].T
    laid["w_projT"] = g["L1_mix_w_proj"].T
    laid["eb1"] = g["L1_ffn_b1"].reshape(E1, F1 // 128, 128).transpose(2, 0, 1).reshape(128, E1 * F1 // 128)
    for name, src in (("v_b", g["L0_mix_kqv_b"][2 * H:]), ("proj_b", g["L0_mix_proj_b"]), ("mlp_b2", g["L0_mix_mlp_b2"]),
                      ("bias2", g["L0_gnn_bias2"]), ("ffn_b2", g["L0_ffn_b2"])):
        laid["row_" + name] = src
    nc = _bacc.Bacc("TRN2", target_bir_lowering=False, num_devices=1)
    arrays, aps = {}, {}
    for name, a in laid.items():
        arrays["in_" + name] = _np.ascontiguousarray(a)
        aps[name] = nc.dram_tensor("in_" + name, a.shape, _mybir.dt.from_np(a.dtype), kind="ExternalInput").ap()
    out = nc.dram_tensor("out_0", (N, H), _mybir.dt.float32, kind="ExternalOutput").ap()
    gps_two_layers(nc, aps, out)
    r = _run(nc, [arrays], core_ids=[0])
    return r.results[0]["out_0"]
```

```python
import concourse.bass as bass
from concourse import mybir
from contextlib import ExitStack

N = 625
H = 512
NE = 10000
P = 125
TT = N // P
KT = H // 128
ET = NE // P
EU = 4
EG = ET // EU
NB = 30
M = 256
E0 = 64
CAP = 512
F0 = 128
E1, F1 = 8, 2048
HEADS, DH = 8, 64
NA = 128
HALF = ((0, 312), (312, 313))
Y0 = 8
ROW = TT * H
COLW = 626
SLOT = 2624

COLS = [("n1_g", 4), ("n1_b", 4), ("kq_b", 8), ("n2_g", 4), ("n2_b", 4), ("mlp_b1", 4), ("bias1", 4),
        ("ffn_b1", 1), ("b_conv", 4), ("g1", 4), ("b1n", 4), ("g2", 4), ("b2n", 4), ("b_proj", 4)]
COL_AT, _at = {}, 0
for _n, _c in COLS:
    COL_AT[_n] = _at
    _at += _c
NCOLS = _at
ROWS = {"v_b": 0, "proj_b": 1, "mlp_b2": 2, "bias2": 3, "ffn_b2": 4}

PSUM_ORDER = [("xnT", 5), ("hT", 5), ("rng", 1), ("A", 20),
              ("kq", 16), ("v", 5), ("wk", 3), ("xdk", 1), ("wq", 3), ("xdq", 1),
              ("qpT", 5), ("kptv", 2), ("ks", 1), ("pv", 2), ("D", 1), ("proj", 5), ("gate1", 1), ("h2T", 5), ("m1", 8),
              ("m2", 5), ("Z1", 16), ("h1T", 8), ("gate2", 1), ("h1r", 5), ("Z2", 16), ("o2", 5),
              ("AnT", 7), ("xfT", 5), ("rt", 1), ("hf", 2), ("fy", 5), ("pos", 1),
              ("xn2T", 5), ("aq", 1), ("ak", 1), ("av", 1), ("xbr", 5), ("agg", 8),
              ("ad", 1), ("uk", 4), ("conv", 8), ("uq", 4), ("kv", 3), ("qfT", 4),
              ("at", 2), ("atT", 1), ("ha", 1),
              ("xq", 8), ("xk", 5), ("xv", 5), ("xkv", 1), ("xo", 8), ("xp", 8), ("x3r", 5),
              ("xeT", 5), ("el", 1), ("en", 1), ("combT", 2), ("eb2", 5)]
TILE0, _at = {}, 0
for _n, _c in PSUM_ORDER:
    TILE0[_n] = _at
    _at += _c
ACT_READS = [("xnT", 5), ("hT", 5), ("A", 20), ("kq", 16), ("v", 5), ("xdk", 1), ("wk", 5), ("xdq", 1), ("wq", 5),
             ("qpT", 5), ("kptv", 2), ("ks", 1), ("pv", 2), ("proj", 5), ("gate1", 1), ("h2T", 5), ("m1", 8), ("m2", 5),
             ("Z1", 16), ("h1T", 8), ("gate2", 1), ("h1r", 5), ("Z2", 16), ("AnT", 7), ("xfT", 5), ("hf", 2), ("fy", 5),
             ("xn2T", 5), ("aq", 1), ("ak", 1), ("av", 1), ("xbr", 5), ("agg", 8), ("ad", 1),
             ("uk", 8), ("conv", 8), ("uq", 8), ("kv", 3), ("qfT", 4), ("atT", 1), ("ha", 1), ("xv", 5), ("xo", 8), ("xeT", 5),
             ("combT", 2)]
READ0, _at = {}, 0
for _n, _c in ACT_READS:
    READ0[_n] = _at
    _at += _c


def gps_two_layers(nc, I, out):
    f32, f16, i32, f32r = mybir.dt.float32, mybir.dt.float16, mybir.dt.int32, mybir.dt.float32r
    ALU, ACT, AX = mybir.AluOpType, mybir.ActivationFunctionType, mybir.AxisListType
    ctx = ExitStack()
    with ctx:
        def sb(name, shape, dt=f32):
            return ctx.enter_context(nc.sbuf_tensor(name, shape, dt))

        sems = {}

        def S(name):
            if name not in sems:
                sems[name] = ctx.enter_context(nc.semaphore(name))
            return sems[name]

        slot = [None] * 8
        slot[0], slot[7] = sb("slot0", [128, SLOT]), sb("slot7", [128, SLOT])
        bank = [ctx.enter_context(nc.psum_tensor(f"bank{i}", [128, 512], f32)) for i in range(8)]
        ident = sb("ident", [128, 128])
        ones = sb("ones", [128, 128])
        tri = sb("tri", [P, P])
        tmp = sb("tmp", [128, 2, 512])
        zero = sb("zero", [1, 320], f16)
        cols = sb("cols", [128, NCOLS])
        att = sb("att", [128, 2, 2, NB])
        gate_w = sb("gate_w", [128, 2, KT, 2])
        eps = sb("eps", [128, 3])
        st = sb("st", [128, TT, 6])
        mv = sb("mv", [128, TT, 2])
        sd = sb("sd", [128, TT])
        rs = sb("rs", [128, TT])
        gates = sb("gates", [P, 2, TT, 2])
        edges = sb("edges", [P, 3, ET], i32)
        small = sb("small", [128, 1024])
        rng_i = sb("rng_i", [1, 16], i32)
        el_i = sb("el_i", [1, 16], i32)

        with ExitStack() as before:
            def sb_before(name, shape, dt=f32):
                return before.enter_context(nc.sbuf_tensor(name, shape, dt))

            for i in range(1, 7):
                slot[i] = sb_before(f"slot{i}", [128, SLOT])
            AT = sb_before("AT", [P, 2, TT, N])
            weights = sb_before("weights", [128, 20736])
        sb("_slots12", [128, 2 * SLOT])
        xe_hi, xe_lo = (sb(name, [128, KT, COLW], f32r) for name in ("xe_hi", "xe_lo"))
        sb("_slots56", [128, 4 * SLOT - 2 * KT * COLW])
        hid_hi, hid_lo = (sb(name, [128, 4, COLW], f32r) for name in ("hid_hi", "hid_lo"))
        sb("_rest_of_AT", [128, 2 * TT * N - 8 * COLW])
        sb("_raw_chunks", [128, 4096])
        ew_hi, ew_lo = (sb(name, [128, 4, 2048], f32r) for name in ("ew_hi", "ew_lo"))
        sb("_rest_of_weights", [128, 20736 - 4096 - 16384])

        def row(s):
            return slot[s][0:P, 0:ROW].rearrange("p (j n) -> p j n", j=TT)

        def col(s):
            return slot[s][:, 0:KT * COLW].rearrange("p (k t) -> p k t", k=KT)

        def wmat(at, k=KT, n=H):
            return weights[:, at:at + k * n].rearrange("p (k n) -> p k n", k=k)

        def rowvec(name):
            return slot[7][0:P, ROWS[name] * H:(ROWS[name] + 1) * H]

        def colvec(name, k):
            return cols[:, COL_AT[name] + k:COL_AT[name] + k + 1]

        x, xn, xnT = row(0), row(1), col(2)
        basis = [wmat(2048 * u) for u in range(2)]
        wrel = [[wmat(4096 + 2048 * (2 * l + r)) for r in range(2)] for l in range(2)]
        kqv_w = wmat(12288, KT, 3 * H)
        proj_w, mlp_w1, mlp_w2 = wmat(12288), wmat(14336), wmat(16384)
        root = [wmat(12288), wmat(14336)]
        prm_w = wmat(18432, KT, M)
        ffn_rt, ffn_w1, ffn_w2 = wmat(19456, KT, E0), wmat(19712, KT, F0), weights[:, 20224:20736]
        Wq, Wk, Wv, Wo = wmat(0), wmat(2048), wmat(4096), wmat(6144)
        W_conv = wmat(8192)
        projT = weights[:, 18432:18432 + M]
        Wg = wmat(20480, KT, E1)
        oh = weights[0:P, 8192:8192 + 438 * (EU + 1)].bitcast(f16)
        oh_src = [oh[:, 876 * u:876 * u + N] for u in range(EU)]
        oh_dst = [oh[:, 876 * u + 626:876 * u + 876] for u in range(EU)]
        iota_src = oh[:, 876 * EU:876 * EU + N]
        iota_dst = oh[:, 876 * EU + 626:876 * EU + 876]
        srcf = small[0:P, 0:ET]
        keyf = small[0:P, ET:ET * (1 + TT)].rearrange("p (j t) -> p j t", j=TT)
        dstf, relf = small[0:P, 480:560], small[0:P, 560:640]
        pres = tmp[0:P, 0, 0:TT * ET].rearrange("p (j t) -> p j t", j=TT)
        gez = tmp[0:P, 1, 0:TT * ET].rearrange("p (j t) -> p j t", j=TT)
        rg = small[0:1, 640:960]
        AT0 = AT[:, 0, :, :].rearrange("p j s -> p (j s)")
        AT1 = AT[:, 1, :, :].rearrange("p j s -> p (j s)")
        An = AT[:, 1, :, :]

        LIN = {"q": 0, "k": 1, "v": 2, "proj": 3}
        LIN_ORDER = ["q", "v", "k", "proj"]

        def lin(t, name):
            return t[:, LIN[name], :].rearrange("p (k n) -> p k n", k=KT)

        def wait_split(eng, it, c):
            if c == 1:
                eng.wait_ge(S("ew_split1"), it + 1)
            else:
                eng.wait_ge(S("ew_split"), 7 * it + max(c, 1))

        def raw1(c):
            return wmat(2048 * (c % 2), KT, 256)

        def raw2(c):
            return wmat(2048 * (c % 2) + 1024, 2, H)

        def w1_half(t, f):
            return t[:, f // 2 % 4, 0:1024].rearrange("p (k f) -> p k f", k=KT)[:, :, 128 * (f % 2):128 * (f % 2) + 128]

        def w2_half(t, f):
            return t[:, f // 2 % 4, 1024 + H * (f % 2):1024 + H * (f % 2) + H]

        eb1 = sb("eb1", [128, E1 * F1 // 128])
        eb1_now = sb("eb1_now", [128, F1 // 128])
        eb2 = slot[7][0:E1, 512:1024]
        combT = slot[7][0:E1, 1024:1024 + N]

        aqT = slot[1][:, 0:512].rearrange("p (k t) -> p k t", k=KT)
        akT = slot[1][:, 512:1024].rearrange("p (k t) -> p k t", k=KT)
        sq_aq = slot[1][:, 1024:1536].rearrange("p (k t) -> p k t", k=KT)
        sq_ak = slot[1][:, 1536:2048].rearrange("p (k t) -> p k t", k=KT)
        haT = slot[1][:, 2048:2560].rearrange("p (k t) -> p k t", k=KT)
        qe = slot[3][:, 0:HEADS * M].rearrange("p (h m) -> p h m", h=HEADS)
        ke = slot[4][:, 0:HEADS * M].rearrange("p (h m) -> p h m", h=HEADS)
        qfT = slot[5][:, 0:HEADS * M].rearrange("p (h c t) -> p h c t", h=HEADS, c=2)
        v_aug = slot[7][:, 0:HEADS * (DH + 1)].rearrange("p (h d) -> p h d", h=HEADS)
        attn = slot[7][:, 520:1032]
        attnT = slot[7][:, 1032:1544].rearrange("p (k t) -> p k t", k=KT)
        kv_sb = slot[7][:, 1544:1544 + 1040].rearrange("p (g d) -> p g d", g=16)
        halfsum = sb("halfsum", [128, 2])
        kvb = slot[7][:, 0:512].rearrange("p (k e) -> p k e", k=KT)
        adiag = small[:, 16:32]
        amax_k, amax_kr, amax_q, abias_k, abias_q = (small[:, 32 + 8 * i:40 + 8 * i] for i in range(5))
        aden = small[:, 72:80]
        hid = col(5)
        comb = small[0:P, 128:128 + TT * E1].rearrange("p (j e) -> p j e", j=TT)

        kp = slot[4][0:P, 0:TT * M].rearrange("p (j m) -> p j m", j=TT)
        qp = slot[4][0:P, TT * M:2 * TT * M].rearrange("p (j m) -> p j m", j=TT)
        qpT = slot[6][:, 0:2 * COLW].rearrange("p (c t) -> p c t", c=2)
        vtkp = slot[6][:, 1252:1252 + 1024].rearrange("p (k m) -> p k m", k=KT)
        pv = slot[5][:, 0:1024].rearrange("p (c n) -> p c n", c=2)
        xdk, xdq, ksum, rD = small[0:P, 960:965], small[0:P, 965:970], small[:, 970:972], small[0:P, 972:977]
        hfT = slot[3][:, 0:N]
        HEAD_ORDER = [0, 2, 1, 3, 4, 6, 5, 7]

        def ub(stage, h):
            at = HEAD_ORDER.index(h)
            return B(stage, at // 2)[:, M * (at % 2):M * (at % 2) + M]

        def table(s, i, e):
            return slot[s][0:P, TT * e * i:TT * e * (i + 1)].rearrange("p (j e) -> p j e", j=TT)

        rtp, eexp = table(6, 1, E0), small[0:P, 40:45]
        iota_e = sb("iota_e", [128, E0])

        def B(stage, n=0):
            return bank[(TILE0[stage] + n) % 8]

        freed = {}
        for name, count in PSUM_ORDER:
            for n in range(count):
                freed[TILE0[name] + n] = (name, n + 1)
        for n in range(4):
            freed[TILE0["uk"] + n] = ("uk", 2 * n + 2)
            freed[TILE0["uq"] + n] = ("uq", 2 * n + 2)
        for n in range(3):
            freed[TILE0["wk"] + n] = ("wk", min(2 * n + 2, TT))
            freed[TILE0["wq"] + n] = ("wq", min(2 * n + 2, TT))

        for n in range(8):
            freed[TILE0["xo"] + n] = ("xo_low", n + 1)

        def filled(stage, count):
            return TILE0[stage] + count

        def claim(pe, stage, n=0):
            g = TILE0[stage] + n
            if g >= 8:
                name, value = freed[g - 8]
                if name in READ0:
                    pe.wait_ge(S("act_read"), READ0[name] + value)
                else:
                    pe.wait_ge(S(name if name == "xo_low" else name + "_out"), value)
            return B(stage, n)

        block = ctx.enter_context(nc.Block())

        @block.sync
        def _(sp):
            def load(dst, src, name):
                sp.dma_start(dst, src).then_inc(S(name), 16)

            load(x, I["x"].rearrange("(j p) n -> p j n", p=P), "x_in")
            load(edges[:, :, :], I["edges"], "edges_in")
            load(att[:, :, :, :], I["att"].partition_broadcast(128), "att_in")
            for l in range(2):
                b = I[f"L0_gnn_basis{l + 1}"].rearrange("b (k p) n -> b p k n", p=128)
                done = S(f"w{l}_sum")
                for u in range(2):
                    if l == 1:
                        sp.wait_ge(S("w0_sum"), 4 * 14 + 2 * u + 2)
                    load(basis[u], b[u], f"basis_in{u}")
                with sp.Fori(1, NB // 2) as p:
                    for u in range(2):
                        sp.wait_ge(done, 4 * p + (2 * u - 2))
                        sp.dma_start(basis[u], b[bass.ds(2 * p + u, 1)].rearrange("o p k n -> (o p) k n")).then_inc(S(f"basis_in{u}"), 16)
            sp.wait_ge(S("w1_sum"), 4 * 15)
            load(Wq, I["L1_gnn_Wq"].rearrange("(k p) n -> p k n", p=128), "Wqkvo_in")
            load(Wk, I["L1_gnn_Wk"].rearrange("(k p) n -> p k n", p=128), "Wqkvo_in")
            sp.wait_ge(S("psum_full"), filled("h1T", 8))
            load(Wv, I["L1_gnn_Wv"].rearrange("(k p) n -> p k n", p=128), "Wqkvo_in")
            load(Wo, I["L1_gnn_Wo"].rearrange("(k p) n -> p k n", p=128), "Wqkvo_in")
            sp.wait_ge(S("psum_full"), filled("o2", 5))
            load(W_conv, I["L1_gnn_W_conv"].rearrange("(k p) n -> p k n", p=128), "Wconv_in")
            load(projT[0:64, :], I["projT"], "projT_in")
            load(projT[64:128, :], I["projT"], "projT_in")
            load(small[0:P, 0:E1], I["L1_ffn_bg"].partition_broadcast(P), "Wg_in")
            load(eb1[:, :], I["eb1"], "eb_in")
            sp.wait_ge(S("psum_full"), filled("fy", 5))
            load(Wg, I["L1_ffn_Wg"].rearrange("(k p) n -> p k n", p=128), "Wg_in")
            sp.wait_ge(S("psum_full"), filled("ak", 1))
            w_lin = [I["w_projT"] if name == "proj" else I["w_qkvT"][:, H * LIN[name]:H * LIN[name] + H] for name in LIN_ORDER]
            for i in range(4):
                if i >= 2:
                    sp.wait_ge(S("lin_split"), i - 1)
                load(wmat(2048 * (i % 2)), w_lin[i].rearrange("(k p) n -> p k n", p=128), f"lin_in{i % 2}")
            sp.wait_ge(S("psum_full"), filled("ha", 1))
            load(eb2, I["L1_ffn_b2"], "eb_in")
            sp.wait_ge(S("elist"), 1)
            sp.wait_ge(S("lin_split"), 4)
            n_act = sp.value_load(el_i[0:1, 8:9], min_val=2, max_val=E1)
            w1v = I["L1_ffn_W1"].rearrange("e (k p) f -> e p k f", p=128)
            w2v = I["L1_ffn_W2"].rearrange("e (f p) n -> e p f n", p=128)

            def load_chunk(e, c):
                w1c, w2c = raw1(c), raw2(c)
                sp.dma_start(w1c, w1v[bass.ds(e, 1), :, :, 256 * c:256 * c + 256].rearrange("o p k f -> (o p) k f")).then_inc(S(f"ew_in{c % 2}"), 16)
                sp.dma_start(w2c, w2v[bass.ds(e, 1), :, 2 * c:2 * c + 2, :].rearrange("o p f n -> (o p) f n")).then_inc(S(f"ew_in{c % 2}"), 16)

            e = sp.value_load(el_i[0:1, 0:1], min_val=0, max_val=E1 - 1)
            for c in range(8):
                if c >= 2:
                    wait_split(sp, 0, c - 2)
                load_chunk(e, c)
            with sp.Fori(0, n_act - 1) as it:
                e = sp.value_load(el_i[0:1, bass.ds(it + 1, 1)], min_val=0, max_val=E1 - 1)
                for c in range(8):
                    wait_split(sp, it + 1 if c >= 2 else it, (c + 6) % 8)
                    load_chunk(e, c)
            for j in range(TT):
                sp.wait_ge(S("x4"), TT * n_act + (j + 1))
                sp.dma_start(out[P * j:P * j + P, :], x[:, j, :]).then_inc(S("stored"), 16)
            sp.wait_ge(S("stored"), 16 * TT)

        @block.gpsimd
        def _(pool):
            step = [0]

            def link(ins):
                step[0] += 1
                ins.then_inc(S("pool_step"), 1)
                pool.wait_ge(S("pool_step"), step[0])

            link(pool.memset(ident[:, :], 0.0))
            link(pool.memset(ones[:, :], 1.0))
            link(pool.memset(zero[:, :], 0.0))
            link(pool.memset(halfsum[:, :], 0.5))
            link(pool.memset(eps[:, 0:1], 1e-5))
            link(pool.memset(eps[:, 1:2], 1e-3))
            link(pool.memset(eps[:, 2:3], -0.5))
            link(pool.affine_select(out=ident[:, :], in_=ident[:, :], compare_op=ALU.not_equal, fill=1.0,
                                    base=0, pattern=[[-1, 128]], channel_multiplier=1))
            link(pool.affine_select(out=tri[:, :], in_=ones[0:P, 0:P], compare_op=ALU.is_gt, fill=0.0,
                                    base=0, pattern=[[1, P]], channel_multiplier=-1))
            link(pool.affine_select(out=halfsum[:, 0:1], in_=halfsum[:, 0:1], compare_op=ALU.is_ge, fill=0.0,
                                    base=63, pattern=[[0, 1]], channel_multiplier=-1))
            link(pool.affine_select(out=halfsum[:, 1:2], in_=halfsum[:, 1:2], compare_op=ALU.is_ge, fill=0.0,
                                    base=-64, pattern=[[0, 1]], channel_multiplier=1))
            link(pool.iota(iota_src, pattern=[[1, N]], base=0, channel_multiplier=0, allow_small_or_imprecise_dtypes=True))
            link(pool.iota(iota_e[:, :], pattern=[[1, E0]], base=0, channel_multiplier=0, allow_small_or_imprecise_dtypes=True))
            pool.iota(iota_dst, pattern=[[1024, 2], [1, P]], base=0, channel_multiplier=0,
                      allow_small_or_imprecise_dtypes=True).then_inc(S("consts"), 1)

            pool.wait_ge(S("rows_in"), 16 * len(ROWS))
            for j in range(TT):
                pool.wait_ge(S("act_read"), READ0["v"] + j + 1)
                pool.tensor_tensor(row(3)[:, j, :], row(3)[:, j, :], rowvec("v_b"), ALU.add).then_inc(S("vrow"), 1)
            for s, name in ((4, "sqk"), (5, "sqq")):
                pool.wait_ge(S(name), 1)
                link(pool.tensor_tensor(col(s)[:, 0:2, 0:N], col(s)[:, 0:2, 0:N], col(s)[:, 2:4, 0:N], ALU.add))
                pool.tensor_tensor(col(s)[:, 0, 0:N], col(s)[:, 0, 0:N], col(s)[:, 1, 0:N], ALU.add).then_inc(S(name + "_sum"), 1)
            pool.wait_ge(S("vrow"), 5)
            pool.wait_ge(S("psum_full"), filled("kptv", 2))
            for j in range(TT):
                pool.tensor_tensor(row(3)[:, j, :], row(3)[:, j, :], rowvec("proj_b"), ALU.add).then_inc(S("vb"), 1)
            for j in range(TT):
                pool.wait_ge(S("act_read"), READ0["proj"] + j + 1)
                pool.wait_ge(S("vb"), j + 1)
                pool.tensor_tensor(row(4)[:, j, :], row(4)[:, j, :], row(3)[:, j, :], ALU.add).then_inc(S("y_row"), 1)
            link(pool.tensor_tensor(rowvec("mlp_b2"), rowvec("mlp_b2"), rowvec("bias2"), ALU.add))
            pool.wait_ge(S("xn_row"), 5)
            for j in range(TT):
                link(pool.tensor_tensor(x[:, j, :], x[:, j, :], rowvec("mlp_b2"), ALU.add))
            pool.wait_ge(S("y_row"), 5)
            for j in range(TT):
                pool.tensor_tensor(x[:, j, :], x[:, j, :], row(4)[:, j, :], ALU.add).then_inc(S("x_y"), 1)
            for j in range(TT):
                pool.wait_ge(S("act_read"), READ0["m2"] + j + 1)
                pool.wait_ge(S("x_y"), j + 1)
                pool.tensor_tensor(x[:, j, :], x[:, j, :], row(5)[:, j, :], ALU.add).then_inc(S("x_mix"), 1)

            pool.wait_ge(S("psum_full"), filled("Z2", 16))
            pool.tensor_tensor(AT0, AT0, AT1, ALU.add).then_inc(S("A_sum"), 1)
            for j in range(TT):
                pool.wait_ge(S("act_read"), READ0["fy"] + j + 1)
                pool.tensor_tensor(row(4)[:, j, :], row(4)[:, j, :], rowvec("ffn_b2"), ALU.add).then_inc(S("fy_row"), 1)
            pool.wait_ge(S("act_read"), READ0["ak"] + 1)
            pool.tensor_tensor(sq_ak, akT, akT, ALU.mult).then_inc(S("a_sq"), 1)
            pool.wait_ge(S("act_read"), READ0["aq"] + 1)
            pool.tensor_tensor(sq_aq, aqT, aqT, ALU.mult).then_inc(S("a_sq"), 1)

            def split_linear(i, used):
                hi, lo = (t[:, LIN[LIN_ORDER[i]], :] for t in (ew_hi, ew_lo))
                raw = weights[:, 2048 * (i % 2):2048 * (i % 2) + 2048]
                pool.wait_ge(S(f"lin_in{i % 2}"), 16 * (i // 2) + 16)
                pool.wait_ge(S("psum_full"), used)
                pool.tensor_copy(hi, raw).then_inc(S("lin_high"), 1)
                pool.wait_ge(S("lin_high"), i + 1)
                pool.tensor_tensor(lo, raw, hi.bitcast(f32), ALU.subtract).then_inc(S("lin_split"), 1)

            split_linear(0, filled("av", 1))
            pool.wait_ge(S("kmax"), 1)
            pool.partition_all_reduce(amax_kr, amax_k, 128, bass.bass_isa.ReduceOp.max).then_inc(S("kmax_all"), 1)
            split_linear(1, filled("conv", 8))
            split_linear(2, filled("ha", 1))
            split_linear(3, filled("uq", 4))
            pool.wait_ge(S("psum_full"), filled("xo", 8))
            link(pool.memset(xe_hi[:, :, N:COLW].bitcast(f32), 0.0))
            pool.memset(xe_lo[:, :, N:COLW].bitcast(f32), 0.0).then_inc(S("x_pad"), 1)
            pool.wait_ge(S("elist"), 1)
            n_act = pool.value_load(el_i[0:1, 8:9], min_val=2, max_val=E1)
            with pool.Fori(0, n_act) as it:
                for c in (0, 2, 3, 4, 5, 6, 7):
                    pool.wait_ge(S("ew_high"), 8 * it + c + 1)
                    pool.tensor_tensor(ew_lo[:, c % 4, :], weights[:, 2048 * (c % 2):2048 * (c % 2) + 2048],
                                       ew_hi[:, c % 4, :].bitcast(f32), ALU.subtract).then_inc(S("ew_split"), 1)

        @block.scalar
        def _(act):
            def load(dst, src, name):
                act.dma_start(dst, src).then_inc(S(name), 16)

            step = [0]

            def link(ins):
                step[0] += 1
                ins.then_inc(S("act_step"), 1)
                act.wait_ge(S("act_step"), step[0])

            def sqrt_for(n, e):
                act.wait_ge(S("ln_var"), n + 1)
                act.activation(sd[:, :] if e == 2 else sd[0:P, :], mv[0:P, :, 1:2].rearrange("p j o -> p (j o)"), ACT.Sqrt,
                               bias=eps[0:P, e:e + 1]).then_inc(S("ln_std"), 1)

            def copy_out(stage, n, dst, src, func=ACT.Copy, **kw):
                act.wait_ge(S("psum_full"), filled(stage, n + 1))
                act.activation(dst, src, func, **kw).then_inc(S("act_read"), 1)

            def transposed(stage, dst):
                for j in range(TT):
                    copy_out(stage, j, dst[:, :, P * j:P * j + P], B(stage, j)[:, 0:KT * P].rearrange("p (k t) -> p k t", k=KT))

            load(cols[:, :], I["cols"], "cols_in")
            load(kqv_w, I["L0_mix_kqv_w"].rearrange("(k p) n -> p k n", p=128), "kqv_in")
            load(prm_w, I["prm_wT"].rearrange("(k p) n -> p k n", p=128), "prm_in")
            load(gate_w[:, :, :, :], I["gate_w"], "gate_in")
            for name in ROWS:
                load(rowvec(name), I["row_" + name].partition_broadcast(P), "rows_in")
            load(ffn_rt, I["router_wT"].rearrange("(k p) n -> p k n", p=128), "ffn_in")
            load(ffn_w1, I["ffn_w1T"].rearrange("(k p) n -> p k n", p=128), "ffn_in")
            load(ffn_w2, I["ffn_w2T"], "ffn_in")

            act.wait_ge(S("consts"), 1)
            sqrt_for(0, 0)
            sqrt_for(1, 1)
            transposed("xnT", xnT)
            act.wait_ge(S("cols_in"), 16)
            for j in range(TT):
                act.wait_ge(S("psum_full"), filled("hT", j + 1))
                for k in range(KT):
                    ins = act.activation(col(4)[:, k, P * j:P * j + P], B("hT", j)[:, P * k:P * k + P], ACT.Identity,
                                         scale=colvec("n1_g", k), bias=colvec("n1_b", k))
                ins.then_inc(S("act_read"), 1)
            for j in range(TT):
                for q in range(4):
                    r, (a, w) = q // 2, HALF[q % 2]
                    copy_out("A", 4 * j + q, AT[:, r, j, a:a + w], B("A", 4 * j + q)[0:P, 0:w])
            for n in range(16):
                m, (a, w) = n // 2, HALF[n % 2]
                copy_out("kq", n, col(5 if m < 4 else 6)[:, m % 4, a:a + w], B("kq", n)[:, 0:w], ACT.Identity, bias=colvec("kq_b", m))
            for j in range(TT):
                copy_out("v", j, row(3)[:, j, :], B("v", j)[0:P, :])
            act.wait_ge(S("act_read"), READ0["kq"] + 8)
            act.activation(col(4)[:, :, 0:N], col(5)[:, :, 0:N], ACT.Square).then_inc(S("sqk"), 1)
            load(proj_w, I["L0_mix_proj_w"].rearrange("(k p) n -> p k n", p=128), "projw_in")
            load(mlp_w1, I["L0_mix_mlp_w1"].rearrange("(k p) n -> p k n", p=128), "mlp1_in")
            load(mlp_w2, I["L0_mix_mlp_w2"].rearrange("(k p) n -> p k n", p=128), "mlp2_in")

            def exps(w, xd, dst, xdv):
                copy_out(xd, 0, xdv, B(xd)[0:P, 0:TT])
                act.wait_ge(S("act_read"), READ0[xd] + 1)
                for j in range(TT):
                    act.wait_ge(S("psum_full"), filled(w, j // 2 + 1))
                    act.activation(dst[:, j, :], B(w, j // 2)[0:P, M * (j % 2):M * (j % 2) + M], ACT.Exp,
                                   bias=xdv[:, j:j + 1]).then_inc(S("act_read"), 1)

            exps("wk", "xdk", kp, xdk)
            act.wait_ge(S("sqk"), 1)
            act.wait_ge(S("act_read"), READ0["kq"] + 16)
            act.activation(col(5)[:, :, 0:N], col(6)[:, :, 0:N], ACT.Square).then_inc(S("sqq"), 1)
            exps("wq", "xdq", qp, xdq)
            for j in range(TT):
                copy_out("qpT", j, qpT[:, :, P * j:P * j + P], B("qpT", j)[:, 0:2 * P].rearrange("p (c t) -> p c t", c=2))
            for n in range(2):
                copy_out("kptv", n, vtkp[:, 2 * n:2 * n + 2, :], B("kptv", n)[:, :].rearrange("p (k m) -> p k m", k=2))
            copy_out("ks", 0, ksum, B("ks")[:, 0:2])
            act.wait_ge(S("psum_full"), filled("xdq", 1))
            for n in range(2):
                copy_out("pv", n, pv[:, n, :], B("pv", n)[:, :])
            act.wait_ge(S("rD"), 1)
            for j in range(TT):
                copy_out("proj", j, row(4)[:, j, :], B("proj", j)[0:P, :], ACT.Copy, scale=rD[:, j:j + 1])
            copy_out("gate1", 0, gates[:, 0, :, :], B("gate1")[0:P, 0:2 * TT].rearrange("p (j r) -> p j r", r=2), ACT.Sigmoid)
            load(root[0], I["L0_gnn_root1"].rearrange("(k p) n -> p k n", p=128), "root1_in")
            sqrt_for(2, 1)
            for j in range(TT):
                act.wait_ge(S("psum_full"), filled("h2T", j + 1))
                for k in range(KT):
                    ins = act.activation(col(5)[:, k, P * j:P * j + P], B("h2T", j)[:, P * k:P * k + P], ACT.Identity,
                                         scale=colvec("n2_g", k), bias=colvec("n2_b", k))
                ins.then_inc(S("act_read"), 1)
            for n in range(8):
                m, (a, w) = n // 2, HALF[n % 2]
                copy_out("m1", n, col(6)[:, m, a:a + w], B("m1", n)[:, 0:w], ACT.Gelu, bias=colvec("mlp_b1", m))
            load(root[1], I["L0_gnn_root2"].rearrange("(k p) n -> p k n", p=128), "root2_in")
            act.wait_ge(S("act_read"), READ0["gate1"] + 1)
            act.wait_ge(S("y_row"), 5)
            act.wait_ge(S("psum_full"), filled("h2T", 5))
            act.wait_ge(S("x_y"), 5)
            for j in range(TT):
                for r in range(2):
                    act.activation(row(3 + r)[:, j, :], xn[:, j, :], ACT.Copy, scale=gates[:, 0, j, r:r + 1]).then_inc(S("xg1"), 1)
            for j in range(TT):
                copy_out("m2", j, row(5)[:, j, :], B("m2", j)[0:P, :])

            act.wait_ge(S("x_mix"), 5)
            for l, (Z, last) in enumerate((("Z1", "h1T"), ("Z2", "o2"))):
                if l == 1:
                    for n in range(8):
                        m, (a, w) = n // 2, HALF[n % 2]
                        copy_out("h1T", n, col(1)[:, m, a:a + w], B("h1T", n)[:, 0:w], ACT.Relu, bias=colvec("bias1", m))
                    copy_out("gate2", 0, gates[:, 1, :, :], B("gate2")[0:P, 0:2 * TT].rearrange("p (j r) -> p j r", r=2), ACT.Sigmoid)
                    act.wait_ge(S("act_read"), READ0["gate2"] + 1)
                    for j in range(TT):
                        act.wait_ge(S("psum_full"), filled("h1r", j + 1))
                        for r in range(2):
                            ins = act.activation(row(3 + r)[:, j, :], B("h1r", j)[0:P, :], ACT.Copy, scale=gates[:, 1, j, r:r + 1])
                        ins.then_inc(S("act_read"), 1)
                for n in range(16):
                    r, m, (a, w) = n // 8, n // 2 % 4, HALF[n % 2]
                    copy_out(Z, n, col(5 + r)[:, m, a:a + w], B(Z, n)[:, 0:w])

            for n in range(7):
                w = min(4, 25 - 4 * n) * P
                copy_out("AnT", n, AT1[:, 500 * n:500 * n + w], B("AnT", n)[0:P, 0:w])
            sqrt_for(3, 0)
            transposed("xfT", col(2))
            act.wait_ge(S("rt_sub"), 1)
            act.activation(rtp, rtp, ACT.Exp).then_inc(S("rt_exp"), 1)
            for n in range(2):
                a, w = HALF[n]
                copy_out("hf", n, hfT[:, a:a + w], B("hf", n)[:, 0:w], ACT.Gelu, bias=colvec("ffn_b1", 0))
            for j in range(TT):
                copy_out("fy", j, row(4)[:, j, :], B("fy", j)[0:P, :])
            sqrt_for(4, 0)
            transposed("xn2T", col(2))
            SC = float(DH) ** -0.25
            copy_out("aq", 0, aqT, B("aq")[:, :].rearrange("p (k t) -> p k t", k=KT), ACT.Copy, scale=SC)
            act.wait_ge(S("bn_var"), 1)
            act.activation(sd[:, 0:KT], mv[:, 0:KT, 1:2].rearrange("p j o -> p (j o)"), ACT.Sqrt, bias=eps[:, 0:1]).then_inc(S("bn_std"), 1)
            copy_out("ak", 0, akT, B("ak")[:, :].rearrange("p (k t) -> p k t", k=KT), ACT.Copy, scale=SC)
            for k in range(KT):
                act.wait_ge(S("bn1"), k + 1)
                act.activation(col(3)[:, k, 0:N], col(3)[:, k, 0:N], ACT.Identity, bias=colvec("b1n", k)).then_inc(S("xbT"), 1)
            copy_out("av", 0, v_aug[:, :, 0:DH], B("av")[:, :].rearrange("p (h d) -> p h d", h=HEADS))
            for j in range(TT):
                copy_out("xbr", j, row(4)[:, j, :], B("xbr", j)[0:P, :])
            for n in range(8):
                m, (a, w) = n // 2, HALF[n % 2]
                copy_out("agg", n, col(5)[:, m, a:a + w], B("agg", n)[:, 0:w])
            copy_out("ad", 0, adiag, B("ad")[:, 0:16])
            act.wait_ge(S("kbias"), 1)
            for h in HEAD_ORDER:
                act.activation(ke[:, h, :], ub("uk", h), ACT.Exp, bias=abias_k[:, h:h + 1]).then_inc(S("act_read"), 1)
            for n in range(8):
                m, (a, w) = n // 2, HALF[n % 2]
                copy_out("conv", n, col(6)[:, m, a:a + w], B("conv", n)[:, 0:w], ACT.Relu, bias=colvec("b_conv", m))
            act.wait_ge(S("qbias"), 1)
            for h in HEAD_ORDER:
                act.activation(qe[:, h, :], ub("uq", h), ACT.Exp, bias=abias_q[:, h:h + 1]).then_inc(S("act_read"), 1)
            for n in range(3):
                w = min(6, 16 - 6 * n)
                copy_out("kv", n, kv_sb[:, 6 * n:6 * n + w, :], B("kv", n)[:, 0:65 * w].rearrange("p (g d) -> p g d", g=w))
            for n in range(4):
                copy_out("qfT", n, qfT[:, 2 * n:2 * n + 2, :, :], B("qfT", n)[:, :].rearrange("p (h c t) -> p h c t", h=2, c=2))
            copy_out("atT", 0, attnT, B("atT")[:, :].rearrange("p (k t) -> p k t", k=KT))
            copy_out("ha", 0, haT, B("ha")[:, :].rearrange("p (k t) -> p k t", k=KT))
            for n in range(8 + TT):
                act.wait_ge(S("xmin"), n + 1)
                w = HALF[n % 2][1] if n < 8 else H
                t = tmp[:, n % 2, 0:w] if n < 8 else tmp[0:P, n % 2, 0:w]
                act.activation(t, t, ACT.Exp).then_inc(S("xexp"), 1)
            for j in range(TT):
                copy_out("xv", j, row(5)[:, j, :], B("xv", j)[0:P, :])
            for n in range(8):
                m, (a, w) = n // 2, HALF[n % 2]
                copy_out("xo", n, hid_hi[:, m, a:a + w], B("xo", n)[:, 0:w])
            act.wait_ge(S("bn_var"), 2)
            act.activation(sd[:, 0:KT], mv[:, 0:KT, 1:2].rearrange("p j o -> p (j o)"), ACT.Sqrt, bias=eps[:, 0:1]).then_inc(S("bn_std"), 1)
            sqrt_for(5, 0)
            transposed("xeT", col(2))
            act.wait_ge(S("x_pad"), 1)
            act.wait_ge(S("act_read"), READ0["xeT"] + 5)
            act.activation(xe_hi[:, :, 0:N], col(2)[:, :, 0:N], ACT.Copy).then_inc(S("xe_high"), 1)
            act.wait_ge(S("el_sub"), 1)
            act.activation(eexp, eexp, ACT.Exp).then_inc(S("el_exp"), 1)
            act.wait_ge(S("elist"), 1)
            for n in range(2):
                w = (500, 125)[n]
                copy_out("combT", n, combT[:, 500 * n:500 * n + w], B("combT", n)[0:E1, 0:w])
            n_act = act.value_load(el_i[0:1, 8:9], min_val=2, max_val=E1)

            def split_chunk(it, c):
                act.wait_ge(S(f"ew_in{c % 2}"), 128 * it + 32 * (c // 2) + 32)
                act.wait_ge(S("y_mm"), 16 * it + 2 * c - 6 + Y0)
                act.activation(ew_hi[:, c % 4, :], weights[:, 2048 * (c % 2):2048 * (c % 2) + 2048], ACT.Copy).then_inc(S("ew_high"), 1)

            with act.Fori(0, n_act) as it:
                e = act.value_load(el_i[0:1, bass.ds(it, 1)], min_val=0, max_val=E1 - 1)
                split_chunk(it, 0)
                split_chunk(it, 1)
                act.wait_ge(S("eh_out"), 32 * it + 1)
                act.wait_ge(S("eb_in"), 32)
                act.activation(eb1_now[:, :], eb1[:, bass.ds(16 * e, 16)], ACT.Copy).then_inc(S("eb1_now"), 1)
                act.wait_ge(S("eb1_now"), it + 1)

                for f in range(16):
                    for hf in range(2):
                        a, w = ((0, 312), (312, 314))[hf]
                        n = 2 * f + hf
                        act.wait_ge(S("hid_split"), 16 * it + max(f - 3, 0) + 1)
                        act.wait_ge(S("eh_mm"), 32 * it + n + 1)
                        act.activation(hid[:, f % 4, a:a + w], bank[5 + n % 3][:, 0:w], ACT.Silu,
                                       bias=eb1_now[:, f:f + 1]).then_inc(S("eh_out"), 1)
                    if f % 2 == 0 and f < 12:
                        split_chunk(it, f // 2 + 2)

        @block.vector
        def _(dve):
            step = [0]

            def link(ins):
                step[0] += 1
                ins.then_inc(S("dve_step"), 1)
                dve.wait_ge(S("dve_step"), step[0])

            norms = [0]

            def layernorm(src, dst, name, wait=None):
                for j in range(TT):
                    if wait:
                        dve.wait_ge(S(wait), j + 1)
                    ins = dve.bn_stats(st[0:P, j, :], src[:, j, :])
                link(ins)
                for j in range(TT):
                    ins = dve.bn_aggr(mv[0:P, j, :], st[0:P, j, :])
                ins.then_inc(S("ln_var"), 1)
                norms[0] += 1
                dve.wait_ge(S("ln_std"), norms[0])
                link(dve.reciprocal(rs[0:P, :], sd[0:P, :]))
                for j in range(TT):
                    dve.tensor_scalar(dst[:, j, :], src[:, j, :], mv[0:P, j, 0:1], rs[0:P, j:j + 1],
                                      ALU.subtract, ALU.mult).then_inc(S(name), 1)

            bns = [0]

            def batchnorm(src, dst, gain, name):
                for k in range(KT):
                    for hf, (a, w) in enumerate(HALF):
                        ins = dve.bn_stats(tmp[:, 0, 12 * k + 6 * hf:12 * k + 6 * hf + 6], src[:, k, a:a + w])
                link(ins)
                for k in range(KT):
                    ins = dve.bn_aggr(mv[:, k, :], tmp[:, 0, 12 * k:12 * k + 12])
                ins.then_inc(S("bn_var"), 1)
                bns[0] += 1
                dve.wait_ge(S("bn_std"), bns[0])
                link(dve.reciprocal(rs[:, 0:KT], sd[:, 0:KT]))
                link(dve.tensor_tensor(rs[:, 0:KT], rs[:, 0:KT], cols[:, COL_AT[gain]:COL_AT[gain] + KT], ALU.mult))
                for k in range(KT):
                    dve.tensor_scalar(dst[:, k, 0:N], src[:, k, 0:N], mv[:, k, 0:1], rs[:, k:k + 1],
                                      ALU.subtract, ALU.mult).then_inc(S(name), 1)

            def bc(v, e):
                return v.unsqueeze(2).to_broadcast([P, TT, e])

            def iota_bc(e):
                return iota_e[0:P, 0:e].unsqueeze(1).to_broadcast([P, TT, e])

            def top_two(val, e, tables, best, low):
                eq, hot = tables[0], tables[1:3]
                idx = small[0:P, 20:25]
                for i in range(2):
                    link(dve.tensor_reduce(best[i], val, AX.X, ALU.max))
                    link(dve.tensor_tensor(eq, val, bc(best[i], e), ALU.is_equal))
                    link(dve.scalar_tensor_tensor(eq, eq, -float(e), iota_bc(e), ALU.mult, ALU.add))
                    link(dve.tensor_reduce(idx, eq, AX.X, ALU.min))
                    link(dve.tensor_tensor(hot[i], eq, bc(idx, e), ALU.is_equal))
                    if i == 0:
                        link(dve.scalar_tensor_tensor(tables[3], hot[0], -low, val, ALU.mult, ALU.add))
                        val = tables[3]

            dve.wait_ge(S("x_in"), 16)
            dve.wait_ge(S("consts"), 1)
            layernorm(x, xn, "xn_row")
            layernorm(xn, row(3), "h_row", wait="xn_row")

            dve.wait_ge(S("edges_in"), 16)
            link(dve.tensor_copy(srcf, edges[:, 0, :]))
            link(dve.tensor_copy(dstf, edges[:, 1, :]))
            link(dve.tensor_copy(relf, edges[:, 2, :]))
            link(dve.tensor_scalar(relf, relf, 0.0, 1024.0, ALU.not_equal, ALU.mult))
            link(dve.tensor_tensor(relf, relf, dstf, ALU.add))
            for j in range(TT):
                dve.tensor_scalar(keyf[:, j, :], relf, -float(P * j), None, ALU.add)
                link(dve.tensor_scalar(gez[:, j, :], dstf, float(P * j), None, ALU.is_ge))
            for j in range(TT - 1):
                dve.tensor_tensor(pres[:, j, :], gez[:, j, :], gez[:, j + 1, :], ALU.subtract)
            dve.tensor_copy(pres[:, TT - 1, :], gez[:, TT - 1, :]).then_inc(S("presence"), 1)
            rr = rg[:, 0:TT * EG].rearrange("p (j q) -> p j q", j=TT)
            rt2 = rg[:, 200:210]
            iq = iota_e[0:1, 0:EG].unsqueeze(1).to_broadcast([1, TT, EG])
            dve.wait_ge(S("psum_full"), filled("rng", 1))
            cnt = B("rng")[0:1, 0:TT * ET].rearrange("p (j q u) -> p j q u", j=TT, u=EU)
            dve.tensor_reduce(rr, cnt, AX.X, ALU.add).then_inc(S("rng_out"), 1)
            dve.wait_ge(S("rng_out"), 1)
            link(dve.tensor_scalar(rr, rr, 0.5, None, ALU.is_ge))
            hit = small[0:1, 850:850 + 100]
            last, first = rt2[:, 0:5], rt2[:, 5:10]
            t40 = tmp[0:1, 1, 0:TT * EG].rearrange("p (j q) -> p j q", j=TT)
            link(dve.scalar_tensor_tensor(t40, iq, 1.0, rr, ALU.add, ALU.mult))
            link(dve.tensor_reduce(last, t40, AX.X, ALU.max))
            link(dve.scalar_tensor_tensor(t40, iq, -float(EG), rr, ALU.add, ALU.mult))
            link(dve.tensor_reduce(first, t40, AX.X, ALU.min))
            link(dve.tensor_scalar(first, first, float(EG), float(EG - 1), ALU.add, ALU.min))
            link(dve.tensor_tensor(last, last, first, ALU.subtract))
            link(dve.tensor_scalar(last, last, 1.0, None, ALU.max))
            dve.tensor_copy(rng_i[0:1, 0:10], rt2).then_inc(S("ranges"), 1)
            dve.wait_ge(S("ranges"), 1)
            for j in range(TT):
                groups = dve.value_load(rng_i[0:1, j:j + 1], min_val=1, max_val=EG)
                q0 = dve.value_load(rng_i[0:1, 5 + j:6 + j], min_val=0, max_val=EG - 1)
                if j:
                    dve.wait_ge(S("psum_full"), filled("A", 4 * j))
                with dve.Fori(0, groups) as i:
                    for u in range(EU):
                        dve.wait_ge(S(f"oh_used{j}"), EU * i + u + 1)
                        dve.tensor_scalar(oh_src[u], iota_src, small[0:P, bass.ds(EU * q0 + EU * i + u, 1)], None, ALU.is_equal)
                        dve.tensor_scalar(oh_dst[u], iota_dst, small[0:P, bass.ds(EU * q0 + EU * i + (ET * (j + 1) + u), 1)], None,
                                          ALU.is_equal).then_inc(S(f"oh_ready{j}"), 1)

            def sum_bases(l, p0, p1):
                done = S(f"w{l}_sum")
                if p0 == 0:
                    if l == 0:
                        dve.wait_ge(S("att_in"), 16)
                    for u in range(2):
                        dve.wait_ge(S(f"basis_in{u}"), 16 * (15 * l + 1))
                        for r in range(2):
                            if u == 0:
                                dve.tensor_scalar(wrel[l][r], basis[u], att[:, l, r, 0:1], None, ALU.mult).then_inc(done, 1)
                            else:
                                dve.wait_ge(done, r + 1)
                                dve.scalar_tensor_tensor(wrel[l][r], basis[u], att[:, l, r, 1:2], wrel[l][r],
                                                         ALU.mult, ALU.add).then_inc(done, 1)
                    p0 = 1
                with dve.Fori(p0, p1) as p:
                    for u in range(2):
                        dve.wait_ge(S(f"basis_in{u}"), 16 * p + 16 * (15 * l + 1))
                        for r in range(2):
                            dve.wait_ge(done, 4 * p + (2 * u + r - 1))
                            dve.scalar_tensor_tensor(wrel[l][r], basis[u], att[:, l, r, bass.ds(2 * p + u, 1)], wrel[l][r],
                                                     ALU.mult, ALU.add).then_inc(done, 1)

            dve.wait_ge(S("psum_full"), filled("A", 20))
            sum_bases(0, 0, 9)
            dve.wait_ge(S("psum_full"), filled("D", 1))
            dve.tensor_scalar(rD, B("D")[0:P, 0:TT], 256e-8, None, ALU.add).then_inc(S("D_out"), 1)
            dve.wait_ge(S("D_out"), 1)
            dve.reciprocal(rD, rD).then_inc(S("rD"), 1)
            sum_bases(0, 9, 10)
            layernorm(row(4), row(3), "yn_row", wait="y_row")
            sum_bases(0, 10, 15)
            sum_bases(1, 0, 15)

            dve.wait_ge(S("A_sum"), 1)
            deg = small[0:P, 982:987]
            link(dve.tensor_reduce(deg, AT[:, 0, :, :], AX.X, ALU.add))
            link(dve.tensor_scalar(deg, deg, 1.0, None, ALU.max))
            link(dve.reciprocal(deg, deg))
            for j in range(TT):
                dve.tensor_scalar(AT[:, 0, j, :], AT[:, 0, j, :], deg[:, j:j + 1], None, ALU.mult).then_inc(S("A_mean"), 1)
            for j in range(TT):
                dve.wait_ge(S("psum_full"), filled("o2", j + 1))
                dve.wait_ge(S("x_mix"), j + 1)
                dve.tensor_tensor(x[:, j, :], B("o2", j)[0:P, :], x[:, j, :], ALU.add).then_inc(S("o2_out"), 1)
            layernorm(x, row(1), "xf_row", wait="o2_out")

            dve.wait_ge(S("psum_full"), filled("rt", 1))
            T = [table(6, i, E0) for i in range(8)]
            b1, b2, s1 = small[0:P, 25:30], small[0:P, 30:35], small[0:P, 35:40]
            logit = B("rt")[0:P, 0:TT * E0].rearrange("p (j e) -> p j e", j=TT)
            dve.tensor_copy(T[0], logit).then_inc(S("rt_out"), 1)
            dve.wait_ge(S("rt_out"), 1)
            link(dve.tensor_reduce(b1, T[0], AX.X, ALU.max))
            dve.tensor_tensor(T[1], T[0], bc(b1, E0), ALU.subtract).then_inc(S("rt_sub"), 1)
            dve.wait_ge(S("rt_exp"), 1)
            link(dve.tensor_reduce(s1, T[1], AX.X, ALU.add))
            link(dve.reciprocal(s1, s1))
            link(dve.tensor_tensor(T[1], T[1], bc(s1, E0), ALU.mult))
            top_two(T[1], E0, [T[2], T[3], T[4], T[5]], [b1, b2], 4.0)
            dve.tensor_tensor(T[6], T[3], T[4], ALU.add).then_inc(S("chosen"), 1)
            dve.wait_ge(S("chosen"), 1)
            link(dve.tensor_tensor(T[1], T[1], T[6], ALU.mult))
            dve.wait_ge(S("psum_full"), filled("pos", 1))
            pos = B("pos")[0:P, 0:TT * E0].rearrange("p (j e) -> p j e", j=TT)
            dve.tensor_scalar(T[2], pos, float(CAP) - 0.5, None, ALU.is_lt).then_inc(S("pos_out"), 1)
            dve.wait_ge(S("pos_out"), 1)
            link(dve.tensor_tensor(T[2], T[2], T[1], ALU.mult))
            gate = small[0:P, 977:982]
            link(dve.tensor_reduce(gate, T[2], AX.X, ALU.add))
            for j in range(TT):
                dve.wait_ge(S("fy_row"), j + 1)
                dve.scalar_tensor_tensor(x[:, j, :], row(4)[:, j, :], gate[:, j:j + 1], x[:, j, :],
                                         ALU.mult, ALU.add).then_inc(S("x2"), 1)
            layernorm(x, row(1), "xn2_row", wait="x2")
            dve.memset(v_aug[:, :, DH:DH + 1], 1.0).then_inc(S("v_ones"), 1)
            dve.wait_ge(S("act_read"), READ0["xn2T"] + 5)
            batchnorm(col(2), col(3), "g1", "bn1")

            for n in range(4):
                dve.wait_ge(S("psum_full"), filled("uk", n + 1))
                h = HEAD_ORDER[2 * n]
                ins = dve.tensor_reduce(amax_k[:, h:h + 3:2], B("uk", n)[:, :].rearrange("p (h m) -> p h m", h=2), AX.X, ALU.max)
            ins.then_inc(S("kmax"), 1)
            dve.wait_ge(S("kmax_all"), 1)
            dve.wait_ge(S("act_read"), READ0["ad"] + 1)
            dve.scalar_tensor_tensor(abias_k, adiag[:, 8:16], -1.0, amax_kr, ALU.mult, ALU.subtract).then_inc(S("kbias"), 1)
            dve.wait_ge(S("act_read"), READ0["uk"] + 8)
            dve.tensor_scalar(ke, ke, 1.0 / 16, 1e-6, ALU.mult, ALU.add).then_inc(S("kf"), 1)
            dve.wait_ge(S("psum_full"), filled("agg", 8))
            for t in (hid_hi, hid_lo):
                link(dve.memset(t[:, :, N:COLW].bitcast(f32), 0.0))
            link(dve.tensor_copy(hid_hi[:, :, 0:N], col(2)[:, :, 0:N]))
            dve.tensor_tensor(hid_lo[:, :, 0:N], col(2)[:, :, 0:N], hid_hi[:, :, 0:N].bitcast(f32), ALU.subtract).then_inc(S("xn2_split"), 1)
            for n in range(4):
                dve.wait_ge(S("psum_full"), filled("uq", n + 1))
                h = HEAD_ORDER[2 * n]
                ins = dve.tensor_reduce(amax_q[:, h:h + 3:2], B("uq", n)[:, :].rearrange("p (h m) -> p h m", h=2), AX.X, ALU.max)
            link(ins)
            dve.scalar_tensor_tensor(abias_q, adiag[:, 0:8], -1.0, amax_q, ALU.mult, ALU.subtract).then_inc(S("qbias"), 1)
            dve.wait_ge(S("act_read"), READ0["uq"] + 8)
            dve.tensor_scalar(qe, qe, 1.0 / 16, 1e-6, ALU.mult, ALU.add).then_inc(S("qf"), 1)
            for n in range(2):
                dve.wait_ge(S("psum_full"), filled("at", n + 1))
                heads = B("at", n)[:, 0:4 * 65].rearrange("p (h d) -> p h d", h=4)
                den = aden[:, 4 * n:4 * n + 4]
                link(dve.tensor_scalar(den, heads[:, :, DH:DH + 1].rearrange("p h o -> p (h o)"), 1e-6, None, ALU.add))
                link(dve.reciprocal(den, den))
                dve.tensor_tensor(attn[:, 256 * n:256 * n + 256].rearrange("p (h d) -> p h d", h=4), heads[:, :, 0:DH],
                                  den.unsqueeze(2).to_broadcast([128, 4, DH]), ALU.mult).then_inc(S("at_out"), 1)
            dve.wait_ge(S("act_read"), READ0["conv"] + 8)
            link(dve.tensor_tensor(col(6)[:, :, 0:N], col(6)[:, :, 0:N], col(2)[:, :, 0:N], ALU.add))
            dve.wait_ge(S("act_read"), READ0["ha"] + 1)
            dve.tensor_tensor(col(6)[:, :, 0:NA], col(6)[:, :, 0:NA], haT, ALU.add)
            for k in range(KT):
                ins = dve.tensor_scalar(col(6)[:, k, NA:N], col(6)[:, k, NA:N], haT[:, k, NA - 1:NA], None, ALU.add)
            link(ins)
            dve.memset(kvb, 0.0).then_inc(S("kvb_zero"), 1)

            def phi_tile(n):
                if n < 8:
                    a, w = HALF[n % 2]
                    return B("xq", n)[:, 0:w], tmp[:, n % 2, 0:w], col(3)[:, n // 2, a:a + w]
                return B("xk", n - 8)[0:P, :], tmp[0:P, n % 2, :], row(4)[:, n - 8, :]

            def phi_min(n):
                name, at = ("xq", n) if n < 8 else ("xk", n - 8)
                dve.wait_ge(S("psum_full"), filled(name, at + 1))
                if n >= 2:
                    dve.wait_ge(S("xq_out" if n - 2 < 8 else "xk_out"), n - 1 if n - 2 < 8 else n - 9)
                src, t, _ = phi_tile(n)
                dve.tensor_scalar(t, src, 0.0, None, ALU.min).then_inc(S("xmin"), 1)

            phi_min(0)
            for n in range(8 + TT):
                if n + 1 < 8 + TT:
                    phi_min(n + 1)
                dve.wait_ge(S("xexp"), n + 1)
                src, t, dst = phi_tile(n)
                dve.scalar_tensor_tensor(dst, src, 0.0, t, ALU.max, ALU.add).then_inc(S("xq_out" if n < 8 else "xk_out"), 1)
            dve.wait_ge(S("psum_full"), filled("xkv", 1))
            dve.wait_ge(S("kvb_zero"), 1)
            kvp = B("xkv")[:, :].rearrange("p (k e) -> p k e", k=KT)
            SCALE = float(DH) ** -0.5
            dve.tensor_scalar(kvb[0:64, :, 0:64], kvp[0:64, :, 0:64], SCALE, None, ALU.mult)
            dve.tensor_scalar(kvb[64:128, :, 64:128], kvp[64:128, :, 64:128], SCALE, None, ALU.mult).then_inc(S("xkv_out"), 1)
            bsum = small[:, 990:994]
            link(dve.tensor_tensor(bsum, cols[:, COL_AT["b_proj"]:COL_AT["b_proj"] + KT], cols[:, COL_AT["b2n"]:COL_AT["b2n"] + KT], ALU.add))
            for n in range(8):
                m, (a, w) = n // 2, HALF[n % 2]
                dve.wait_ge(S("act_read"), READ0["xo"] + n + 1)
                dve.tensor_tensor(hid_lo[:, m, a:a + w], B("xo", n)[:, 0:w], hid_hi[:, m, a:a + w].bitcast(f32),
                                  ALU.subtract).then_inc(S("xo_low"), 1)
            batchnorm(col(6), col(6), "g2", "bn2")
            dve.wait_ge(S("bn2"), 4)
            for n in range(8):
                m, (a, w) = n // 2, HALF[n % 2]
                dve.wait_ge(S("psum_full"), filled("xp", n + 1))
                dve.scalar_tensor_tensor(col(6)[:, m, a:a + w], B("xp", n)[:, 0:w], bsum[:, m:m + 1], col(6)[:, m, a:a + w],
                                         ALU.add, ALU.add).then_inc(S("xp_out"), 1)
            for j in range(TT):
                dve.wait_ge(S("psum_full"), filled("x3r", j + 1))
                dve.tensor_tensor(x[:, j, :], B("x3r", j)[0:P, :], x[:, j, :], ALU.add).then_inc(S("x3r_out"), 1)
            layernorm(x, row(1), "xe_row", wait="x3r_out")

            dve.wait_ge(S("xe_high"), 1)
            dve.tensor_tensor(xe_lo[:, :, 0:N], col(2)[:, :, 0:N], xe_hi[:, :, 0:N].bitcast(f32), ALU.subtract).then_inc(S("xe_low"), 1)
            U = [table(6, i, E1) for i in range(6)]
            dve.wait_ge(S("psum_full"), filled("el", 1))
            dve.wait_ge(S("Wg_in"), 32)
            dve.tensor_tensor(U[0], B("el")[0:P, 0:TT * E1].rearrange("p (j e) -> p j e", j=TT),
                              small[0:P, 0:E1].unsqueeze(1).to_broadcast([P, TT, E1]), ALU.add).then_inc(S("el_out"), 1)
            dve.wait_ge(S("el_out"), 1)
            top_two(U[0], E1, [U[1], U[2], U[3], U[4]], [b1, b2], 1e30)
            link(dve.tensor_tensor(U[4], U[2], U[3], ALU.add))
            sel = U[5].rearrange("p j e -> p (j e)")[:, 0:E1]
            dve.tensor_reduce(sel, U[4].rearrange("p j e -> p e j"), AX.X, ALU.add).then_inc(S("selected"), 1)
            dve.tensor_tensor(eexp, b2, b1, ALU.subtract).then_inc(S("el_sub"), 1)
            for i, (name, first) in enumerate((("y_mm", Y0), ("eh_out", 1), ("x4", TT), ("hid_split", 1))):
                dve.memset(small[0:1, 1015 + i:1016 + i], 0.0).then_inc(S(name), first)
            dve.wait_ge(S("psum_full"), filled("en", 1))
            act1, key1, srt = small[0:1, 800:808], small[0:1, 808:816], small[0:1, 816:824]
            dve.tensor_scalar(act1, B("en")[0:1, 0:E1], 0.5, None, ALU.is_ge).then_inc(S("en_out"), 1)
            dve.wait_ge(S("en_out"), 1)
            link(dve.scalar_tensor_tensor(key1, iota_e[0:1, 0:E1], -float(E1), act1, ALU.add, ALU.mult))
            link(dve.tensor_scalar(key1, key1, -1.0, None, ALU.mult))
            link(dve.max(srt, key1))
            link(dve.tensor_scalar(srt, srt, -1.0, float(E1), ALU.mult, ALU.add))
            link(dve.tensor_scalar(srt, srt, float(E1 - 1), None, ALU.min))
            link(dve.tensor_copy(el_i[0:1, 0:8], srt))
            link(dve.tensor_reduce(key1[:, 0:1], act1, AX.X, ALU.add))
            dve.tensor_copy(el_i[0:1, 8:9], key1[:, 0:1]).then_inc(S("elist"), 1)
            dve.wait_ge(S("el_exp"), 1)
            link(dve.tensor_scalar(s1, eexp, 1.0, None, ALU.add))
            link(dve.reciprocal(s1, s1))
            link(dve.tensor_tensor(b2, s1, eexp, ALU.mult))
            link(dve.tensor_tensor(U[2], U[2], bc(s1, E1), ALU.mult))
            link(dve.tensor_tensor(U[3], U[3], bc(b2, E1), ALU.mult))
            dve.tensor_tensor(comb, U[2], U[3], ALU.add).then_inc(S("comb"), 1)
            dve.wait_ge(S("elist"), 1)
            for j in range(TT):
                dve.wait_ge(S("psum_full"), filled("eb2", j + 1))
                dve.tensor_tensor(x[:, j, :], B("eb2", j)[0:P, :], x[:, j, :], ALU.add).then_inc(S("eb2_out"), 1)
            dve.wait_ge(S("eb2_out"), 5)
            n_act = dve.value_load(el_i[0:1, 8:9], min_val=2, max_val=E1)
            with dve.Fori(0, n_act) as it:
                e = dve.value_load(el_i[0:1, bass.ds(it, 1)], min_val=0, max_val=E1 - 1)
                dve.wait_ge(S("ew_high"), 8 * it + 2)
                dve.tensor_tensor(ew_lo[:, 1, :], weights[:, 2048:4096], ew_hi[:, 1, :].bitcast(f32), ALU.subtract).then_inc(S("ew_split1"), 1)
                for f in range(16):
                    dve.wait_ge(S("y_mm"), 16 * it + f - 3 + Y0)
                    dve.wait_ge(S("eh_out"), 32 * it + 2 * f + 3)
                    dve.tensor_copy(hid_hi[:, f % 4, :], hid[:, f % 4, :]).then_inc(S("hid_high"), 1)
                    dve.wait_ge(S("hid_high"), 16 * it + f + 1)
                    dve.tensor_tensor(hid_lo[:, f % 4, :], hid[:, f % 4, :], hid_hi[:, f % 4, :].bitcast(f32),
                                      ALU.subtract).then_inc(S("hid_split"), 1)
                dve.wait_ge(S("y_mm"), 16 * it + 16 + Y0)
                dve.wait_ge(S("x4"), TT * it + TT)
                for j in range(TT):
                    dve.scalar_tensor_tensor(x[:, j, :], bank[j][0:P, :], comb[:, j, bass.ds(e, 1)], x[:, j, :],
                                             ALU.mult, ALU.add).then_inc(S("x4"), 1)

        @block.tensor
        def _(pe):
            def group(out, pairs):
                for i, (a, b) in enumerate(pairs):
                    ins = pe.matmul(out, a, b, start=i == 0, stop=i == len(pairs) - 1)
                return ins

            def to_cols(stage, src, ready, n=TT, free=P):
                for j in range(n):
                    bk = claim(pe, stage, j)
                    pe.wait_ge(S(ready), j + 1)
                    for k in range(KT):
                        ins = pe.transpose(bk[:, P * k:P * k + P], src[:, j, 128 * k:128 * k + 128], ident[0:P, 0:P])
                    ins.then_inc(S("psum_full"), 1)

            def to_rows(stage, src):
                for j in range(TT):
                    bk = claim(pe, stage, j)
                    for k in range(KT):
                        ins = pe.transpose(bk[0:P, 128 * k:128 * k + 128], src[:, k, P * j:P * j + P], ident[:, :])
                    ins.then_inc(S("psum_full"), 1)

            def cols_out(stage, w, at, act_in, tiles=KT, n0=0, k_in=KT):
                for m in range(tiles):
                    for hf, (a, wd) in enumerate(HALF):
                        n = n0 + 2 * m + hf
                        bk = claim(pe, stage, n)
                        group(bk[:, 0:wd], [(w[:, k, at + 128 * m:at + 128 * m + 128], act_in[:, k, a:a + wd])
                                            for k in range(k_in)]).then_inc(S("psum_full"), 1)

            def rows_out(stage, act_in, w, at=0, k_in=KT, width=H):
                for j in range(TT):
                    bk = claim(pe, stage, j)
                    group(bk[0:P, 0:width], [(act_in[:, k, P * j:P * j + P], w[:, k, at:at + width])
                                             for k in range(k_in)]).then_inc(S("psum_full"), 1)

            def split_cols_out(stage, name):
                wh, wl = lin(ew_hi, name), lin(ew_lo, name)
                for n in range(8):
                    m, (a, w) = n // 2, ((0, 312), (312, 314))[n % 2]
                    bk = claim(pe, stage, n)
                    group(bk[:, 0:w], [(wt[:, k, 128 * m:128 * m + 128], t[:, k, a:a + w]) for k in range(KT)
                                       for wt, t in ((wh, hid_hi), (wh, hid_lo), (wl, hid_hi))]).then_inc(S("psum_full"), 1)

            def split_rows_out(stage, name):
                wh, wl = lin(ew_hi, name), lin(ew_lo, name)
                for j in range(TT):
                    bk = claim(pe, stage, j)
                    group(bk[0:P, :], [(t[:, k, P * j:P * j + P], wt[:, k, :]) for k in range(KT)
                                       for t, wt in ((hid_hi, wh), (hid_hi, wl), (hid_lo, wh))]).then_inc(S("psum_full"), 1)

            def small_rows(stage, act_in, w, width):
                bk = claim(pe, stage)
                for j in range(TT):
                    ins = group(bk[0:P, width * j:width * j + width], [(act_in[:, k, P * j:P * j + P], w[:, k, :]) for k in range(KT)])
                ins.then_inc(S("psum_full"), 1)

            pe.wait_ge(S("consts"), 1)
            to_cols("xnT", xn, "xn_row")
            to_cols("hT", row(3), "h_row")
            bk = claim(pe, "rng")
            pe.wait_ge(S("presence"), 1)
            group(bk[0:1, 0:TT * ET], [(ones[0:P, 0:1], pres.rearrange("p j t -> p (j t)"))]).then_inc(S("psum_full"), 1)
            pe.wait_ge(S("ranges"), 1)
            for j in range(TT):
                groups = pe.value_load(rng_i[0:1, j:j + 1], min_val=1, max_val=EG)
                parts = [(B("A", 4 * j + q), q // 2, HALF[q % 2]) for q in range(4)]
                for q, (bkq, r, (a, w)) in enumerate(parts):
                    claim(pe, "A", 4 * j + q)
                    pe.matmul(bkq[0:P, 0:w], zero[:, 0:P], zero[:, 0:w], start=True, stop=False)
                    if q < EU:
                        pe.matmul(bkq[0:P, 0:1], zero[:, 0:P], zero[:, 0:1], start=False, stop=False).then_inc(S(f"oh_used{j}"), 1)
                with pe.Fori(0, groups) as i:
                    for u in range(EU):
                        pe.wait_ge(S(f"oh_ready{j}"), EU * i + u + 1)
                        for bkq, r, (a, w) in parts:
                            ins = pe.matmul(bkq[0:P, 0:w], oh_dst[u][:, P * r:P * r + P], oh_src[u][:, a:a + w], start=False, stop=False)
                        ins.then_inc(S(f"oh_used{j}"), 1)
                for bkq, r, (a, w) in parts:
                    pe.matmul(bkq[0:P, 0:w], zero[:, 0:P], zero[:, 0:w], start=False, stop=True).then_inc(S("psum_full"), 1)

            pe.wait_ge(S("act_read"), READ0["hT"] + 5)
            pe.wait_ge(S("kqv_in"), 16)
            cols_out("kq", kqv_w, 0, col(4), tiles=8)
            rows_out("v", col(4), kqv_w, at=2 * H)
            pe.wait_ge(S("prm_in"), 16)

            def features(w, xd, srcT, squares, ready):
                for j in range(TT):
                    if j % 2 == 0:
                        bk = claim(pe, w, j // 2)
                    ins = group(bk[0:P, M * (j % 2):M * (j % 2) + M], [(srcT[:, k, P * j:P * j + P], prm_w[:, k, :]) for k in range(KT)])
                    if j % 2 == 1 or j == TT - 1:
                        ins.then_inc(S("psum_full"), 1)
                bk = claim(pe, xd)
                pe.wait_ge(S(ready), 1)
                for j in range(TT):
                    ins = group(bk[0:P, j:j + 1], [(squares[:, 0, P * j:P * j + P], eps[:, 2:3])])
                ins.then_inc(S("psum_full"), 1)

            pe.wait_ge(S("act_read"), READ0["kq"] + 8)
            features("wk", "xdk", col(5), col(4), "sqk_sum")
            pe.wait_ge(S("act_read"), READ0["kq"] + 16)
            features("wq", "xdq", col(6), col(5), "sqq_sum")
            for j in range(TT):
                bk = claim(pe, "qpT", j)
                pe.wait_ge(S("act_read"), READ0["wq"] + j + 1)
                for c in range(2):
                    ins = pe.transpose(bk[:, P * c:P * c + P], qp[:, j, 128 * c:128 * c + 128], ident[0:P, 0:P])
                ins.then_inc(S("psum_full"), 1)
            pe.wait_ge(S("act_read"), READ0["wk"] + 5)
            pe.wait_ge(S("vrow"), 5)
            for n in range(2):
                bk = claim(pe, "kptv", n)
                for k in (2 * n, 2 * n + 1):
                    ins = group(bk[:, M * (k % 2):M * (k % 2) + M], [(row(3)[:, j, 128 * k:128 * k + 128], kp[:, j, :]) for j in range(TT)])
                ins.then_inc(S("psum_full"), 1)
            bk = claim(pe, "ks")
            for c in range(2):
                ins = group(bk[:, c:c + 1], [(kp[:, j, 128 * c:128 * c + 128], ones[0:P, 0:1]) for j in range(TT)])
            ins.then_inc(S("psum_full"), 1)
            pe.wait_ge(S("act_read"), READ0["kptv"] + 2)
            pe.wait_ge(S("projw_in"), 16)
            for c in range(2):
                bk = claim(pe, "pv", c)
                group(bk[:, :], [(vtkp[:, k, 128 * c:128 * c + 128], proj_w[:, k, :]) for k in range(KT)]).then_inc(S("psum_full"), 1)
            bk = claim(pe, "D")
            pe.wait_ge(S("act_read"), READ0["ks"] + 1)
            pe.wait_ge(S("act_read"), READ0["qpT"] + 5)
            for j in range(TT):
                ins = group(bk[0:P, j:j + 1], [(qpT[:, c, P * j:P * j + P], ksum[:, c:c + 1]) for c in range(2)])
            ins.then_inc(S("psum_full"), 1)
            pe.wait_ge(S("act_read"), READ0["pv"] + 2)
            rows_out("proj", qpT, pv, k_in=2)
            pe.wait_ge(S("gate_in"), 16)
            small_rows("gate1", xnT, gate_w[:, 0, :, :], 2)
            to_cols("h2T", row(3), "yn_row")
            pe.wait_ge(S("act_read"), READ0["h2T"] + 5)
            pe.wait_ge(S("mlp1_in"), 16)
            cols_out("m1", mlp_w1, 0, col(5))
            pe.wait_ge(S("act_read"), READ0["m1"] + 8)
            pe.wait_ge(S("mlp2_in"), 16)
            rows_out("m2", col(6), mlp_w2)

            def neighbours(stage):
                for n in range(16):
                    r, m, (a, w) = n // 8, n // 2 % 4, HALF[n % 2]
                    bk = claim(pe, stage, n)
                    group(bk[:, 0:w], [(row(3 + r)[:, j, 128 * m:128 * m + 128], AT[:, r, j, a:a + w]) for j in range(TT)])\
                        .then_inc(S("psum_full"), 1)

            pe.wait_ge(S("act_read"), READ0["A"] + 20)
            pe.wait_ge(S("xg1"), 10)
            neighbours("Z1")
            pe.wait_ge(S("act_read"), READ0["Z1"] + 16)
            pe.wait_ge(S("root1_in"), 16)
            pe.wait_ge(S("w0_sum"), 60)
            for m in range(KT):
                for hf, (a, w) in enumerate(HALF):
                    bk = claim(pe, "h1T", 2 * m + hf)
                    group(bk[:, 0:w], [(wt[:, k, 128 * m:128 * m + 128], act_in[:, k, a:a + w])
                                       for wt, act_in in ((root[0], xnT), (wrel[0][0], col(5)), (wrel[0][1], col(6)))
                                       for k in range(KT)]).then_inc(S("psum_full"), 1)
            pe.wait_ge(S("act_read"), READ0["h1T"] + 8)
            small_rows("gate2", col(1), gate_w[:, 1, :, :], 2)
            to_rows("h1r", col(1))
            pe.wait_ge(S("act_read"), READ0["h1r"] + 5)
            neighbours("Z2")
            pe.wait_ge(S("act_read"), READ0["Z2"] + 16)
            pe.wait_ge(S("root2_in"), 16)
            pe.wait_ge(S("w1_sum"), 60)
            for j in range(TT):
                bk = claim(pe, "o2", j)
                group(bk[0:P, :], [(act_in[:, k, P * j:P * j + P], wt[:, k, :])
                                   for wt, act_in in ((root[1], col(1)), (wrel[1][0], col(5)), (wrel[1][1], col(6)))
                                   for k in range(KT)]).then_inc(S("psum_full"), 1)

            pe.wait_ge(S("A_mean"), 5)
            for n in range(7):
                bk = claim(pe, "AnT", n)
                for b in range(4 * n, min(4 * n + 4, 25)):
                    i, j = b // TT, b % TT
                    ins = pe.transpose(bk[0:P, P * (b % 4):P * (b % 4) + P], AT[:, 0, j, P * i:P * i + P], ident[0:P, 0:P])
                ins.then_inc(S("psum_full"), 1)
            to_cols("xfT", row(1), "xf_row")
            pe.wait_ge(S("act_read"), READ0["xfT"] + 5)
            pe.wait_ge(S("ffn_in"), 48)
            small_rows("rt", col(2), ffn_rt, E0)
            cols_out("hf", ffn_w1, 0, col(2), tiles=1)
            pe.wait_ge(S("act_read"), READ0["hf"] + 2)
            for j in range(TT):
                bk = claim(pe, "fy", j)
                group(bk[0:P, :], [(hfT[:, P * j:P * j + P], ffn_w2)]).then_inc(S("psum_full"), 1)
            bk = claim(pe, "pos")
            pe.wait_ge(S("chosen"), 1)
            chosen = table(6, 6, E0)
            for j in range(TT):
                ins = group(bk[0:P, E0 * j:E0 * j + E0], [(ones[0:P, 0:P], chosen[:, i, :]) for i in range(j)] + [(tri[:, :], chosen[:, j, :])])
            ins.then_inc(S("psum_full"), 1)

            to_cols("xn2T", row(1), "xn2_row")
            pe.wait_ge(S("act_read"), READ0["xn2T"] + 5)
            pe.wait_ge(S("Wqkvo_in"), 64)
            for stage, w in (("aq", Wq), ("ak", Wk)):
                bk = claim(pe, stage)
                for m in range(KT):
                    ins = group(bk[:, NA * m:NA * m + NA], [(w[:, k, 128 * m:128 * m + 128], col(2)[:, k, 0:NA]) for k in range(KT)])
                ins.then_inc(S("psum_full"), 1)
            bk = claim(pe, "av")
            group(bk[:, :], [(col(2)[:, k, 0:NA], Wv[:, k, :]) for k in range(KT)]).then_inc(S("psum_full"), 1)
            pe.wait_ge(S("xbT"), 4)
            to_rows("xbr", col(3))
            pe.wait_ge(S("act_read"), READ0["xbr"] + 5)
            pe.wait_ge(S("act_read"), READ0["AnT"] + 7)
            for n in range(8):
                m, (a, w) = n // 2, HALF[n % 2]
                bk = claim(pe, "agg", n)
                group(bk[:, 0:w], [(row(4)[:, i, 128 * m:128 * m + 128], An[:, i, a:a + w]) for i in range(TT)]).then_inc(S("psum_full"), 1)
            bk = claim(pe, "ad")
            pe.wait_ge(S("a_sq"), 2)
            for i, sq in enumerate((sq_aq, sq_ak)):
                for k in range(KT):
                    ins = group(bk[:, 8 * i + 2 * k:8 * i + 2 * k + 2], [(sq[:, k, :], halfsum[:, :])])
            ins.then_inc(S("psum_full"), 1)
            pe.wait_ge(S("projT_in"), 32)

            def random_features(stage, t):
                for n in range(4):
                    claim(pe, stage, n)
                    for h in HEAD_ORDER[2 * n:2 * n + 2]:
                        o = 64 * (h % 2)
                        ins = group(ub(stage, h), [(t[o:o + 64, h // 2, :], projT[o:o + 64, :])])
                    ins.then_inc(S("psum_full"), 1)

            random_features("uk", akT)
            pe.wait_ge(S("act_read"), READ0["agg"] + 8)
            pe.wait_ge(S("Wconv_in"), 16)
            cols_out("conv", W_conv, 0, col(5))
            random_features("uq", aqT)
            pe.wait_ge(S("kf"), 1)
            pe.wait_ge(S("act_read"), READ0["av"] + 1)
            pe.wait_ge(S("v_ones"), 1)
            for g in range(16):
                if g % 6 == 0:
                    bk = claim(pe, "kv", g // 6)
                h, c = g // 2, g % 2
                ins = group(bk[:, 65 * (g % 6):65 * (g % 6) + 65], [(ke[:, h, 128 * c:128 * c + 128], v_aug[:, h, :])])
                if g % 6 == 5 or g == 15:
                    ins.then_inc(S("psum_full"), 1)
            pe.wait_ge(S("qf"), 1)
            for n in range(4):
                bk = claim(pe, "qfT", n)
                for i in range(4):
                    h, c = 2 * n + i // 2, i % 2
                    ins = pe.transpose(bk[:, 128 * i:128 * i + 128], qe[:, h, 128 * c:128 * c + 128], ident[:, :])
                ins.then_inc(S("psum_full"), 1)
            pe.wait_ge(S("act_read"), READ0["kv"] + 3)
            pe.wait_ge(S("act_read"), READ0["qfT"] + 4)
            for n in range(2):
                bk = claim(pe, "at", n)
                for i in range(4):
                    h = 4 * n + i
                    ins = group(bk[:, 65 * i:65 * i + 65], [(qfT[:, h, c, :], kv_sb[:, 2 * h + c, :]) for c in range(2)])
                ins.then_inc(S("psum_full"), 1)
            bk = claim(pe, "atT")
            pe.wait_ge(S("at_out"), 2)
            for k in range(KT):
                ins = pe.transpose(bk[:, 128 * k:128 * k + 128], attn[:, 128 * k:128 * k + 128], ident[:, :])
            ins.then_inc(S("psum_full"), 1)
            bk = claim(pe, "ha")
            pe.wait_ge(S("act_read"), READ0["atT"] + 1)
            for m in range(KT):
                ins = group(bk[:, 128 * m:128 * m + 128], [(Wo[:, k, 128 * m:128 * m + 128], attnT[:, k, :]) for k in range(KT)])
            ins.then_inc(S("psum_full"), 1)
            pe.wait_ge(S("xn2_split"), 1)
            pe.wait_ge(S("lin_split"), 1)
            split_cols_out("xq", "q")
            pe.wait_ge(S("lin_split"), 3)
            split_rows_out("xk", "k")
            split_rows_out("xv", "v")
            bk = claim(pe, "xkv")
            pe.wait_ge(S("xk_out"), 5)
            pe.wait_ge(S("act_read"), READ0["xv"] + 5)
            for p in range(KT):
                ins = group(bk[:, 128 * p:128 * p + 128], [(row(4)[:, j, 128 * p:128 * p + 128], row(5)[:, j, 128 * p:128 * p + 128]) for j in range(TT)])
            ins.then_inc(S("psum_full"), 1)
            pe.wait_ge(S("xkv_out"), 1)
            pe.wait_ge(S("xq_out"), 8)
            for n in range(8):
                m, (a, w) = n // 2, HALF[n % 2]
                bk = claim(pe, "xo", n)
                group(bk[:, 0:w], [(kvb[:, m, :], col(3)[:, m, a:a + w])]).then_inc(S("psum_full"), 1)
            pe.wait_ge(S("xo_low"), 8)
            pe.wait_ge(S("lin_split"), 4)
            split_cols_out("xp", "proj")
            pe.wait_ge(S("xp_out"), 8)
            to_rows("x3r", col(6))
            to_cols("xeT", row(1), "xe_row")
            pe.wait_ge(S("act_read"), READ0["xeT"] + 5)
            pe.wait_ge(S("Wg_in"), 32)
            small_rows("el", col(2), Wg, E1)
            bk = claim(pe, "en")
            pe.wait_ge(S("selected"), 1)
            group(bk[0:1, 0:E1], [(ones[0:P, 0:1], table(6, 5, E1).rearrange("p j e -> p (j e)")[:, 0:E1])]).then_inc(S("psum_full"), 1)
            pe.wait_ge(S("comb"), 1)
            for n in range(2):
                bk = claim(pe, "combT", n)
                for j in ((0, 1, 2, 3), (4,))[n]:
                    ins = pe.transpose(bk[0:E1, P * (j % 4):P * (j % 4) + P], comb[:, j, :], ident[0:P, 0:P])
                ins.then_inc(S("psum_full"), 1)
            pe.wait_ge(S("act_read"), READ0["combT"] + 2)
            pe.wait_ge(S("eb_in"), 32)
            for j in range(TT):
                bk = claim(pe, "eb2", j)
                group(bk[0:P, :], [(combT[:, P * j:P * j + P], eb2)]).then_inc(S("psum_full"), 1)
            pe.wait_ge(S("eb2_out"), 5)
            pe.wait_ge(S("elist"), 1)
            pe.wait_ge(S("xe_low"), 1)
            n_act = pe.value_load(el_i[0:1, 8:9], min_val=2, max_val=E1)
            with pe.Fori(0, n_act) as it:
                def output(f):
                    pe.wait_ge(S("hid_split"), 16 * it + f + 2)
                    for j in range(TT):
                        hh, hl = (t[:, f % 4, P * j:P * j + P] for t in (hid_hi, hid_lo))
                        products = ((hh, w2_half(ew_hi, f)), (hh, w2_half(ew_lo, f)), (hl, w2_half(ew_hi, f)))
                        for i, (a, b) in enumerate(products):
                            ins = pe.matmul(bank[j][0:P, :], a, b, start=f == 0 and i == 0, stop=f == 15 and i == 2)
                    ins.then_inc(S("y_mm"), 1)

                for f in range(16):
                    if f % 2 == 0:
                        wait_split(pe, it, f // 2)
                    for hf, (a, w) in enumerate(((0, 312), (312, 314))):
                        n = 2 * f + hf
                        pe.wait_ge(S("eh_out"), 32 * it + max(n - 2, 0) + 1)
                        wh, wl = w1_half(ew_hi, f), w1_half(ew_lo, f)
                        group(bank[5 + n % 3][:, 0:w], [(wt[:, k, :], xt[:, k, a:a + w]) for k in range(KT)
                                                        for wt, xt in ((wh, xe_hi), (wh, xe_lo), (wl, xe_hi))]).then_inc(S("eh_mm"), 1)
                    if f == 1:
                        pe.wait_ge(S("x4"), TT * it + TT)
                    if f:
                        output(f - 1)
                output(15)


_COLS = {"n1_g": "L0_mix_n1_g", "n1_b": "L0_mix_n1_b", "n2_g": "L0_mix_n2_g", "n2_b": "L0_mix_n2_b", "mlp_b1": "L0_mix_mlp_b1",
         "bias1": "L0_gnn_bias1", "ffn_b1": "L0_ffn_b1", "b_conv": "L1_gnn_b_conv", "g1": "L1_gnn_norm1_g", "b1n": "L1_gnn_norm1_b",
         "g2": "L1_gnn_norm2_g", "b2n": "L1_gnn_norm2_b", "b_proj": "L1_mix_b_proj"}
_PLAIN = ["x", "L0_gnn_basis1", "L0_gnn_basis2", "L0_gnn_root1", "L0_gnn_root2", "L0_mix_kqv_w",
          "L0_mix_proj_w", "L0_mix_mlp_w1", "L0_mix_mlp_w2", "L1_gnn_Wq", "L1_gnn_Wk", "L1_gnn_Wv", "L1_gnn_Wo", "L1_gnn_W_conv",
          "L1_ffn_Wg", "L1_ffn_bg", "L1_ffn_W1", "L1_ffn_W2", "L1_ffn_b2"]


def kernel(**inputs):
    import numpy as _np
    import concourse.bacc as _bacc
    from concourse import mybir as _mybir
    from concourse.bass_utils import run_bass_kernel_spmd as _run

    g = {k: _np.asarray(v) for k, v in inputs.items()}
    laid = {name: g[name] for name in _PLAIN}
    by_feature = dict({n: g[src] for n, src in _COLS.items()}, kq_b=g["L0_mix_kqv_b"][:2 * H])
    laid["cols"] = _np.concatenate([by_feature[n].reshape(-1, 128).T for n, _ in COLS], axis=1)
    laid["edges"] = _np.stack([g["src"], g["dst"], g["edge_type_2"]]).reshape(3, ET, P).transpose(2, 0, 1)
    laid["att"] = _np.stack([g["L0_gnn_att1"], g["L0_gnn_att2"]])
    laid["gate_w"] = _np.stack([g[f"L0_gnn_gate_w{l}"][:, :, 0].reshape(2, KT, 128).transpose(2, 1, 0) for l in (1, 2)], axis=1)
    laid["prm_wT"] = g["L0_mix_w"].T
    laid["router_wT"] = g["L0_ffn_router_w"].T
    laid["ffn_w1T"] = g["L0_ffn_w1"].T
    laid["ffn_w2T"] = g["L0_ffn_w2"].T
    laid["projT"] = g["L1_gnn_proj"].T
    laid["w_qkvT"] = g["L1_mix_w_qkv"].T
    laid["w_projT"] = g["L1_mix_w_proj"].T
    laid["eb1"] = g["L1_ffn_b1"].reshape(E1, F1 // 128, 128).transpose(2, 0, 1).reshape(128, E1 * F1 // 128)
    for name, src in (("v_b", g["L0_mix_kqv_b"][2 * H:]), ("proj_b", g["L0_mix_proj_b"]), ("mlp_b2", g["L0_mix_mlp_b2"]),
                      ("bias2", g["L0_gnn_bias2"]), ("ffn_b2", g["L0_ffn_b2"])):
        laid["row_" + name] = src
    nc = _bacc.Bacc("TRN2", target_bir_lowering=False, num_devices=1)
    arrays, aps = {}, {}
    for name, a in laid.items():
        arrays["in_" + name] = _np.ascontiguousarray(a)
        aps[name] = nc.dram_tensor("in_" + name, a.shape, _mybir.dt.from_np(a.dtype), kind="ExternalInput").ap()
    out = nc.dram_tensor("out_0", (N, H), _mybir.dt.float32, kind="ExternalOutput").ap()
    gps_two_layers(nc, aps, out)
    r = _run(nc, [arrays], core_ids=[0])
    return r.results[0]["out_0"]
```

```python
import concourse.bass as bass
from concourse import mybir
from contextlib import ExitStack

N = 625
H = 512
NE = 10000
P = 125
TT = N // P
KT = H // 128
ET = NE // P
EU = 4
EG = ET // EU
NB = 30
M = 256
E0 = 64
CAP = 512
F0 = 128
E1, F1 = 8, 2048
HEADS, DH = 8, 64
NA = 128
HALF = ((0, 312), (312, 313))
USES1 = -(-NB // 4)
Y0 = 8
EVEN = ((0, 312), (311, 314))
ROW = TT * H
COLW = 626
SLOT = 2624

COLS = [("n1_g", 4), ("n1_b", 4), ("kq_b", 8), ("n2_g", 4), ("n2_b", 4), ("mlp_b1", 4), ("bias1", 4),
        ("ffn_b1", 1), ("b_conv", 4), ("g1", 4), ("b1n", 4), ("g2", 4), ("b2n", 4), ("b_proj", 4)]
COL_AT, _at = {}, 0
for _n, _c in COLS:
    COL_AT[_n] = _at
    _at += _c
NCOLS = _at
ROWS = {"v_b": 0, "proj_b": 1, "mlp_b2": 2, "bias2": 3, "ffn_b2": 4}

PSUM_ORDER = [("rng", 1), ("xnT", 5), ("hT", 5), ("A", 20),
              ("kq", 16), ("v", 5), ("wk", 3), ("xdk", 1), ("wq", 3), ("xdq", 1),
              ("qpT", 5), ("kptv", 2), ("ks", 1), ("pv", 2), ("D", 1), ("proj", 5), ("gate1", 1), ("h2T", 5), ("m1", 8),
              ("m2", 5), ("Z1", 16), ("h1T", 8), ("gate2", 1), ("h1r", 5), ("Z2", 16), ("o2", 5),
              ("AnT", 7), ("xfT", 5), ("rt", 1), ("hf", 2), ("fy", 5), ("pos", 1),
              ("xn2T", 5), ("aq", 1), ("ak", 1), ("av", 1), ("xbr", 5), ("agg", 8),
              ("ad", 1), ("uk", 4), ("conv", 8), ("uq", 4), ("kv", 3), ("qfT", 4),
              ("xqa", 4), ("at", 2), ("atT", 1), ("ha", 1),
              ("xqb", 4), ("xv", 5), ("xk", 5), ("xkv", 1), ("xo", 8), ("xp", 8), ("x3r", 5),
              ("xeT", 5), ("el", 1), ("en", 1), ("combT", 2), ("eb2", 5)]
TILE0, _at = {}, 0
for _n, _c in PSUM_ORDER:
    TILE0[_n] = _at
    _at += _c
ACT_READS = [("xnT", 5), ("hT", 5), ("A", 20), ("kq", 16), ("v", 5), ("xdk", 1), ("wk", 5), ("xdq", 1), ("wq", 5),
             ("qpT", 5), ("kptv", 2), ("ks", 1), ("pv", 2), ("proj", 5), ("gate1", 1), ("h2T", 5), ("m1", 8), ("m2", 5),
             ("Z1", 16), ("h1T", 8), ("gate2", 1), ("h1r", 5), ("Z2", 16), ("AnT", 7), ("xfT", 5), ("hf", 2), ("fy", 5),
             ("xn2T", 5), ("aq", 1), ("ak", 1), ("av", 1), ("xbr", 5), ("agg", 8), ("ad", 1),
             ("uk", 8), ("conv", 8), ("uq", 8), ("kv", 3), ("qfT", 4), ("atT", 1), ("ha", 1), ("xv", 5), ("xo", 8), ("xeT", 5),
             ("combT", 2)]
READ0, _at = {}, 0
for _n, _c in ACT_READS:
    READ0[_n] = _at
    _at += _c


def gps_two_layers(nc, I, out):
    f32, f16, i32, f32r = mybir.dt.float32, mybir.dt.float16, mybir.dt.int32, mybir.dt.float32r
    ALU, ACT, AX = mybir.AluOpType, mybir.ActivationFunctionType, mybir.AxisListType
    ctx = ExitStack()
    with ctx:
        def sb(name, shape, dt=f32):
            return ctx.enter_context(nc.sbuf_tensor(name, shape, dt))

        sems = {}

        def S(name):
            if name not in sems:
                sems[name] = ctx.enter_context(nc.semaphore(name))
            return sems[name]

        slot = [None] * 8
        slot[0], slot[7] = sb("slot0", [128, SLOT]), sb("slot7", [128, SLOT])
        bank = [ctx.enter_context(nc.psum_tensor(f"bank{i}", [128, 512], f32)) for i in range(8)]
        ident = sb("ident", [128, 128])
        ones = sb("ones", [128, 128])
        tri = sb("tri", [P, P])
        tmp = sb("tmp", [128, 2, 512])
        zero = sb("zero", [1, 320], f16)
        cols = sb("cols", [128, NCOLS])
        att = sb("att", [128, 2, 2, NB])
        gate_w = sb("gate_w", [128, 2, KT, 2])
        eps = sb("eps", [128, 3])
        st = sb("st", [128, TT, 6])
        mv = sb("mv", [128, TT, 2])
        sd = sb("sd", [128, TT])
        rs = sb("rs", [128, TT])
        gates = sb("gates", [P, 2, TT, 2])
        edges = sb("edges", [P, 3, ET], i32)
        small = sb("small", [128, 1024])
        rng_i = sb("rng_i", [1, 16], i32)
        el_i = sb("el_i", [1, 16], i32)

        with ExitStack() as before:
            def sb_before(name, shape, dt=f32):
                return before.enter_context(nc.sbuf_tensor(name, shape, dt))

            for i in range(1, 7):
                slot[i] = sb_before(f"slot{i}", [128, SLOT])
            AT = sb_before("AT", [P, 2, TT, N])
            weights = sb_before("weights", [128, 20736])
        half = {}
        for i in range(1, 7):
            half[i] = sb(f"half{i}", [128, KT, COLW], f32r)
            sb(f"_rest_of_slot{i}", [128, SLOT - KT * COLW])
        xe_hi, xe_lo = half[3], half[4]
        hid_hi, hid_lo = (sb(name, [128, 4, COLW], f32r) for name in ("hid_hi", "hid_lo"))
        sb("_rest_of_AT", [128, 2 * TT * N - 8 * COLW])
        sb("_raw_chunks", [128, 4096])
        ew_hi, ew_lo = (sb(name, [128, 4, 2048], f32r) for name in ("ew_hi", "ew_lo"))
        sb("_rest_of_weights", [128, 20736 - 4096 - 16384])

        def row(s):
            return slot[s][0:P, 0:ROW].rearrange("p (j n) -> p j n", j=TT)

        def col(s):
            return slot[s][:, 0:KT * COLW].rearrange("p (k t) -> p k t", k=KT)

        def wmat(at, k=KT, n=H):
            return weights[:, at:at + k * n].rearrange("p (k n) -> p k n", k=k)

        def rowvec(name):
            return slot[7][0:P, ROWS[name] * H:(ROWS[name] + 1) * H]

        def colvec(name, k):
            return cols[:, COL_AT[name] + k:COL_AT[name] + k + 1]

        x, xn, xnT = row(0), row(1), col(2)
        basis = [wmat(at) for at in (0, 2048, 8192, 10240)]
        wrel = [[wmat(4096 + 2048 * (2 * l + r)) for r in range(2)] for l in range(2)]
        kqv_w = wmat(12288, KT, 3 * H)
        proj_w, mlp_w1, mlp_w2 = wmat(12288), wmat(14336), wmat(16384)
        root = [wmat(12288), wmat(14336)]
        prm_w = wmat(18432, KT, M)
        ffn_rt, ffn_w1, ffn_w2 = wmat(19456, KT, E0), wmat(19712, KT, F0), weights[:, 20224:20736]
        Wq, Wk, Wv, Wo = wmat(0), wmat(2048), wmat(4096), wmat(6144)
        W_conv = wmat(8192)
        projT = weights[:, 18432:18432 + M]
        Wg = wmat(20480, KT, E1)
        oh = weights[0:P, 8192:8192 + 438 * (EU + 1)].bitcast(f16)
        oh_src = [oh[:, 876 * u:876 * u + N] for u in range(EU)]
        oh_dst = [oh[:, 876 * u + 626:876 * u + 876] for u in range(EU)]
        iota_src = oh[:, 876 * EU:876 * EU + N]
        iota_dst = oh[:, 876 * EU + 626:876 * EU + 876]
        srcf = small[0:P, 0:ET]
        keyf = small[0:P, ET:ET * (1 + TT)].rearrange("p (j t) -> p j t", j=TT)
        dstf, relf = small[0:P, 480:560], small[0:P, 560:640]
        pres = tmp[0:P, 0, 0:TT * ET].rearrange("p (j t) -> p j t", j=TT)
        gez = tmp[0:P, 1, 0:TT * ET].rearrange("p (j t) -> p j t", j=TT)
        rg = small[0:1, 640:960]
        AT0 = AT[:, 0, :, :].rearrange("p j s -> p (j s)")
        AT1 = AT[:, 1, :, :].rearrange("p j s -> p (j s)")
        An = AT[:, 1, :, :]

        LIN = {"q": 0, "k": 1, "v": 2, "proj": 3}
        LIN_ORDER = ["q", "v", "k", "proj"]

        agg_hi, agg_lo = half[5], half[3]
        conv_hi, conv_lo = (t[:, b, :].rearrange("p (k n) -> p k n", k=KT) for t, b in ((ew_hi, 3), (ew_lo, 1)))

        Z_AT = (5, 3)
        Z_hi, Z_lo = ((half[6], half[1]), (half[6], half[2])), (half[5], half[3])
        GATED = ((3, 4), (3, 1))
        wrel_raw = [[weights[:, 4096 + 2048 * (2 * l + r):4096 + 2048 * (2 * l + r + 1)] for r in range(2)] for l in range(2)]
        wrel_hi = [[ew_lo[:, b, :] for b in (2, 3)], [ew_hi[:, b, :] for b in (0, 1)]]
        wrel_lo = [[ew_hi[:, b, :] for b in (0, 1)], [ew_lo[:, b, :] for b in (0, 2)]]
        h1 = col(4)

        def lin(t, name):
            return t[:, LIN[name], :].rearrange("p (k n) -> p k n", k=KT)

        def wait_split(eng, it, c, part=1):
            if c == 1:
                eng.wait_ge(S("ew_split1"), it + 1)
            else:
                eng.wait_ge(S("ew_split"), 14 * it + (2 * max(c - 1, 0) + part + 1))

        def raw1(c):
            return wmat(2048 * (c % 2), KT, 256)

        def raw2(c):
            return wmat(2048 * (c % 2) + 1024, 2, H)

        def w1_half(t, f):
            return t[:, f // 2 % 4, 0:1024].rearrange("p (k f) -> p k f", k=KT)[:, :, 128 * (f % 2):128 * (f % 2) + 128]

        def w2_half(t, f):
            return t[:, f // 2 % 4, 1024 + H * (f % 2):1024 + H * (f % 2) + H]

        eb1 = sb("eb1", [128, E1 * F1 // 128])
        eb1_now = sb("eb1_now", [128, F1 // 128])
        eb2 = slot[7][0:E1, 512:1024]
        combT = slot[7][0:E1, 1024:1024 + N]

        aqT = slot[1][:, 0:512].rearrange("p (k t) -> p k t", k=KT)
        akT = slot[1][:, 512:1024].rearrange("p (k t) -> p k t", k=KT)
        sq_aq = slot[1][:, 1024:1536].rearrange("p (k t) -> p k t", k=KT)
        sq_ak = slot[1][:, 1536:2048].rearrange("p (k t) -> p k t", k=KT)
        haT = slot[1][:, 2048:2560].rearrange("p (k t) -> p k t", k=KT)
        qe = slot[3][:, 0:HEADS * M].rearrange("p (h m) -> p h m", h=HEADS)
        ke = slot[4][:, 0:HEADS * M].rearrange("p (h m) -> p h m", h=HEADS)
        qfT = slot[5][:, 0:HEADS * M].rearrange("p (h c t) -> p h c t", h=HEADS, c=2)
        v_aug = slot[7][:, 0:HEADS * (DH + 1)].rearrange("p (h d) -> p h d", h=HEADS)
        attn = slot[7][:, 520:1032]
        attnT = slot[7][:, 1032:1544].rearrange("p (k t) -> p k t", k=KT)
        kv_sb = slot[7][:, 1544:1544 + 1040].rearrange("p (g d) -> p g d", g=16)
        halfsum = sb("halfsum", [128, 2])
        kvb = slot[7][:, 0:512].rearrange("p (k e) -> p k e", k=KT)
        adiag = small[:, 16:32]
        amax_k, amax_kr, amax_q, abias_k, abias_q = (small[:, 32 + 8 * i:40 + 8 * i] for i in range(5))
        aden = small[:, 72:80]
        hid = col(5)
        comb = small[0:P, 128:128 + TT * E1].rearrange("p (j e) -> p j e", j=TT)

        kp = slot[4][0:P, 0:TT * M].rearrange("p (j m) -> p j m", j=TT)
        qp = slot[4][0:P, TT * M:2 * TT * M].rearrange("p (j m) -> p j m", j=TT)
        qpT = slot[6][:, 0:2 * COLW].rearrange("p (c t) -> p c t", c=2)
        vtkp = slot[6][:, 1252:1252 + 1024].rearrange("p (k m) -> p k m", k=KT)
        pv = slot[5][:, 0:1024].rearrange("p (c n) -> p c n", c=2)
        xdk, xdq, ksum, rD = small[0:P, 960:965], small[0:P, 965:970], small[:, 970:972], small[0:P, 972:977]
        hfT = slot[3][:, 0:N]
        HEAD_ORDER = [0, 2, 1, 3, 4, 6, 5, 7]

        def ub(stage, h):
            at = HEAD_ORDER.index(h)
            return B(stage, at // 2)[:, M * (at % 2):M * (at % 2) + M]

        def table(s, i, e):
            return slot[s][0:P, TT * e * i:TT * e * (i + 1)].rearrange("p (j e) -> p j e", j=TT)

        rtp, eexp = table(6, 1, E0), small[0:P, 40:45]
        iota_e = sb("iota_e", [128, E0])

        def B(stage, n=0):
            return bank[(TILE0[stage] + n) % 8]

        freed = {}
        for name, count in PSUM_ORDER:
            for n in range(count):
                freed[TILE0[name] + n] = (name, n + 1)
        for n in range(4):
            freed[TILE0["uk"] + n] = ("uk", 2 * n + 2)
            freed[TILE0["uq"] + n] = ("uq", 2 * n + 2)
        for n in range(3):
            freed[TILE0["wk"] + n] = ("wk", min(2 * n + 2, TT))
            freed[TILE0["wq"] + n] = ("wq", min(2 * n + 2, TT))

        for n in range(8):
            freed[TILE0["xo"] + n] = ("xo_low", n + 1)
            freed[TILE0["agg"] + n] = ("agg_low", n + 1)
            freed[TILE0["xqa"] + n if n < 4 else TILE0["xqb"] + n - 4] = ("xq", n + 1)

        def xq_tile(n):
            return ("xqa", n) if n < 4 else ("xqb", n - 4)

        def filled(stage, count):
            return TILE0[stage] + count

        def claim(pe, stage, n=0):
            g = TILE0[stage] + n
            if g >= 8:
                name, value = freed[g - 8]
                if name in READ0:
                    pe.wait_ge(S("act_read"), READ0[name] + value)
                else:
                    pe.wait_ge(S(name if name.endswith("_low") else name + "_out"), value)
            return B(stage, n)

        block = ctx.enter_context(nc.Block())

        @block.sync
        def _(sp):
            def load(dst, src, name):
                sp.dma_start(dst, src).then_inc(S(name), 16)

            load(edges[:, :, :], I["edges"], "edges_in")
            load(x, I["x"].rearrange("(j p) n -> p j n", p=P), "x_in")
            load(att[:, :, :, :], I["att"].partition_broadcast(128), "att_in")
            b = I["L0_gnn_basis1"].rearrange("b (k p) n -> b p k n", p=128)
            for u in range(4):
                if u == 2:
                    sp.wait_ge(S("psum_full"), filled("A", 20))
                load(basis[u], b[u], f"basis_in{u}")
            with sp.Fori(1, NB // 4) as q:
                for u in range(4):
                    sp.wait_ge(S("w0_sum"), 8 * q + (2 * u - 6))
                    sp.dma_start(basis[u], b[bass.ds(4 * q + u, 1)].rearrange("o p k n -> (o p) k n")).then_inc(S(f"basis_in{u}"), 16)
            for g in range(NB // 4 * 4, NB):
                sp.wait_ge(S("w0_sum"), 2 * g - 6)
                load(basis[g % 4], b[g], f"basis_in{g % 4}")
            b = I["L0_gnn_basis2"].rearrange("b (k p) n -> b p k n", p=128)
            for u in range(2):
                sp.wait_ge(S("w0_sum"), 2 * (NB - 2 + u) + 2)
                load(basis[u], b[u], f"basis_in{u}")
            with sp.Fori(1, NB // 2) as p:
                for u in range(2):
                    sp.wait_ge(S("w1_sum"), 4 * p + (2 * u - 2))
                    sp.dma_start(basis[u], b[bass.ds(2 * p + u, 1)].rearrange("o p k n -> (o p) k n")).then_inc(S(f"basis_in{u}"), 16)
            sp.wait_ge(S("psum_full"), filled("h1T", 8))
            load(ffn_rt, I["router_wT"].rearrange("(k p) n -> p k n", p=128), "ffn_in")
            load(ffn_w1, I["ffn_w1T"].rearrange("(k p) n -> p k n", p=128), "ffn_in")
            load(ffn_w2, I["ffn_w2T"], "ffn_in")
            sp.wait_ge(S("w1_sum"), 4 * 15)
            load(Wq, I["L1_gnn_Wq"].rearrange("(k p) n -> p k n", p=128), "Wqkvo_in")
            load(Wk, I["L1_gnn_Wk"].rearrange("(k p) n -> p k n", p=128), "Wqkvo_in")
            sp.wait_ge(S("psum_full"), filled("o2", 5))
            load(Wv, I["L1_gnn_Wv"].rearrange("(k p) n -> p k n", p=128), "Wqkvo_in")
            load(Wo, I["L1_gnn_Wo"].rearrange("(k p) n -> p k n", p=128), "Wqkvo_in")
            load(W_conv, I["L1_gnn_W_conv"].rearrange("(k p) n -> p k n", p=128), "Wconv_in")
            load(projT[0:64, :], I["projT"], "projT_in")
            load(projT[64:128, :], I["projT"], "projT_in")
            load(small[0:P, 0:E1], I["L1_ffn_bg"].partition_broadcast(P), "Wg_in")
            load(eb1[:, :], I["eb1"], "eb_in")
            sp.wait_ge(S("psum_full"), filled("fy", 5))
            load(Wg, I["L1_ffn_Wg"].rearrange("(k p) n -> p k n", p=128), "Wg_in")
            sp.wait_ge(S("psum_full"), filled("ak", 1))
            w_lin = [I["w_projT"] if name == "proj" else I["w_qkvT"][:, H * LIN[name]:H * LIN[name] + H] for name in LIN_ORDER]
            for i in range(4):
                if i >= 2:
                    sp.wait_ge(S("lin_split"), i - 1)
                load(wmat(2048 * (i % 2)), w_lin[i].rearrange("(k p) n -> p k n", p=128), f"lin_in{i % 2}")
            sp.wait_ge(S("psum_full"), filled("ha", 1))
            load(eb2, I["L1_ffn_b2"], "eb_in")
            sp.wait_ge(S("elist"), 1)
            sp.wait_ge(S("lin_split"), 4)
            n_act = sp.value_load(el_i[0:1, 8:9], min_val=2, max_val=E1)
            w1v = I["L1_ffn_W1"].rearrange("e (k p) f -> e p k f", p=128)
            w2v = I["L1_ffn_W2"].rearrange("e (f p) n -> e p f n", p=128)

            def load_chunk(e, c):
                w1c, w2c = raw1(c), raw2(c)
                sp.dma_start(w1c, w1v[bass.ds(e, 1), :, :, 256 * c:256 * c + 256].rearrange("o p k f -> (o p) k f")).then_inc(S(f"ew_in{c % 2}"), 16)
                sp.dma_start(w2c, w2v[bass.ds(e, 1), :, 2 * c:2 * c + 2, :].rearrange("o p f n -> (o p) f n")).then_inc(S(f"ew2_in{c % 2}"), 16)

            e = sp.value_load(el_i[0:1, 0:1], min_val=0, max_val=E1 - 1)
            for c in range(8):
                if c >= 2:
                    wait_split(sp, 0, c - 2)
                load_chunk(e, c)
            with sp.Fori(0, n_act - 1) as it:
                e = sp.value_load(el_i[0:1, bass.ds(it + 1, 1)], min_val=0, max_val=E1 - 1)
                for c in range(8):
                    wait_split(sp, it + 1 if c >= 2 else it, (c + 6) % 8)
                    load_chunk(e, c)
            for j in range(TT):
                sp.wait_ge(S("x4"), TT * n_act + (j + 1))
                sp.dma_start(out[P * j:P * j + P, :], x[:, j, :]).then_inc(S("stored"), 16)
            sp.wait_ge(S("stored"), 16 * TT)

        @block.gpsimd
        def _(pool):
            step = [0]

            def link(ins):
                step[0] += 1
                ins.then_inc(S("pool_step"), 1)
                pool.wait_ge(S("pool_step"), step[0])

            link(pool.memset(ident[:, :], 0.0))
            link(pool.memset(ones[:, :], 1.0))
            link(pool.memset(zero[:, :], 0.0))
            link(pool.memset(halfsum[:, :], 0.5))
            link(pool.memset(eps[:, 0:1], 1e-5))
            link(pool.memset(eps[:, 1:2], 1e-3))
            link(pool.memset(eps[:, 2:3], -0.5))
            link(pool.affine_select(out=ident[:, :], in_=ident[:, :], compare_op=ALU.not_equal, fill=1.0,
                                    base=0, pattern=[[-1, 128]], channel_multiplier=1))
            link(pool.affine_select(out=tri[:, :], in_=ones[0:P, 0:P], compare_op=ALU.is_gt, fill=0.0,
                                    base=0, pattern=[[1, P]], channel_multiplier=-1))
            link(pool.affine_select(out=halfsum[:, 0:1], in_=halfsum[:, 0:1], compare_op=ALU.is_ge, fill=0.0,
                                    base=63, pattern=[[0, 1]], channel_multiplier=-1))
            link(pool.affine_select(out=halfsum[:, 1:2], in_=halfsum[:, 1:2], compare_op=ALU.is_ge, fill=0.0,
                                    base=-64, pattern=[[0, 1]], channel_multiplier=1))
            link(pool.iota(iota_src, pattern=[[1, N]], base=0, channel_multiplier=0, allow_small_or_imprecise_dtypes=True))
            link(pool.iota(iota_e[:, :], pattern=[[1, E0]], base=0, channel_multiplier=0, allow_small_or_imprecise_dtypes=True))
            pool.iota(iota_dst, pattern=[[1024, 2], [1, P]], base=0, channel_multiplier=0,
                      allow_small_or_imprecise_dtypes=True).then_inc(S("consts"), 1)

            pool.wait_ge(S("rows_in"), 16 * len(ROWS))
            for j in range(TT):
                pool.wait_ge(S("act_read"), READ0["v"] + j + 1)
                pool.tensor_tensor(row(3)[:, j, :], row(3)[:, j, :], rowvec("v_b"), ALU.add).then_inc(S("vrow"), 1)
            for s, name in ((4, "sqk"), (5, "sqq")):
                pool.wait_ge(S(name), 1)
                link(pool.tensor_tensor(col(s)[:, 0:2, 0:N], col(s)[:, 0:2, 0:N], col(s)[:, 2:4, 0:N], ALU.add))
                pool.tensor_tensor(col(s)[:, 0, 0:N], col(s)[:, 0, 0:N], col(s)[:, 1, 0:N], ALU.add).then_inc(S(name + "_sum"), 1)
            pool.wait_ge(S("vrow"), 5)
            pool.wait_ge(S("psum_full"), filled("kptv", 2))
            for j in range(TT):
                pool.tensor_tensor(row(3)[:, j, :], row(3)[:, j, :], rowvec("proj_b"), ALU.add).then_inc(S("vb"), 1)
            for j in range(TT):
                pool.wait_ge(S("act_read"), READ0["proj"] + j + 1)
                pool.wait_ge(S("vb"), j + 1)
                pool.tensor_tensor(row(4)[:, j, :], row(4)[:, j, :], row(3)[:, j, :], ALU.add).then_inc(S("y_row"), 1)
            link(pool.tensor_tensor(rowvec("mlp_b2"), rowvec("mlp_b2"), rowvec("bias2"), ALU.add))
            pool.wait_ge(S("xn_row"), 5)
            for j in range(TT):
                link(pool.tensor_tensor(x[:, j, :], x[:, j, :], rowvec("mlp_b2"), ALU.add))
            pool.wait_ge(S("y_row"), 5)
            for j in range(TT):
                pool.tensor_tensor(x[:, j, :], x[:, j, :], row(4)[:, j, :], ALU.add).then_inc(S("x_y"), 1)
            for j in range(TT):
                pool.wait_ge(S("act_read"), READ0["m2"] + j + 1)
                pool.wait_ge(S("x_y"), j + 1)
                pool.tensor_tensor(x[:, j, :], x[:, j, :], row(5)[:, j, :], ALU.add).then_inc(S("x_mix"), 1)

            for r in range(2):
                pool.wait_ge(S("wrel_high"), r + 1)
                pool.tensor_tensor(wrel_lo[0][r], wrel_raw[0][r], wrel_hi[0][r].bitcast(f32), ALU.subtract).then_inc(S("wrel_low0"), 1)
            for l, Z in enumerate(("Z1", "Z2")):
                for n in range(16):
                    r, m, (a, w) = n // 8, n // 2 % 4, HALF[n % 2]
                    pool.wait_ge(S("Z_full"), 16 * l + n + 1)
                    pool.wait_ge(S("act_read"), READ0[Z] + n + 1)
                    pool.tensor_tensor(Z_lo[r][:, m, a:a + w], col(Z_AT[r])[:, m, a:a + w], Z_hi[l][r][:, m, a:a + w].bitcast(f32),
                                       ALU.subtract).then_inc(S("Z_low"), 1)

            pool.wait_ge(S("psum_full"), filled("Z2", 16))
            pool.tensor_tensor(AT0, AT0, AT1, ALU.add).then_inc(S("A_sum"), 1)
            for j in range(TT):
                pool.wait_ge(S("act_read"), READ0["fy"] + j + 1)
                pool.tensor_tensor(row(4)[:, j, :], row(4)[:, j, :], rowvec("ffn_b2"), ALU.add).then_inc(S("fy_row"), 1)
            pool.wait_ge(S("act_read"), READ0["ak"] + 1)
            pool.tensor_tensor(sq_ak, akT, akT, ALU.mult).then_inc(S("a_sq"), 1)
            pool.wait_ge(S("act_read"), READ0["aq"] + 1)
            pool.tensor_tensor(sq_aq, aqT, aqT, ALU.mult).then_inc(S("a_sq"), 1)

            pool.wait_ge(S("Wconv_in"), 16)
            pool.tensor_copy(conv_hi, W_conv).then_inc(S("conv_high"), 1)
            pool.wait_ge(S("conv_high"), 1)
            pool.tensor_tensor(conv_lo, W_conv, conv_hi.bitcast(f32), ALU.subtract).then_inc(S("conv_split"), 1)

            def split_linear(i, used):
                hi, lo = (t[:, LIN[LIN_ORDER[i]], :] for t in (ew_hi, ew_lo))
                raw = weights[:, 2048 * (i % 2):2048 * (i % 2) + 2048]
                pool.wait_ge(S(f"lin_in{i % 2}"), 16 * (i // 2) + 16)
                pool.wait_ge(S("psum_full"), used)
                pool.tensor_copy(hi, raw).then_inc(S("lin_high"), 1)
                pool.wait_ge(S("lin_high"), i + 1)
                pool.tensor_tensor(lo, raw, hi.bitcast(f32), ALU.subtract).then_inc(S("lin_split"), 1)

            split_linear(0, filled("av", 1))
            pool.wait_ge(S("kmax"), 1)
            pool.partition_all_reduce(amax_kr, amax_k, 128, bass.bass_isa.ReduceOp.max).then_inc(S("kmax_all"), 1)
            split_linear(1, filled("conv", 8))
            split_linear(2, filled("ha", 1))
            split_linear(3, filled("uq", 4))
            pool.wait_ge(S("psum_full"), filled("xo", 8))
            link(pool.memset(xe_hi[:, :, N:COLW].bitcast(f32), 0.0))
            pool.memset(xe_lo[:, :, N:COLW].bitcast(f32), 0.0).then_inc(S("x_pad"), 1)
            pool.wait_ge(S("elist"), 1)
            n_act = pool.value_load(el_i[0:1, 8:9], min_val=2, max_val=E1)
            with pool.Fori(0, n_act) as it:
                for c in (0, 2, 3, 4, 5, 6, 7):
                    for part in range(2):
                        at = 1024 * part
                        pool.wait_ge(S("ew_high"), 16 * it + (2 * c + part + 1))
                        pool.tensor_tensor(ew_lo[:, c % 4, at:at + 1024], weights[:, 2048 * (c % 2) + at:2048 * (c % 2) + at + 1024],
                                           ew_hi[:, c % 4, at:at + 1024].bitcast(f32), ALU.subtract).then_inc(S("ew_split"), 1)

        @block.scalar
        def _(act):
            def load(dst, src, name):
                act.dma_start(dst, src).then_inc(S(name), 16)

            step = [0]

            def link(ins):
                step[0] += 1
                ins.then_inc(S("act_step"), 1)
                act.wait_ge(S("act_step"), step[0])

            def sqrt_for(n, e):
                act.wait_ge(S("ln_var"), n + 1)
                act.activation(sd[:, :] if e == 2 else sd[0:P, :], mv[0:P, :, 1:2].rearrange("p j o -> p (j o)"), ACT.Sqrt,
                               bias=eps[0:P, e:e + 1]).then_inc(S("ln_std"), 1)

            def copy_out(stage, n, dst, src, func=ACT.Copy, **kw):
                act.wait_ge(S("psum_full"), filled(stage, n + 1))
                act.activation(dst, src, func, **kw).then_inc(S("act_read"), 1)

            def transposed(stage, dst):
                for j in range(TT):
                    copy_out(stage, j, dst[:, :, P * j:P * j + P], B(stage, j)[:, 0:KT * P].rearrange("p (k t) -> p k t", k=KT))

            load(cols[:, :], I["cols"], "cols_in")
            load(kqv_w, I["L0_mix_kqv_w"].rearrange("(k p) n -> p k n", p=128), "kqv_in")
            load(prm_w, I["prm_wT"].rearrange("(k p) n -> p k n", p=128), "prm_in")
            load(gate_w[:, :, :, :], I["gate_w"], "gate_in")
            for name in ROWS:
                load(rowvec(name), I["row_" + name].partition_broadcast(P), "rows_in")

            act.wait_ge(S("consts"), 1)
            sqrt_for(0, 0)
            sqrt_for(1, 1)
            transposed("xnT", xnT)
            act.wait_ge(S("cols_in"), 16)
            for j in range(TT):
                act.wait_ge(S("psum_full"), filled("hT", j + 1))
                for k in range(KT):
                    ins = act.activation(col(4)[:, k, P * j:P * j + P], B("hT", j)[:, P * k:P * k + P], ACT.Identity,
                                         scale=colvec("n1_g", k), bias=colvec("n1_b", k))
                ins.then_inc(S("act_read"), 1)
            for j in range(TT):
                for q in range(4):
                    r, (a, w) = q // 2, HALF[q % 2]
                    copy_out("A", 4 * j + q, AT[:, r, j, a:a + w], B("A", 4 * j + q)[0:P, 0:w])
            for n in range(16):
                m, (a, w) = n // 2, HALF[n % 2]
                copy_out("kq", n, col(5 if m < 4 else 6)[:, m % 4, a:a + w], B("kq", n)[:, 0:w], ACT.Identity, bias=colvec("kq_b", m))
            for j in range(TT):
                copy_out("v", j, row(3)[:, j, :], B("v", j)[0:P, :])
            act.wait_ge(S("act_read"), READ0["kq"] + 8)
            act.activation(col(4)[:, :, 0:N], col(5)[:, :, 0:N], ACT.Square).then_inc(S("sqk"), 1)
            load(proj_w, I["L0_mix_proj_w"].rearrange("(k p) n -> p k n", p=128), "projw_in")
            load(mlp_w1, I["L0_mix_mlp_w1"].rearrange("(k p) n -> p k n", p=128), "mlp1_in")
            load(mlp_w2, I["L0_mix_mlp_w2"].rearrange("(k p) n -> p k n", p=128), "mlp2_in")

            def exps(w, xd, dst, xdv):
                copy_out(xd, 0, xdv, B(xd)[0:P, 0:TT])
                act.wait_ge(S("act_read"), READ0[xd] + 1)
                for j in range(TT):
                    act.wait_ge(S("psum_full"), filled(w, j // 2 + 1))
                    act.activation(dst[:, j, :], B(w, j // 2)[0:P, M * (j % 2):M * (j % 2) + M], ACT.Exp,
                                   bias=xdv[:, j:j + 1]).then_inc(S("act_read"), 1)

            exps("wk", "xdk", kp, xdk)
            act.wait_ge(S("sqk"), 1)
            act.wait_ge(S("act_read"), READ0["kq"] + 16)
            act.activation(col(5)[:, :, 0:N], col(6)[:, :, 0:N], ACT.Square).then_inc(S("sqq"), 1)
            exps("wq", "xdq", qp, xdq)
            for j in range(TT):
                copy_out("qpT", j, qpT[:, :, P * j:P * j + P], B("qpT", j)[:, 0:2 * P].rearrange("p (c t) -> p c t", c=2))
            for n in range(2):
                copy_out("kptv", n, vtkp[:, 2 * n:2 * n + 2, :], B("kptv", n)[:, :].rearrange("p (k m) -> p k m", k=2))
            copy_out("ks", 0, ksum, B("ks")[:, 0:2])
            act.wait_ge(S("psum_full"), filled("xdq", 1))
            for n in range(2):
                copy_out("pv", n, pv[:, n, :], B("pv", n)[:, :])
            act.wait_ge(S("rD"), 1)
            for j in range(TT):
                copy_out("proj", j, row(4)[:, j, :], B("proj", j)[0:P, :], ACT.Copy, scale=rD[:, j:j + 1])
            copy_out("gate1", 0, gates[:, 0, :, :], B("gate1")[0:P, 0:2 * TT].rearrange("p (j r) -> p j r", r=2), ACT.Sigmoid)
            load(root[0], I["L0_gnn_root1"].rearrange("(k p) n -> p k n", p=128), "root1_in")
            sqrt_for(2, 1)
            for j in range(TT):
                act.wait_ge(S("psum_full"), filled("h2T", j + 1))
                for k in range(KT):
                    ins = act.activation(col(5)[:, k, P * j:P * j + P], B("h2T", j)[:, P * k:P * k + P], ACT.Identity,
                                         scale=colvec("n2_g", k), bias=colvec("n2_b", k))
                ins.then_inc(S("act_read"), 1)
            for n in range(8):
                m, (a, w) = n // 2, HALF[n % 2]
                copy_out("m1", n, col(6)[:, m, a:a + w], B("m1", n)[:, 0:w], ACT.Gelu, bias=colvec("mlp_b1", m))
            load(root[1], I["L0_gnn_root2"].rearrange("(k p) n -> p k n", p=128), "root2_in")
            act.wait_ge(S("act_read"), READ0["gate1"] + 1)
            act.wait_ge(S("y_row"), 5)
            act.wait_ge(S("psum_full"), filled("h2T", 5))
            act.wait_ge(S("x_y"), 5)
            for j in range(TT):
                for r in range(2):
                    act.activation(row(3 + r)[:, j, :], xn[:, j, :], ACT.Copy, scale=gates[:, 0, j, r:r + 1]).then_inc(S("xg1"), 1)
            for j in range(TT):
                copy_out("m2", j, row(5)[:, j, :], B("m2", j)[0:P, :])

            act.wait_ge(S("x_mix"), 5)

            def high_weights(l):
                act.wait_ge(S("psum_full"), filled("m2", 5) if l == 0 else filled("h1T", 8))
                act.wait_ge(S(f"w{l}_sum"), 4 * 15)
                for r in range(2):
                    act.activation(wrel_hi[l][r], wrel_raw[l][r], ACT.Copy).then_inc(S("wrel_high"), 1)

            high_weights(0)
            for l, Z in enumerate(("Z1", "Z2")):
                if l == 1:
                    for n in range(8):
                        m, (a, w) = n // 2, HALF[n % 2]
                        skip = a - EVEN[n % 2][0]
                        copy_out("h1T", n, h1[:, m, a:a + w], B("h1T", n)[:, skip:skip + w], ACT.Relu, bias=colvec("bias1", m))
                    copy_out("gate2", 0, gates[:, 1, :, :], B("gate2")[0:P, 0:2 * TT].rearrange("p (j r) -> p j r", r=2), ACT.Sigmoid)
                    act.wait_ge(S("act_read"), READ0["gate2"] + 1)
                    for j in range(TT):
                        act.wait_ge(S("psum_full"), filled("h1r", j + 1))
                        for r in range(2):
                            ins = act.activation(row(GATED[1][r])[:, j, :], B("h1r", j)[0:P, :], ACT.Copy, scale=gates[:, 1, j, r:r + 1])
                        ins.then_inc(S("act_read"), 1)
                for n in range(16):
                    r, m, (a, w) = n // 8, n // 2 % 4, HALF[n % 2]
                    act.wait_ge(S("psum_full"), filled(Z, n + 1))
                    act.activation(col(Z_AT[r])[:, m, a:a + w], B(Z, n)[:, 0:w], ACT.Copy).then_inc(S("Z_full"), 1)
                    act.activation(Z_hi[l][r][:, m, a:a + w], B(Z, n)[:, 0:w], ACT.Copy).then_inc(S("act_read"), 1)
            high_weights(1)

            for n in range(7):
                w = min(4, 25 - 4 * n) * P
                copy_out("AnT", n, AT1[:, 500 * n:500 * n + w], B("AnT", n)[0:P, 0:w])
            sqrt_for(3, 0)
            transposed("xfT", col(2))
            act.wait_ge(S("rt_sub"), 1)
            act.activation(rtp, rtp, ACT.Exp).then_inc(S("rt_exp"), 1)
            for n in range(2):
                a, w = HALF[n]
                copy_out("hf", n, hfT[:, a:a + w], B("hf", n)[:, 0:w], ACT.Gelu, bias=colvec("ffn_b1", 0))
            for j in range(TT):
                copy_out("fy", j, row(4)[:, j, :], B("fy", j)[0:P, :])
            sqrt_for(4, 0)
            transposed("xn2T", col(2))
            SC = float(DH) ** -0.25
            copy_out("aq", 0, aqT, B("aq")[:, :].rearrange("p (k t) -> p k t", k=KT), ACT.Copy, scale=SC)
            act.wait_ge(S("bn_var"), 1)
            act.activation(sd[:, 0:KT], mv[:, 0:KT, 1:2].rearrange("p j o -> p (j o)"), ACT.Sqrt, bias=eps[:, 0:1]).then_inc(S("bn_std"), 1)
            copy_out("ak", 0, akT, B("ak")[:, :].rearrange("p (k t) -> p k t", k=KT), ACT.Copy, scale=SC)
            for k in range(KT):
                act.wait_ge(S("bn1"), k + 1)
                act.activation(col(3)[:, k, 0:N], col(3)[:, k, 0:N], ACT.Identity, bias=colvec("b1n", k)).then_inc(S("xbT"), 1)
            copy_out("av", 0, v_aug[:, :, 0:DH], B("av")[:, :].rearrange("p (h d) -> p h d", h=HEADS))
            for j in range(TT):
                copy_out("xbr", j, row(4)[:, j, :], B("xbr", j)[0:P, :])
            for n in range(8):
                m, (a, w) = n // 2, HALF[n % 2]
                copy_out("agg", n, agg_hi[:, m, a:a + w], B("agg", n)[:, 0:w])
            copy_out("ad", 0, adiag, B("ad")[:, 0:16])
            act.wait_ge(S("kbias"), 1)
            for h in HEAD_ORDER:
                act.activation(ke[:, h, :], ub("uk", h), ACT.Exp, bias=abias_k[:, h:h + 1]).then_inc(S("act_read"), 1)
            for n in range(8):
                m, (a, w) = n // 2, HALF[n % 2]
                copy_out("conv", n, col(6)[:, m, a:a + w], B("conv", n)[:, 0:w], ACT.Relu, bias=colvec("b_conv", m))
            act.wait_ge(S("qbias"), 1)
            for h in HEAD_ORDER:
                act.activation(qe[:, h, :], ub("uq", h), ACT.Exp, bias=abias_q[:, h:h + 1]).then_inc(S("act_read"), 1)
            for n in range(3):
                w = min(6, 16 - 6 * n)
                copy_out("kv", n, kv_sb[:, 6 * n:6 * n + w, :], B("kv", n)[:, 0:65 * w].rearrange("p (g d) -> p g d", g=w))
            for n in range(4):
                copy_out("qfT", n, qfT[:, 2 * n:2 * n + 2, :, :], B("qfT", n)[:, :].rearrange("p (h c t) -> p h c t", h=2, c=2))
            copy_out("atT", 0, attnT, B("atT")[:, :].rearrange("p (k t) -> p k t", k=KT))

            def phi_exp(n0, n1):
                for n in range(n0, n1):
                    act.wait_ge(S("xmin"), n + 1)
                    w = HALF[n % 2][1] if n < 8 else H
                    t = tmp[:, n % 2, 0:w] if n < 8 else tmp[0:P, n % 2, 0:w]
                    act.activation(t, t, ACT.Exp).then_inc(S("xexp"), 1)

            phi_exp(0, 4)
            copy_out("ha", 0, haT, B("ha")[:, :].rearrange("p (k t) -> p k t", k=KT))
            phi_exp(4, 8)
            for j in range(TT):
                copy_out("xv", j, row(5)[:, j, :], B("xv", j)[0:P, :])
            phi_exp(8, 8 + TT)
            for n in range(8):
                m, (a, w) = n // 2, HALF[n % 2]
                copy_out("xo", n, hid_hi[:, m, a:a + w], B("xo", n)[:, 0:w])
            act.wait_ge(S("bn_var"), 2)
            act.activation(sd[:, 0:KT], mv[:, 0:KT, 1:2].rearrange("p j o -> p (j o)"), ACT.Sqrt, bias=eps[:, 0:1]).then_inc(S("bn_std"), 1)
            sqrt_for(5, 0)
            transposed("xeT", col(2))
            act.wait_ge(S("x_pad"), 1)
            act.wait_ge(S("act_read"), READ0["xeT"] + 5)
            act.activation(xe_hi[:, :, 0:N], col(2)[:, :, 0:N], ACT.Copy).then_inc(S("xe_high"), 1)
            act.wait_ge(S("el_sub"), 1)
            act.activation(eexp, eexp, ACT.Exp).then_inc(S("el_exp"), 1)
            act.wait_ge(S("elist"), 1)
            for n in range(2):
                w = (500, 125)[n]
                copy_out("combT", n, combT[:, 500 * n:500 * n + w], B("combT", n)[0:E1, 0:w])
            n_act = act.value_load(el_i[0:1, 8:9], min_val=2, max_val=E1)

            def split_chunk(it, c):
                act.wait_ge(S("y_mm"), 16 * it + 2 * c - 6 + Y0)
                for part, name in enumerate(("ew_in", "ew2_in")):
                    act.wait_ge(S(f"{name}{c % 2}"), 64 * it + 16 * (c // 2) + 16)
                    at = 2048 * (c % 2) + 1024 * part
                    act.activation(ew_hi[:, c % 4, 1024 * part:1024 * part + 1024], weights[:, at:at + 1024], ACT.Copy)\
                        .then_inc(S("ew_high"), 1)

            with act.Fori(0, n_act) as it:
                e = act.value_load(el_i[0:1, bass.ds(it, 1)], min_val=0, max_val=E1 - 1)
                split_chunk(it, 0)
                split_chunk(it, 1)
                act.wait_ge(S("eh_out"), 32 * it + 1)
                act.wait_ge(S("eb_in"), 32)
                act.activation(eb1_now[:, :], eb1[:, bass.ds(16 * e, 16)], ACT.Copy).then_inc(S("eb1_now"), 1)
                act.wait_ge(S("eb1_now"), it + 1)

                for f in range(16):
                    for hf in range(2):
                        a, w = ((0, 312), (312, 314))[hf]
                        n = 2 * f + hf
                        act.wait_ge(S("hid_split"), 16 * it + max(f - 3, 0) + 1)
                        act.wait_ge(S("eh_mm"), 32 * it + n + 1)
                        act.activation(hid[:, f % 4, a:a + w], bank[5 + n % 3][:, 0:w], ACT.Silu,
                                       bias=eb1_now[:, f:f + 1]).then_inc(S("eh_out"), 1)
                    if f % 2 == 0 and f < 12:
                        split_chunk(it, f // 2 + 2)

        @block.vector
        def _(dve):
            step = [0]

            def link(ins):
                step[0] += 1
                ins.then_inc(S("dve_step"), 1)
                dve.wait_ge(S("dve_step"), step[0])

            norms = [0]

            def layernorm(src, dst, name, wait=None):
                for j in range(TT):
                    if wait:
                        dve.wait_ge(S(wait), j + 1)
                    ins = dve.bn_stats(st[0:P, j, :], src[:, j, :])
                link(ins)
                for j in range(TT):
                    ins = dve.bn_aggr(mv[0:P, j, :], st[0:P, j, :])
                ins.then_inc(S("ln_var"), 1)
                norms[0] += 1
                dve.wait_ge(S("ln_std"), norms[0])
                link(dve.reciprocal(rs[0:P, :], sd[0:P, :]))
                for j in range(TT):
                    dve.tensor_scalar(dst[:, j, :], src[:, j, :], mv[0:P, j, 0:1], rs[0:P, j:j + 1],
                                      ALU.subtract, ALU.mult).then_inc(S(name), 1)

            bns = [0]

            def batchnorm(src, dst, gain, name):
                for k in range(KT):
                    for hf, (a, w) in enumerate(HALF):
                        ins = dve.bn_stats(tmp[:, 0, 12 * k + 6 * hf:12 * k + 6 * hf + 6], src[:, k, a:a + w])
                link(ins)
                for k in range(KT):
                    ins = dve.bn_aggr(mv[:, k, :], tmp[:, 0, 12 * k:12 * k + 12])
                ins.then_inc(S("bn_var"), 1)
                bns[0] += 1
                dve.wait_ge(S("bn_std"), bns[0])
                link(dve.reciprocal(rs[:, 0:KT], sd[:, 0:KT]))
                link(dve.tensor_tensor(rs[:, 0:KT], rs[:, 0:KT], cols[:, COL_AT[gain]:COL_AT[gain] + KT], ALU.mult))
                for k in range(KT):
                    dve.tensor_scalar(dst[:, k, 0:N], src[:, k, 0:N], mv[:, k, 0:1], rs[:, k:k + 1],
                                      ALU.subtract, ALU.mult).then_inc(S(name), 1)

            def bc(v, e):
                return v.unsqueeze(2).to_broadcast([P, TT, e])

            def iota_bc(e):
                return iota_e[0:P, 0:e].unsqueeze(1).to_broadcast([P, TT, e])

            def top_two(val, e, tables, best, low):
                eq, hot = tables[0], tables[1:3]
                idx = small[0:P, 20:25]
                for i in range(2):
                    link(dve.tensor_reduce(best[i], val, AX.X, ALU.max))
                    link(dve.tensor_tensor(eq, val, bc(best[i], e), ALU.is_equal))
                    link(dve.scalar_tensor_tensor(eq, eq, -float(e), iota_bc(e), ALU.mult, ALU.add))
                    link(dve.tensor_reduce(idx, eq, AX.X, ALU.min))
                    link(dve.tensor_tensor(hot[i], eq, bc(idx, e), ALU.is_equal))
                    if i == 0:
                        link(dve.scalar_tensor_tensor(tables[3], hot[0], -low, val, ALU.mult, ALU.add))
                        val = tables[3]

            dve.wait_ge(S("edges_in"), 16)
            link(dve.tensor_copy(srcf, edges[:, 0, :]))
            link(dve.tensor_copy(dstf, edges[:, 1, :]))
            link(dve.tensor_copy(relf, edges[:, 2, :]))
            link(dve.tensor_scalar(relf, relf, 0.0, 1024.0, ALU.not_equal, ALU.mult))
            link(dve.tensor_tensor(relf, relf, dstf, ALU.add))
            for j in range(TT):
                dve.tensor_scalar(keyf[:, j, :], relf, -float(P * j), None, ALU.add)
                link(dve.tensor_scalar(gez[:, j, :], dstf, float(P * j), None, ALU.is_ge))
            for j in range(TT - 1):
                dve.tensor_tensor(pres[:, j, :], gez[:, j, :], gez[:, j + 1, :], ALU.subtract)
            dve.tensor_copy(pres[:, TT - 1, :], gez[:, TT - 1, :]).then_inc(S("presence"), 1)
            dve.wait_ge(S("x_in"), 16)
            dve.wait_ge(S("consts"), 1)
            layernorm(x, xn, "xn_row")
            layernorm(xn, row(3), "h_row", wait="xn_row")
            rr = rg[:, 0:TT * EG].rearrange("p (j q) -> p j q", j=TT)
            rt2 = rg[:, 200:210]
            iq = iota_e[0:1, 0:EG].unsqueeze(1).to_broadcast([1, TT, EG])
            dve.wait_ge(S("psum_full"), filled("rng", 1))
            cnt = B("rng")[0:1, 0:TT * ET].rearrange("p (j q u) -> p j q u", j=TT, u=EU)
            dve.tensor_reduce(rr, cnt, AX.X, ALU.add).then_inc(S("rng_out"), 1)
            dve.wait_ge(S("rng_out"), 1)
            link(dve.tensor_scalar(rr, rr, 0.5, None, ALU.is_ge))
            hit = small[0:1, 850:850 + 100]
            last, first = rt2[:, 0:5], rt2[:, 5:10]
            t40 = tmp[0:1, 1, 0:TT * EG].rearrange("p (j q) -> p j q", j=TT)
            link(dve.scalar_tensor_tensor(t40, iq, 1.0, rr, ALU.add, ALU.mult))
            link(dve.tensor_reduce(last, t40, AX.X, ALU.max))
            link(dve.scalar_tensor_tensor(t40, iq, -float(EG), rr, ALU.add, ALU.mult))
            link(dve.tensor_reduce(first, t40, AX.X, ALU.min))
            link(dve.tensor_scalar(first, first, float(EG), float(EG - 1), ALU.add, ALU.min))
            link(dve.tensor_tensor(last, last, first, ALU.subtract))
            link(dve.tensor_scalar(last, last, 1.0, None, ALU.max))
            dve.tensor_copy(rng_i[0:1, 0:10], rt2).then_inc(S("ranges"), 1)
            dve.wait_ge(S("ranges"), 1)
            for j in range(TT):
                groups = dve.value_load(rng_i[0:1, j:j + 1], min_val=1, max_val=EG)
                q0 = dve.value_load(rng_i[0:1, 5 + j:6 + j], min_val=0, max_val=EG - 1)
                if j:
                    dve.wait_ge(S("psum_full"), filled("A", 4 * j))
                with dve.Fori(0, groups) as i:
                    for u in range(EU):
                        dve.wait_ge(S(f"oh_used{j}"), EU * i + u + 1)
                        dve.tensor_scalar(oh_src[u], iota_src, small[0:P, bass.ds(EU * q0 + EU * i + u, 1)], None, ALU.is_equal)
                        dve.tensor_scalar(oh_dst[u], iota_dst, small[0:P, bass.ds(EU * q0 + EU * i + (ET * (j + 1) + u), 1)], None,
                                          ALU.is_equal).then_inc(S(f"oh_ready{j}"), 1)

            def first_bases(l, count):
                for g in range(count):
                    dve.wait_ge(S(f"basis_in{g}"), 16 * (USES1 * l + 1))
                    for r in range(2):
                        if g == 0:
                            dve.tensor_scalar(wrel[l][r], basis[g], att[:, l, r, 0:1], None, ALU.mult).then_inc(S(f"w{l}_sum"), 1)
                        else:
                            dve.wait_ge(S(f"w{l}_sum"), 2 * g + r - 1)
                            dve.scalar_tensor_tensor(wrel[l][r], basis[g], att[:, l, r, g:g + 1], wrel[l][r],
                                                     ALU.mult, ALU.add).then_inc(S(f"w{l}_sum"), 1)

            def bases1(g0, g1):
                for g in range(g0, g1):
                    dve.wait_ge(S(f"basis_in{g % 4}"), 16 * (g // 4) + 16)
                    for r in range(2):
                        dve.wait_ge(S("w0_sum"), 2 * g + r - 1)
                        dve.scalar_tensor_tensor(wrel[0][r], basis[g % 4], att[:, 0, r, g:g + 1], wrel[0][r],
                                                 ALU.mult, ALU.add).then_inc(S("w0_sum"), 1)

            dve.wait_ge(S("psum_full"), filled("A", 20))
            dve.wait_ge(S("att_in"), 16)
            first_bases(0, 4)
            with dve.Fori(1, 5) as q:
                for u in range(4):
                    dve.wait_ge(S(f"basis_in{u}"), 16 * q + 16)
                    for r in range(2):
                        dve.wait_ge(S("w0_sum"), 8 * q + (2 * u + r - 1))
                        dve.scalar_tensor_tensor(wrel[0][r], basis[u], att[:, 0, r, bass.ds(4 * q + u, 1)], wrel[0][r],
                                                 ALU.mult, ALU.add).then_inc(S("w0_sum"), 1)
            bases1(20, 21)
            dve.wait_ge(S("psum_full"), filled("D", 1))
            dve.tensor_scalar(rD, B("D")[0:P, 0:TT], 256e-8, None, ALU.add).then_inc(S("D_out"), 1)
            dve.wait_ge(S("D_out"), 1)
            dve.reciprocal(rD, rD).then_inc(S("rD"), 1)
            bases1(21, 23)
            layernorm(row(4), row(3), "yn_row", wait="y_row")
            bases1(23, NB)
            dve.wait_ge(S("w0_sum"), 2 * NB)
            first_bases(1, 2)
            with dve.Fori(1, NB // 2) as p:
                for u in range(2):
                    dve.wait_ge(S(f"basis_in{u}"), 16 * p + 16 * (USES1 + 1))
                    for r in range(2):
                        dve.wait_ge(S("w1_sum"), 4 * p + (2 * u + r - 1))
                        dve.scalar_tensor_tensor(wrel[1][r], basis[u], att[:, 1, r, bass.ds(2 * p + u, 1)], wrel[1][r],
                                                 ALU.mult, ALU.add).then_inc(S("w1_sum"), 1)
            for r in range(2):
                dve.wait_ge(S("wrel_high"), 2 + r + 1)
                dve.tensor_tensor(wrel_lo[1][r], wrel_raw[1][r], wrel_hi[1][r].bitcast(f32), ALU.subtract).then_inc(S("wrel_low1"), 1)

            dve.wait_ge(S("A_sum"), 1)
            deg = small[0:P, 982:987]
            link(dve.tensor_reduce(deg, AT[:, 0, :, :], AX.X, ALU.add))
            link(dve.tensor_scalar(deg, deg, 1.0, None, ALU.max))
            link(dve.reciprocal(deg, deg))
            for j in range(TT):
                dve.tensor_scalar(AT[:, 0, j, :], AT[:, 0, j, :], deg[:, j:j + 1], None, ALU.mult).then_inc(S("A_mean"), 1)
            for j in range(TT):
                dve.wait_ge(S("psum_full"), filled("o2", j + 1))
                dve.wait_ge(S("x_mix"), j + 1)
                dve.tensor_tensor(x[:, j, :], B("o2", j)[0:P, :], x[:, j, :], ALU.add).then_inc(S("o2_out"), 1)
            layernorm(x, row(1), "xf_row", wait="o2_out")

            dve.wait_ge(S("psum_full"), filled("rt", 1))
            T = [table(6, i, E0) for i in range(8)]
            b1, b2, s1 = small[0:P, 25:30], small[0:P, 30:35], small[0:P, 35:40]
            logit = B("rt")[0:P, 0:TT * E0].rearrange("p (j e) -> p j e", j=TT)
            dve.tensor_copy(T[0], logit).then_inc(S("rt_out"), 1)
            dve.wait_ge(S("rt_out"), 1)
            link(dve.tensor_reduce(b1, T[0], AX.X, ALU.max))
            dve.tensor_tensor(T[1], T[0], bc(b1, E0), ALU.subtract).then_inc(S("rt_sub"), 1)
            dve.wait_ge(S("rt_exp"), 1)
            link(dve.tensor_reduce(s1, T[1], AX.X, ALU.add))
            link(dve.reciprocal(s1, s1))
            link(dve.tensor_tensor(T[1], T[1], bc(s1, E0), ALU.mult))
            top_two(T[1], E0, [T[2], T[3], T[4], T[5]], [b1, b2], 4.0)
            dve.tensor_tensor(T[6], T[3], T[4], ALU.add).then_inc(S("chosen"), 1)
            dve.wait_ge(S("chosen"), 1)
            link(dve.tensor_tensor(T[1], T[1], T[6], ALU.mult))
            dve.wait_ge(S("psum_full"), filled("pos", 1))
            pos = B("pos")[0:P, 0:TT * E0].rearrange("p (j e) -> p j e", j=TT)
            dve.tensor_scalar(T[2], pos, float(CAP) - 0.5, None, ALU.is_lt).then_inc(S("pos_out"), 1)
            dve.wait_ge(S("pos_out"), 1)
            link(dve.tensor_tensor(T[2], T[2], T[1], ALU.mult))
            gate = small[0:P, 977:982]
            link(dve.tensor_reduce(gate, T[2], AX.X, ALU.add))
            for j in range(TT):
                dve.wait_ge(S("fy_row"), j + 1)
                dve.scalar_tensor_tensor(x[:, j, :], row(4)[:, j, :], gate[:, j:j + 1], x[:, j, :],
                                         ALU.mult, ALU.add).then_inc(S("x2"), 1)
            layernorm(x, row(1), "xn2_row", wait="x2")
            dve.memset(v_aug[:, :, DH:DH + 1], 1.0).then_inc(S("v_ones"), 1)
            dve.wait_ge(S("act_read"), READ0["xn2T"] + 5)
            batchnorm(col(2), col(3), "g1", "bn1")

            dve.wait_ge(S("psum_full"), filled("xbr", 5))
            for t in (agg_hi, agg_lo):
                link(dve.memset(t[:, :, N:COLW].bitcast(f32), 0.0))
            for n in range(8):
                m, (a, w) = n // 2, HALF[n % 2]
                dve.wait_ge(S("act_read"), READ0["agg"] + n + 1)
                dve.tensor_tensor(agg_lo[:, m, a:a + w], B("agg", n)[:, 0:w], agg_hi[:, m, a:a + w].bitcast(f32),
                                  ALU.subtract).then_inc(S("agg_low"), 1)
            for n in range(4):
                dve.wait_ge(S("psum_full"), filled("uk", n + 1))
                h = HEAD_ORDER[2 * n]
                ins = dve.tensor_reduce(amax_k[:, h:h + 3:2], B("uk", n)[:, :].rearrange("p (h m) -> p h m", h=2), AX.X, ALU.max)
            ins.then_inc(S("kmax"), 1)
            dve.wait_ge(S("kmax_all"), 1)
            dve.wait_ge(S("act_read"), READ0["ad"] + 1)
            dve.scalar_tensor_tensor(abias_k, adiag[:, 8:16], -1.0, amax_kr, ALU.mult, ALU.subtract).then_inc(S("kbias"), 1)
            dve.wait_ge(S("act_read"), READ0["uk"] + 8)
            dve.tensor_scalar(ke, ke, 1.0 / 16, 1e-6, ALU.mult, ALU.add).then_inc(S("kf"), 1)
            dve.wait_ge(S("psum_full"), filled("agg", 8))
            for t in (hid_hi, hid_lo):
                link(dve.memset(t[:, :, N:COLW].bitcast(f32), 0.0))
            link(dve.tensor_copy(hid_hi[:, :, 0:N], col(2)[:, :, 0:N]))
            dve.tensor_tensor(hid_lo[:, :, 0:N], col(2)[:, :, 0:N], hid_hi[:, :, 0:N].bitcast(f32), ALU.subtract).then_inc(S("xn2_split"), 1)
            for n in range(4):
                dve.wait_ge(S("psum_full"), filled("uq", n + 1))
                h = HEAD_ORDER[2 * n]
                ins = dve.tensor_reduce(amax_q[:, h:h + 3:2], B("uq", n)[:, :].rearrange("p (h m) -> p h m", h=2), AX.X, ALU.max)
            link(ins)
            dve.scalar_tensor_tensor(abias_q, adiag[:, 0:8], -1.0, amax_q, ALU.mult, ALU.subtract).then_inc(S("qbias"), 1)
            dve.wait_ge(S("act_read"), READ0["uq"] + 8)
            dve.tensor_scalar(qe, qe, 1.0 / 16, 1e-6, ALU.mult, ALU.add).then_inc(S("qf"), 1)
            for n in range(2):
                dve.wait_ge(S("psum_full"), filled("at", n + 1))
                heads = B("at", n)[:, 0:4 * 65].rearrange("p (h d) -> p h d", h=4)
                den = aden[:, 4 * n:4 * n + 4]
                link(dve.tensor_scalar(den, heads[:, :, DH:DH + 1].rearrange("p h o -> p (h o)"), 1e-6, None, ALU.add))
                link(dve.reciprocal(den, den))
                dve.tensor_tensor(attn[:, 256 * n:256 * n + 256].rearrange("p (h d) -> p h d", h=4), heads[:, :, 0:DH],
                                  den.unsqueeze(2).to_broadcast([128, 4, DH]), ALU.mult).then_inc(S("at_out"), 1)
            def phi_tile(n):
                if n < 8:
                    a, w = HALF[n % 2]
                    return B(*xq_tile(n))[:, 0:w], tmp[:, n % 2, 0:w], col(3)[:, n // 2, a:a + w]
                return B("xk", n - 8)[0:P, :], tmp[0:P, n % 2, :], row(4)[:, n - 8, :]

            def phi_min(n):
                name, at = xq_tile(n) if n < 8 else ("xk", n - 8)
                dve.wait_ge(S("psum_full"), filled(name, at + 1))
                if n >= 2:
                    dve.wait_ge(S("xq_out" if n - 2 < 8 else "xk_out"), n - 1 if n - 2 < 8 else n - 9)
                src, t, _ = phi_tile(n)
                dve.tensor_scalar(t, src, 0.0, None, ALU.min).then_inc(S("xmin"), 1)

            def phi(n0, n1):
                phi_min(n0)
                for n in range(n0, n1):
                    if n + 1 < n1:
                        phi_min(n + 1)
                    dve.wait_ge(S("xexp"), n + 1)
                    src, t, dst = phi_tile(n)
                    dve.scalar_tensor_tensor(dst, src, 0.0, t, ALU.max, ALU.add).then_inc(S("xq_out" if n < 8 else "xk_out"), 1)

            phi(0, 4)
            dve.wait_ge(S("act_read"), READ0["conv"] + 8)
            link(dve.tensor_tensor(col(6)[:, :, 0:N], col(6)[:, :, 0:N], col(2)[:, :, 0:N], ALU.add))
            dve.wait_ge(S("act_read"), READ0["ha"] + 1)
            dve.tensor_tensor(col(6)[:, :, 0:NA], col(6)[:, :, 0:NA], haT, ALU.add)
            for k in range(KT):
                ins = dve.tensor_scalar(col(6)[:, k, NA:N], col(6)[:, k, NA:N], haT[:, k, NA - 1:NA], None, ALU.add)
            link(ins)
            dve.memset(kvb, 0.0).then_inc(S("kvb_zero"), 1)

            phi(4, 8 + TT)
            dve.wait_ge(S("psum_full"), filled("xkv", 1))
            dve.wait_ge(S("kvb_zero"), 1)
            kvp = B("xkv")[:, :].rearrange("p (k e) -> p k e", k=KT)
            SCALE = float(DH) ** -0.5
            dve.tensor_scalar(kvb[0:64, :, 0:64], kvp[0:64, :, 0:64], SCALE, None, ALU.mult)
            dve.tensor_scalar(kvb[64:128, :, 64:128], kvp[64:128, :, 64:128], SCALE, None, ALU.mult).then_inc(S("xkv_out"), 1)
            bsum = small[:, 990:994]
            link(dve.tensor_tensor(bsum, cols[:, COL_AT["b_proj"]:COL_AT["b_proj"] + KT], cols[:, COL_AT["b2n"]:COL_AT["b2n"] + KT], ALU.add))
            for n in range(8):
                m, (a, w) = n // 2, HALF[n % 2]
                dve.wait_ge(S("act_read"), READ0["xo"] + n + 1)
                dve.tensor_tensor(hid_lo[:, m, a:a + w], B("xo", n)[:, 0:w], hid_hi[:, m, a:a + w].bitcast(f32),
                                  ALU.subtract).then_inc(S("xo_low"), 1)
            batchnorm(col(6), col(6), "g2", "bn2")
            dve.wait_ge(S("bn2"), 4)
            for n in range(8):
                m, (a, w) = n // 2, HALF[n % 2]
                dve.wait_ge(S("psum_full"), filled("xp", n + 1))
                dve.scalar_tensor_tensor(col(6)[:, m, a:a + w], B("xp", n)[:, 0:w], bsum[:, m:m + 1], col(6)[:, m, a:a + w],
                                         ALU.add, ALU.add).then_inc(S("xp_out"), 1)
            for j in range(TT):
                dve.wait_ge(S("psum_full"), filled("x3r", j + 1))
                dve.tensor_tensor(x[:, j, :], B("x3r", j)[0:P, :], x[:, j, :], ALU.add).then_inc(S("x3r_out"), 1)
            layernorm(x, row(1), "xe_row", wait="x3r_out")

            dve.wait_ge(S("xe_high"), 1)
            dve.tensor_tensor(xe_lo[:, :, 0:N], col(2)[:, :, 0:N], xe_hi[:, :, 0:N].bitcast(f32), ALU.subtract).then_inc(S("xe_low"), 1)
            U = [table(6, i, E1) for i in range(6)]
            dve.wait_ge(S("psum_full"), filled("el", 1))
            dve.wait_ge(S("Wg_in"), 32)
            dve.tensor_tensor(U[0], B("el")[0:P, 0:TT * E1].rearrange("p (j e) -> p j e", j=TT),
                              small[0:P, 0:E1].unsqueeze(1).to_broadcast([P, TT, E1]), ALU.add).then_inc(S("el_out"), 1)
            dve.wait_ge(S("el_out"), 1)
            top_two(U[0], E1, [U[1], U[2], U[3], U[4]], [b1, b2], 1e30)
            link(dve.tensor_tensor(U[4], U[2], U[3], ALU.add))
            sel = U[5].rearrange("p j e -> p (j e)")[:, 0:E1]
            dve.tensor_reduce(sel, U[4].rearrange("p j e -> p e j"), AX.X, ALU.add).then_inc(S("selected"), 1)
            dve.tensor_tensor(eexp, b2, b1, ALU.subtract).then_inc(S("el_sub"), 1)
            for i, (name, first) in enumerate((("y_mm", Y0), ("eh_out", 1), ("x4", TT), ("hid_split", 1))):
                dve.memset(small[0:1, 1015 + i:1016 + i], 0.0).then_inc(S(name), first)
            dve.wait_ge(S("psum_full"), filled("en", 1))
            act1, key1, srt = small[0:1, 800:808], small[0:1, 808:816], small[0:1, 816:824]
            dve.tensor_scalar(act1, B("en")[0:1, 0:E1], 0.5, None, ALU.is_ge).then_inc(S("en_out"), 1)
            dve.wait_ge(S("en_out"), 1)
            link(dve.scalar_tensor_tensor(key1, iota_e[0:1, 0:E1], -float(E1), act1, ALU.add, ALU.mult))
            link(dve.tensor_scalar(key1, key1, -1.0, None, ALU.mult))
            link(dve.max(srt, key1))
            link(dve.tensor_scalar(srt, srt, -1.0, float(E1), ALU.mult, ALU.add))
            link(dve.tensor_scalar(srt, srt, float(E1 - 1), None, ALU.min))
            link(dve.tensor_copy(el_i[0:1, 0:8], srt))
            link(dve.tensor_reduce(key1[:, 0:1], act1, AX.X, ALU.add))
            dve.tensor_copy(el_i[0:1, 8:9], key1[:, 0:1]).then_inc(S("elist"), 1)
            dve.wait_ge(S("el_exp"), 1)
            link(dve.tensor_scalar(s1, eexp, 1.0, None, ALU.add))
            link(dve.reciprocal(s1, s1))
            link(dve.tensor_tensor(b2, s1, eexp, ALU.mult))
            link(dve.tensor_tensor(U[2], U[2], bc(s1, E1), ALU.mult))
            link(dve.tensor_tensor(U[3], U[3], bc(b2, E1), ALU.mult))
            dve.tensor_tensor(comb, U[2], U[3], ALU.add).then_inc(S("comb"), 1)
            dve.wait_ge(S("elist"), 1)
            for j in range(TT):
                dve.wait_ge(S("psum_full"), filled("eb2", j + 1))
                dve.tensor_tensor(x[:, j, :], B("eb2", j)[0:P, :], x[:, j, :], ALU.add).then_inc(S("eb2_out"), 1)
            dve.wait_ge(S("eb2_out"), 5)
            n_act = dve.value_load(el_i[0:1, 8:9], min_val=2, max_val=E1)
            with dve.Fori(0, n_act) as it:
                e = dve.value_load(el_i[0:1, bass.ds(it, 1)], min_val=0, max_val=E1 - 1)
                dve.wait_ge(S("ew_high"), 16 * it + 4)
                dve.tensor_tensor(ew_lo[:, 1, :], weights[:, 2048:4096], ew_hi[:, 1, :].bitcast(f32), ALU.subtract).then_inc(S("ew_split1"), 1)
                for f in range(16):
                    dve.wait_ge(S("y_mm"), 16 * it + f - 3 + Y0)
                    dve.wait_ge(S("eh_out"), 32 * it + 2 * f + 3)
                    dve.tensor_copy(hid_hi[:, f % 4, :], hid[:, f % 4, :]).then_inc(S("hid_high"), 1)
                    dve.wait_ge(S("hid_high"), 16 * it + f + 1)
                    dve.tensor_tensor(hid_lo[:, f % 4, :], hid[:, f % 4, :], hid_hi[:, f % 4, :].bitcast(f32),
                                      ALU.subtract).then_inc(S("hid_split"), 1)
                dve.wait_ge(S("y_mm"), 16 * it + 16 + Y0)
                dve.wait_ge(S("x4"), TT * it + TT)
                for j in range(TT):
                    dve.scalar_tensor_tensor(x[:, j, :], bank[j][0:P, :], comb[:, j, bass.ds(e, 1)], x[:, j, :],
                                             ALU.mult, ALU.add).then_inc(S("x4"), 1)

        @block.tensor
        def _(pe):
            def group(out, pairs):
                for i, (a, b) in enumerate(pairs):
                    ins = pe.matmul(out, a, b, start=i == 0, stop=i == len(pairs) - 1)
                return ins

            def to_cols(stage, src, ready, n=TT, free=P):
                for j in range(n):
                    bk = claim(pe, stage, j)
                    pe.wait_ge(S(ready), j + 1)
                    for k in range(KT):
                        ins = pe.transpose(bk[:, P * k:P * k + P], src[:, j, 128 * k:128 * k + 128], ident[0:P, 0:P])
                    ins.then_inc(S("psum_full"), 1)

            def to_rows(stage, src):
                for j in range(TT):
                    bk = claim(pe, stage, j)
                    for k in range(KT):
                        ins = pe.transpose(bk[0:P, 128 * k:128 * k + 128], src[:, k, P * j:P * j + P], ident[:, :])
                    ins.then_inc(S("psum_full"), 1)

            def cols_out(stage, w, at, act_in, tiles=KT, n0=0, k_in=KT, columns=None):
                for m in range(tiles):
                    for hf, (a, wd) in enumerate(HALF):
                        n = n0 + 2 * m + hf
                        bk = claim(pe, stage, n)
                        if columns and m == 0:
                            pe.wait_ge(S("act_read"), READ0[columns] + (3, TT)[hf])
                        group(bk[:, 0:wd], [(w[:, k, at + 128 * m:at + 128 * m + 128], act_in[:, k, a:a + wd])
                                            for k in range(k_in)]).then_inc(S("psum_full"), 1)

            def rows_out(stage, act_in, w, at=0, k_in=KT, width=H):
                for j in range(TT):
                    bk = claim(pe, stage, j)
                    group(bk[0:P, 0:width], [(act_in[:, k, P * j:P * j + P], w[:, k, at:at + width])
                                             for k in range(k_in)]).then_inc(S("psum_full"), 1)

            def split_cols_out(stage, wh, wl, th, tl, tiles=range(8), n0=0):
                for n in tiles:
                    m, (a, w) = n // 2, ((0, 312), (312, 314))[n % 2]
                    bk = claim(pe, stage, n - n0)
                    group(bk[:, 0:w], [(wt[:, k, 128 * m:128 * m + 128], t[:, k, a:a + w]) for k in range(KT)
                                       for wt, t in ((wh, th), (wh, tl), (wl, th))]).then_inc(S("psum_full"), 1)

            def split_rows_out(stage, name):
                wh, wl = lin(ew_hi, name), lin(ew_lo, name)
                for j in range(TT):
                    bk = claim(pe, stage, j)
                    group(bk[0:P, :], [(t[:, k, P * j:P * j + P], wt[:, k, :]) for k in range(KT)
                                       for t, wt in ((hid_hi, wh), (hid_hi, wl), (hid_lo, wh))]).then_inc(S("psum_full"), 1)

            def small_rows(stage, act_in, w, width, columns=None):
                bk = claim(pe, stage)
                for j in range(TT):
                    if columns:
                        pe.wait_ge(S("act_read"), READ0[columns] + j + 1)
                    ins = group(bk[0:P, width * j:width * j + width], [(act_in[:, k, P * j:P * j + P], w[:, k, :]) for k in range(KT)])
                ins.then_inc(S("psum_full"), 1)

            pe.wait_ge(S("consts"), 1)
            bk = claim(pe, "rng")
            pe.wait_ge(S("presence"), 1)
            group(bk[0:1, 0:TT * ET], [(ones[0:P, 0:1], pres.rearrange("p j t -> p (j t)"))]).then_inc(S("psum_full"), 1)
            to_cols("xnT", xn, "xn_row")
            to_cols("hT", row(3), "h_row")
            pe.wait_ge(S("ranges"), 1)
            for j in range(TT):
                groups = pe.value_load(rng_i[0:1, j:j + 1], min_val=1, max_val=EG)
                parts = [(B("A", 4 * j + q), q // 2, HALF[q % 2]) for q in range(4)]
                for q, (bkq, r, (a, w)) in enumerate(parts):
                    claim(pe, "A", 4 * j + q)
                    pe.matmul(bkq[0:P, 0:w], zero[:, 0:P], zero[:, 0:w], start=True, stop=False)
                    if q < EU:
                        pe.matmul(bkq[0:P, 0:1], zero[:, 0:P], zero[:, 0:1], start=False, stop=False).then_inc(S(f"oh_used{j}"), 1)
                with pe.Fori(0, groups) as i:
                    for u in range(EU):
                        pe.wait_ge(S(f"oh_ready{j}"), EU * i + u + 1)
                        for bkq, r, (a, w) in parts:
                            ins = pe.matmul(bkq[0:P, 0:w], oh_dst[u][:, P * r:P * r + P], oh_src[u][:, a:a + w], start=False, stop=False)
                        ins.then_inc(S(f"oh_used{j}"), 1)
                for bkq, r, (a, w) in parts:
                    pe.matmul(bkq[0:P, 0:w], zero[:, 0:P], zero[:, 0:w], start=False, stop=True).then_inc(S("psum_full"), 1)

            pe.wait_ge(S("kqv_in"), 16)
            cols_out("kq", kqv_w, 0, col(4), tiles=8, columns="hT")
            rows_out("v", col(4), kqv_w, at=2 * H)
            pe.wait_ge(S("prm_in"), 16)

            def features(w, xd, srcT, squares, ready):
                for j in range(TT):
                    if j % 2 == 0:
                        bk = claim(pe, w, j // 2)
                    ins = group(bk[0:P, M * (j % 2):M * (j % 2) + M], [(srcT[:, k, P * j:P * j + P], prm_w[:, k, :]) for k in range(KT)])
                    if j % 2 == 1 or j == TT - 1:
                        ins.then_inc(S("psum_full"), 1)
                bk = claim(pe, xd)
                pe.wait_ge(S(ready), 1)
                for j in range(TT):
                    ins = group(bk[0:P, j:j + 1], [(squares[:, 0, P * j:P * j + P], eps[:, 2:3])])
                ins.then_inc(S("psum_full"), 1)

            pe.wait_ge(S("act_read"), READ0["kq"] + 8)
            features("wk", "xdk", col(5), col(4), "sqk_sum")
            pe.wait_ge(S("act_read"), READ0["kq"] + 16)
            features("wq", "xdq", col(6), col(5), "sqq_sum")
            for j in range(TT):
                bk = claim(pe, "qpT", j)
                pe.wait_ge(S("act_read"), READ0["wq"] + j + 1)
                for c in range(2):
                    ins = pe.transpose(bk[:, P * c:P * c + P], qp[:, j, 128 * c:128 * c + 128], ident[0:P, 0:P])
                ins.then_inc(S("psum_full"), 1)
            pe.wait_ge(S("act_read"), READ0["wk"] + 5)
            pe.wait_ge(S("vrow"), 5)
            for n in range(2):
                bk = claim(pe, "kptv", n)
                for k in (2 * n, 2 * n + 1):
                    ins = group(bk[:, M * (k % 2):M * (k % 2) + M], [(row(3)[:, j, 128 * k:128 * k + 128], kp[:, j, :]) for j in range(TT)])
                ins.then_inc(S("psum_full"), 1)
            bk = claim(pe, "ks")
            for c in range(2):
                ins = group(bk[:, c:c + 1], [(kp[:, j, 128 * c:128 * c + 128], ones[0:P, 0:1]) for j in range(TT)])
            ins.then_inc(S("psum_full"), 1)
            pe.wait_ge(S("act_read"), READ0["kptv"] + 2)
            pe.wait_ge(S("projw_in"), 16)
            for c in range(2):
                bk = claim(pe, "pv", c)
                group(bk[:, :], [(vtkp[:, k, 128 * c:128 * c + 128], proj_w[:, k, :]) for k in range(KT)]).then_inc(S("psum_full"), 1)
            bk = claim(pe, "D")
            pe.wait_ge(S("act_read"), READ0["ks"] + 1)
            pe.wait_ge(S("act_read"), READ0["qpT"] + 5)
            for j in range(TT):
                ins = group(bk[0:P, j:j + 1], [(qpT[:, c, P * j:P * j + P], ksum[:, c:c + 1]) for c in range(2)])
            ins.then_inc(S("psum_full"), 1)
            pe.wait_ge(S("act_read"), READ0["pv"] + 2)
            rows_out("proj", qpT, pv, k_in=2)
            pe.wait_ge(S("gate_in"), 16)
            small_rows("gate1", xnT, gate_w[:, 0, :, :], 2)
            to_cols("h2T", row(3), "yn_row")
            pe.wait_ge(S("mlp1_in"), 16)
            cols_out("m1", mlp_w1, 0, col(5), columns="h2T")
            pe.wait_ge(S("act_read"), READ0["m1"] + 8)
            pe.wait_ge(S("mlp2_in"), 16)
            rows_out("m2", col(6), mlp_w2)

            def neighbours(stage):
                for n in range(16):
                    r, m, (a, w) = n // 8, n // 2 % 4, HALF[n % 2]
                    bk = claim(pe, stage, n)
                    group(bk[:, 0:w], [(row(GATED[stage == "Z2"][r])[:, j, 128 * m:128 * m + 128], AT[:, r, j, a:a + w]) for j in range(TT)])\
                        .then_inc(S("psum_full"), 1)

            pe.wait_ge(S("act_read"), READ0["A"] + 20)
            pe.wait_ge(S("xg1"), 10)
            neighbours("Z1")
            pe.wait_ge(S("root1_in"), 16)
            for n in range(8):
                m, (a, w) = n // 2, EVEN[n % 2]
                bk = claim(pe, "h1T", n)
                for k in range(KT):
                    pe.matmul(bk[:, 0:w], root[0][:, k, 128 * m:128 * m + 128], xnT[:, k, a:a + w], start=k == 0, stop=False)
            pe.wait_ge(S("Z_low"), 16)
            pe.wait_ge(S("wrel_low0"), 2)
            for n in range(8):
                m, (a, w) = n // 2, EVEN[n % 2]
                products = [(wt[r][:, H * k + 128 * m:H * k + 128 * m + 128], zt[r][:, k, a:a + w]) for r in range(2) for k in range(KT)
                            for wt, zt in ((wrel_hi[0], Z_hi[0]), (wrel_hi[0], Z_lo), (wrel_lo[0], Z_hi[0]))]
                for i, (wk, zk) in enumerate(products):
                    ins = pe.matmul(B("h1T", n)[:, 0:w], wk, zk, start=False, stop=i == len(products) - 1)
                ins.then_inc(S("psum_full"), 1)
            pe.wait_ge(S("act_read"), READ0["h1T"] + 8)
            small_rows("gate2", h1, gate_w[:, 1, :, :], 2)
            to_rows("h1r", h1)
            pe.wait_ge(S("act_read"), READ0["h1r"] + 5)
            neighbours("Z2")
            pe.wait_ge(S("root2_in"), 16)
            for j in range(TT):
                bk = claim(pe, "o2", j)
                for k in range(KT):
                    pe.matmul(bk[0:P, :], h1[:, k, P * j:P * j + P], root[1][:, k, :], start=k == 0, stop=False)
            pe.wait_ge(S("Z_low"), 32)
            pe.wait_ge(S("wrel_low1"), 2)
            for j in range(TT):
                products = [(zt[r][:, k, P * j:P * j + P], wt[r][:, H * k:H * k + H]) for r in range(2) for k in range(KT)
                            for zt, wt in ((Z_hi[1], wrel_hi[1]), (Z_hi[1], wrel_lo[1]), (Z_lo, wrel_hi[1]))]
                for i, (a, b) in enumerate(products):
                    ins = pe.matmul(B("o2", j)[0:P, :], a, b, start=False, stop=i == len(products) - 1)
                ins.then_inc(S("psum_full"), 1)

            pe.wait_ge(S("A_mean"), 5)
            for n in range(7):
                bk = claim(pe, "AnT", n)
                for b in range(4 * n, min(4 * n + 4, 25)):
                    i, j = b // TT, b % TT
                    ins = pe.transpose(bk[0:P, P * (b % 4):P * (b % 4) + P], AT[:, 0, j, P * i:P * i + P], ident[0:P, 0:P])
                ins.then_inc(S("psum_full"), 1)
            to_cols("xfT", row(1), "xf_row")
            pe.wait_ge(S("ffn_in"), 48)
            small_rows("rt", col(2), ffn_rt, E0, columns="xfT")
            cols_out("hf", ffn_w1, 0, col(2), tiles=1)
            pe.wait_ge(S("act_read"), READ0["hf"] + 2)
            for j in range(TT):
                bk = claim(pe, "fy", j)
                group(bk[0:P, :], [(hfT[:, P * j:P * j + P], ffn_w2)]).then_inc(S("psum_full"), 1)
            bk = claim(pe, "pos")
            pe.wait_ge(S("chosen"), 1)
            chosen = table(6, 6, E0)
            for j in range(TT):
                ins = group(bk[0:P, E0 * j:E0 * j + E0], [(ones[0:P, 0:P], chosen[:, i, :]) for i in range(j)] + [(tri[:, :], chosen[:, j, :])])
            ins.then_inc(S("psum_full"), 1)

            to_cols("xn2T", row(1), "xn2_row")
            pe.wait_ge(S("act_read"), READ0["xn2T"] + 2)
            pe.wait_ge(S("Wqkvo_in"), 64)
            for stage, w in (("aq", Wq), ("ak", Wk)):
                bk = claim(pe, stage)
                for m in range(KT):
                    ins = group(bk[:, NA * m:NA * m + NA], [(w[:, k, 128 * m:128 * m + 128], col(2)[:, k, 0:NA]) for k in range(KT)])
                ins.then_inc(S("psum_full"), 1)
            bk = claim(pe, "av")
            group(bk[:, :], [(col(2)[:, k, 0:NA], Wv[:, k, :]) for k in range(KT)]).then_inc(S("psum_full"), 1)
            pe.wait_ge(S("xbT"), 4)
            to_rows("xbr", col(3))
            pe.wait_ge(S("act_read"), READ0["xbr"] + 5)
            pe.wait_ge(S("act_read"), READ0["AnT"] + 7)
            for n in range(8):
                m, (a, w) = n // 2, HALF[n % 2]
                bk = claim(pe, "agg", n)
                group(bk[:, 0:w], [(row(4)[:, i, 128 * m:128 * m + 128], An[:, i, a:a + w]) for i in range(TT)]).then_inc(S("psum_full"), 1)
            bk = claim(pe, "ad")
            pe.wait_ge(S("a_sq"), 2)
            for i, sq in enumerate((sq_aq, sq_ak)):
                for k in range(KT):
                    ins = group(bk[:, 8 * i + 2 * k:8 * i + 2 * k + 2], [(sq[:, k, :], halfsum[:, :])])
            ins.then_inc(S("psum_full"), 1)
            pe.wait_ge(S("projT_in"), 32)

            def random_features(stage, t):
                for n in range(4):
                    claim(pe, stage, n)
                    for h in HEAD_ORDER[2 * n:2 * n + 2]:
                        o = 64 * (h % 2)
                        ins = group(ub(stage, h), [(t[o:o + 64, h // 2, :], projT[o:o + 64, :])])
                    ins.then_inc(S("psum_full"), 1)

            random_features("uk", akT)
            pe.wait_ge(S("agg_low"), 8)
            pe.wait_ge(S("conv_split"), 1)
            split_cols_out("conv", conv_hi, conv_lo, agg_hi, agg_lo)
            random_features("uq", aqT)
            pe.wait_ge(S("kf"), 1)
            pe.wait_ge(S("act_read"), READ0["av"] + 1)
            pe.wait_ge(S("v_ones"), 1)
            for g in range(16):
                if g % 6 == 0:
                    bk = claim(pe, "kv", g // 6)
                h, c = g // 2, g % 2
                ins = group(bk[:, 65 * (g % 6):65 * (g % 6) + 65], [(ke[:, h, 128 * c:128 * c + 128], v_aug[:, h, :])])
                if g % 6 == 5 or g == 15:
                    ins.then_inc(S("psum_full"), 1)
            pe.wait_ge(S("qf"), 1)
            for n in range(4):
                bk = claim(pe, "qfT", n)
                for i in range(4):
                    h, c = 2 * n + i // 2, i % 2
                    ins = pe.transpose(bk[:, 128 * i:128 * i + 128], qe[:, h, 128 * c:128 * c + 128], ident[:, :])
                ins.then_inc(S("psum_full"), 1)
            pe.wait_ge(S("xn2_split"), 1)
            pe.wait_ge(S("lin_split"), 1)
            split_cols_out("xqa", lin(ew_hi, "q"), lin(ew_lo, "q"), hid_hi, hid_lo, range(4))
            pe.wait_ge(S("act_read"), READ0["kv"] + 3)
            pe.wait_ge(S("act_read"), READ0["qfT"] + 4)
            for n in range(2):
                bk = claim(pe, "at", n)
                for i in range(4):
                    h = 4 * n + i
                    ins = group(bk[:, 65 * i:65 * i + 65], [(qfT[:, h, c, :], kv_sb[:, 2 * h + c, :]) for c in range(2)])
                ins.then_inc(S("psum_full"), 1)
            bk = claim(pe, "atT")
            pe.wait_ge(S("at_out"), 2)
            for k in range(KT):
                ins = pe.transpose(bk[:, 128 * k:128 * k + 128], attn[:, 128 * k:128 * k + 128], ident[:, :])
            ins.then_inc(S("psum_full"), 1)
            bk = claim(pe, "ha")
            pe.wait_ge(S("act_read"), READ0["atT"] + 1)
            for m in range(KT):
                ins = group(bk[:, 128 * m:128 * m + 128], [(Wo[:, k, 128 * m:128 * m + 128], attnT[:, k, :]) for k in range(KT)])
            ins.then_inc(S("psum_full"), 1)
            split_cols_out("xqb", lin(ew_hi, "q"), lin(ew_lo, "q"), hid_hi, hid_lo, range(4, 8), n0=4)
            pe.wait_ge(S("lin_split"), 2)
            split_rows_out("xv", "v")
            pe.wait_ge(S("lin_split"), 3)
            split_rows_out("xk", "k")
            bk = claim(pe, "xkv")
            pe.wait_ge(S("xk_out"), 5)
            pe.wait_ge(S("act_read"), READ0["xv"] + 5)
            for p in range(KT):
                ins = group(bk[:, 128 * p:128 * p + 128], [(row(4)[:, j, 128 * p:128 * p + 128], row(5)[:, j, 128 * p:128 * p + 128]) for j in range(TT)])
            ins.then_inc(S("psum_full"), 1)
            pe.wait_ge(S("xkv_out"), 1)
            pe.wait_ge(S("xq_out"), 8)
            for n in range(8):
                m, (a, w) = n // 2, HALF[n % 2]
                bk = claim(pe, "xo", n)
                group(bk[:, 0:w], [(kvb[:, m, :], col(3)[:, m, a:a + w])]).then_inc(S("psum_full"), 1)
            pe.wait_ge(S("xo_low"), 8)
            pe.wait_ge(S("lin_split"), 4)
            split_cols_out("xp", lin(ew_hi, "proj"), lin(ew_lo, "proj"), hid_hi, hid_lo)
            pe.wait_ge(S("xp_out"), 8)
            to_rows("x3r", col(6))
            to_cols("xeT", row(1), "xe_row")
            pe.wait_ge(S("Wg_in"), 32)
            small_rows("el", col(2), Wg, E1, columns="xeT")
            bk = claim(pe, "en")
            pe.wait_ge(S("selected"), 1)
            group(bk[0:1, 0:E1], [(ones[0:P, 0:1], table(6, 5, E1).rearrange("p j e -> p (j e)")[:, 0:E1])]).then_inc(S("psum_full"), 1)
            pe.wait_ge(S("comb"), 1)
            for n in range(2):
                bk = claim(pe, "combT", n)
                for j in ((0, 1, 2, 3), (4,))[n]:
                    ins = pe.transpose(bk[0:E1, P * (j % 4):P * (j % 4) + P], comb[:, j, :], ident[0:P, 0:P])
                ins.then_inc(S("psum_full"), 1)
            pe.wait_ge(S("act_read"), READ0["combT"] + 2)
            pe.wait_ge(S("eb_in"), 32)
            for j in range(TT):
                bk = claim(pe, "eb2", j)
                group(bk[0:P, :], [(combT[:, P * j:P * j + P], eb2)]).then_inc(S("psum_full"), 1)
            pe.wait_ge(S("eb2_out"), 5)
            pe.wait_ge(S("elist"), 1)
            pe.wait_ge(S("xe_low"), 1)
            n_act = pe.value_load(el_i[0:1, 8:9], min_val=2, max_val=E1)
            with pe.Fori(0, n_act) as it:
                def output(f):
                    if f % 2 == 0:
                        wait_split(pe, it, f // 2)
                    pe.wait_ge(S("hid_split"), 16 * it + f + 2)
                    for j in range(TT):
                        hh, hl = (t[:, f % 4, P * j:P * j + P] for t in (hid_hi, hid_lo))
                        products = ((hh, w2_half(ew_hi, f)), (hh, w2_half(ew_lo, f)), (hl, w2_half(ew_hi, f)))
                        for i, (a, b) in enumerate(products):
                            ins = pe.matmul(bank[j][0:P, :], a, b, start=f == 0 and i == 0, stop=f == 15 and i == 2)
                    ins.then_inc(S("y_mm"), 1)

                for f in range(16):
                    if f % 2 == 0:
                        wait_split(pe, it, f // 2, part=0)
                    for hf, (a, w) in enumerate(((0, 312), (312, 314))):
                        n = 2 * f + hf
                        pe.wait_ge(S("eh_out"), 32 * it + max(n - 2, 0) + 1)
                        wh, wl = w1_half(ew_hi, f), w1_half(ew_lo, f)
                        group(bank[5 + n % 3][:, 0:w], [(wt[:, k, :], xt[:, k, a:a + w]) for k in range(KT)
                                                        for wt, xt in ((wh, xe_hi), (wh, xe_lo), (wl, xe_hi))]).then_inc(S("eh_mm"), 1)
                    if f == 1:
                        pe.wait_ge(S("x4"), TT * it + TT)
                    if f:
                        output(f - 1)
                output(15)


_COLS = {"n1_g": "L0_mix_n1_g", "n1_b": "L0_mix_n1_b", "n2_g": "L0_mix_n2_g", "n2_b": "L0_mix_n2_b", "mlp_b1": "L0_mix_mlp_b1",
         "bias1": "L0_gnn_bias1", "ffn_b1": "L0_ffn_b1", "b_conv": "L1_gnn_b_conv", "g1": "L1_gnn_norm1_g", "b1n": "L1_gnn_norm1_b",
         "g2": "L1_gnn_norm2_g", "b2n": "L1_gnn_norm2_b", "b_proj": "L1_mix_b_proj"}
_PLAIN = ["x", "L0_gnn_basis1", "L0_gnn_basis2", "L0_gnn_root1", "L0_gnn_root2", "L0_mix_kqv_w",
          "L0_mix_proj_w", "L0_mix_mlp_w1", "L0_mix_mlp_w2", "L1_gnn_Wq", "L1_gnn_Wk", "L1_gnn_Wv", "L1_gnn_Wo", "L1_gnn_W_conv",
          "L1_ffn_Wg", "L1_ffn_bg", "L1_ffn_W1", "L1_ffn_W2", "L1_ffn_b2"]


def kernel(**inputs):
    import numpy as _np
    import concourse.bacc as _bacc
    from concourse import mybir as _mybir
    from concourse.bass_utils import run_bass_kernel_spmd as _run

    g = {k: _np.asarray(v) for k, v in inputs.items()}
    laid = {name: g[name] for name in _PLAIN}
    by_feature = dict({n: g[src] for n, src in _COLS.items()}, kq_b=g["L0_mix_kqv_b"][:2 * H])
    laid["cols"] = _np.concatenate([by_feature[n].reshape(-1, 128).T for n, _ in COLS], axis=1)
    laid["edges"] = _np.stack([g["src"], g["dst"], g["edge_type_2"]]).reshape(3, ET, P).transpose(2, 0, 1)
    laid["att"] = _np.stack([g["L0_gnn_att1"], g["L0_gnn_att2"]])
    laid["gate_w"] = _np.stack([g[f"L0_gnn_gate_w{l}"][:, :, 0].reshape(2, KT, 128).transpose(2, 1, 0) for l in (1, 2)], axis=1)
    laid["prm_wT"] = g["L0_mix_w"].T
    laid["router_wT"] = g["L0_ffn_router_w"].T
    laid["ffn_w1T"] = g["L0_ffn_w1"].T
    laid["ffn_w2T"] = g["L0_ffn_w2"].T
    laid["projT"] = g["L1_gnn_proj"].T
    laid["w_qkvT"] = g["L1_mix_w_qkv"].T
    laid["w_projT"] = g["L1_mix_w_proj"].T
    laid["eb1"] = g["L1_ffn_b1"].reshape(E1, F1 // 128, 128).transpose(2, 0, 1).reshape(128, E1 * F1 // 128)
    for name, src in (("v_b", g["L0_mix_kqv_b"][2 * H:]), ("proj_b", g["L0_mix_proj_b"]), ("mlp_b2", g["L0_mix_mlp_b2"]),
                      ("bias2", g["L0_gnn_bias2"]), ("ffn_b2", g["L0_ffn_b2"])):
        laid["row_" + name] = src
    nc = _bacc.Bacc("TRN2", target_bir_lowering=False, num_devices=1)
    arrays, aps = {}, {}
    for name, a in laid.items():
        arrays["in_" + name] = _np.ascontiguousarray(a)
        aps[name] = nc.dram_tensor("in_" + name, a.shape, _mybir.dt.from_np(a.dtype), kind="ExternalInput").ap()
    out = nc.dram_tensor("out_0", (N, H), _mybir.dt.float32, kind="ExternalOutput").ap()
    gps_two_layers(nc, aps, out)
    r = _run(nc, [arrays], core_ids=[0])
    return r.results[0]["out_0"]
```
